# Optimizing a Trainium2 kernel written in Bass

```python
import numpy as np
import jax
import jax.numpy as jnp

def _softmax(x, axis=-1):
    return jax.nn.softmax(x, axis=axis)

def _gelu(x):
    return jax.nn.gelu(x, approximate=True)

def _silu(x):
    return jax.nn.silu(x)

def _sigmoid(x):
    return jax.nn.sigmoid(x)

def _layernorm(x, axis=-1, eps=1e-05):
    m = jnp.mean(x, axis=axis, keepdims=True)
    v = jnp.var(x, axis=axis, keepdims=True)
    return (x - m) / jnp.sqrt(v + eps)

def _scatter_add(tgt, idx, src, axis=0):
    return tgt.at[idx].add(src)

def _segment_sum(src, seg, n):
    return jax.ops.segment_sum(src, seg, n)
kernel_name = 'mk_macaron_d2_jaxref_r8_159f03'

def setup_inputs(seed: int=0):
    np.random.seed(seed)
    _w = jnp.asarray

    def _L0_attn_setup():
        import jax, jax.numpy as jnp
        import numpy as np
        B, N, C, H = (4, 1024, 128, 16)
        D = C // H
        EPS = 1e-05
        key = jax.random.key(seed)
        ks = jax.random.split(key, 10)
        s = 1.0 / np.sqrt(C)
        return {'x': jax.random.normal(ks[0], (B, N, C), jnp.float32), 'Wq': jax.random.uniform(ks[1], (C, C), jnp.float32, -s, s), 'bq': jax.random.uniform(ks[2], (C,), jnp.float32, -s, s), 'Wk': jax.random.uniform(ks[3], (C, C), jnp.float32, -s, s), 'bk': jax.random.uniform(ks[4], (C,), jnp.float32, -s, s), 'Wv': jax.random.uniform(ks[5], (C, C), jnp.float32, -s, s), 'bv': jax.random.uniform(ks[6], (C,), jnp.float32, -s, s), 'Wo': jax.random.uniform(ks[7], (C, C), jnp.float32, -s, s), 'bo': jax.random.uniform(ks[8], (C,), jnp.float32, -s, s), 'ln_g': jnp.ones((C,), jnp.float32), 'ln_b': jnp.zeros((C,), jnp.float32)}
    _L0_attn_in = _L0_attn_setup()

    def _L0_ffn_setup():
        import jax, jax.numpy as jnp
        import numpy as np
        key = jax.random.key(seed)
        k0, k1, k2, k3 = jax.random.split(key, 4)
        B, S, D, F, E = (8, 256, 128, 256, 8)
        x = jax.random.normal(k0, (B, S, D), dtype=jnp.float32)
        Wg = jax.random.normal(k1, (D, E), dtype=jnp.float32) * 0.02
        W1 = jax.random.normal(k2, (E, D, F), dtype=jnp.float32) * 0.02
        W2 = jax.random.normal(k3, (E, F, D), dtype=jnp.float32) * 0.02
        return {'x': x, 'Wg': Wg, 'W1': W1, 'W2': W2}
    _L0_ffn_in = _L0_ffn_setup()

    def _L1_attn_setup():
        import jax, jax.numpy as jnp
        import numpy as np
        D_MODEL = 128
        D_STATE = 64
        HEADDIM = 64
        D_INNER = 2 * D_MODEL
        NHEADS = D_INNER // HEADDIM
        D_IN_PROJ = 2 * D_INNER + 2 * D_STATE + NHEADS
        CHANNELS = D_INNER + 2 * D_STATE
        KSIZE = 4
        LN_EPS = 1e-05

        def _segsum(x):
            T = x.shape[-1]
            cs = jnp.cumsum(x, axis=-1)
            seg = cs[..., :, None] - cs[..., None, :]
            mask = jnp.tril(jnp.ones((T, T), bool))
            return jnp.where(mask, seg, -jnp.inf)

        def _ssd(X, A, B, C, block_len):
            b, Lseq, h, p = X.shape
            c = Lseq // block_len
            X = X.reshape(b, c, block_len, h, p)
            A = A.reshape(b, c, block_len, h).transpose(0, 3, 1, 2)
            B = B.reshape(b, c, block_len, -1)
            C = C.reshape(b, c, block_len, -1)
            A_cumsum = jnp.cumsum(A, axis=-1)
            Lmat = jnp.exp(_segsum(A))
            Y_diag = jnp.einsum('bcln,bcsn,bhcls,bcshp->bclhp', C, B, Lmat, X)
            decay_states = jnp.exp(A_cumsum[..., -1:] - A_cumsum)
            states = jnp.einsum('bcln,bhcl,bclhp->bchpn', B, decay_states, X)
            init = jnp.zeros_like(states[:, :1])
            states = jnp.concatenate([init, states], axis=1)
            A_last = jnp.pad(A_cumsum[..., -1], ((0, 0), (0, 0), (1, 0)))
            decay_chunk = jnp.exp(_segsum(A_last))
            new_states = jnp.einsum('bhzc,bchpn->bzhpn', decay_chunk, states)
            states_off, final_state = (new_states[:, :-1], new_states[:, -1])
            state_decay_out = jnp.exp(A_cumsum)
            Y_off = jnp.einsum('bcln,bchpn,bhcl->bclhp', C, states_off, state_decay_out)
            Y = (Y_diag + Y_off).reshape(b, Lseq, h, p)
            return (Y, final_state)
        key = jax.random.key(seed)
        ks = jax.random.split(key, 8)
        B, L = (2, 256)
        u = jax.random.normal(ks[0], (B, L, D_MODEL), jnp.float32)
        W_in1 = jax.random.normal(ks[1], (D_IN_PROJ, D_MODEL), jnp.float32) * 0.02
        A_log = jnp.log(jax.random.uniform(ks[2], (NHEADS,), jnp.float32, 1.0, 16.0))
        conv_w = jax.random.normal(ks[3], (CHANNELS, CHANNELS, KSIZE), jnp.float32) / np.sqrt(CHANNELS * KSIZE)
        conv_b = jax.random.normal(ks[4], (CHANNELS,), jnp.float32) * 0.01
        prelu_a = jnp.array(0.25, jnp.float32)
        W_in2 = jax.random.normal(ks[5], (D_INNER, D_MODEL), jnp.float32) * 0.02
        W_in3 = jax.random.normal(ks[6], (D_MODEL, D_INNER), jnp.float32) * 0.02
        ln_g = jnp.ones((D_INNER,), jnp.float32)
        ln_b = jnp.zeros((D_INNER,), jnp.float32)
        return {'u': u, 'W_in1': W_in1, 'A_log': A_log, 'conv_w': conv_w, 'conv_b': conv_b, 'prelu_a': prelu_a, 'W_in2': W_in2, 'W_in3': W_in3, 'ln_g': ln_g, 'ln_b': ln_b}
    _L1_attn_in = _L1_attn_setup()

    def _L1_ffn_setup():
        import jax, jax.numpy as jnp
        import numpy as np
        D_MODEL = 128
        N_EXPERTS = 8
        TOP_K = 2
        HIDDEN = 4 * D_MODEL
        key = jax.random.key(seed)
        ks = jax.random.split(key, 6)
        B, S = (2, 256)
        x = jax.random.normal(ks[0], (B, S, D_MODEL), dtype=jnp.float32)
        shared_w1 = jax.random.normal(ks[1], (HIDDEN, D_MODEL), dtype=jnp.float32) * 0.02
        shared_w2 = jax.random.normal(ks[2], (D_MODEL, HIDDEN), dtype=jnp.float32) * 0.02
        experts_w1 = jax.random.normal(ks[3], (N_EXPERTS, HIDDEN, D_MODEL), dtype=jnp.float32) * 0.02
        experts_w2 = jax.random.normal(ks[4], (N_EXPERTS, D_MODEL, HIDDEN), dtype=jnp.float32) * 0.02
        gate_w = jax.random.normal(ks[5], (N_EXPERTS, D_MODEL), dtype=jnp.float32) * 0.02
        return {'x': x, 'shared_w1': shared_w1, 'shared_w2': shared_w2, 'experts_w1': experts_w1, 'experts_w2': experts_w2, 'gate_w': gate_w}
    _L1_ffn_in = _L1_ffn_setup()
    _d = {'L0_attn_x': _L0_attn_in['x'], 'L0_attn_Wq': _L0_attn_in['Wq'], 'L0_attn_bq': _L0_attn_in['bq'], 'L0_attn_Wk': _L0_attn_in['Wk'], 'L0_attn_bk': _L0_attn_in['bk'], 'L0_attn_Wv': _L0_attn_in['Wv'], 'L0_attn_bv': _L0_attn_in['bv'], 'L0_attn_Wo': _L0_attn_in['Wo'], 'L0_attn_bo': _L0_attn_in['bo'], 'L0_attn_ln_g': _L0_attn_in['ln_g'], 'L0_attn_ln_b': _L0_attn_in['ln_b'], 'L0_ffn_Wg': _L0_ffn_in['Wg'], 'L0_ffn_W1': _L0_ffn_in['W1'], 'L0_ffn_W2': _L0_ffn_in['W2'], 'L1_attn_W_in1': _L1_attn_in['W_in1'], 'L1_attn_A_log': _L1_attn_in['A_log'], 'L1_attn_conv_w': _L1_attn_in['conv_w'], 'L1_attn_conv_b': _L1_attn_in['conv_b'], 'L1_attn_prelu_a': _L1_attn_in['prelu_a'], 'L1_attn_W_in2': _L1_attn_in['W_in2'], 'L1_attn_W_in3': _L1_attn_in['W_in3'], 'L1_attn_ln_g': _L1_attn_in['ln_g'], 'L1_attn_ln_b': _L1_attn_in['ln_b'], 'L1_ffn_shared_w1': _L1_ffn_in['shared_w1'], 'L1_ffn_shared_w2': _L1_ffn_in['shared_w2'], 'L1_ffn_experts_w1': _L1_ffn_in['experts_w1'], 'L1_ffn_experts_w2': _L1_ffn_in['experts_w2'], 'L1_ffn_gate_w': _L1_ffn_in['gate_w']}
    _x0 = _d['L0_attn_x']
    _d['L0_attn_x'] = jax.random.normal(jax.random.fold_in(jax.random.key(seed), 1), (8, 512, 128), dtype=_x0.dtype)
    del _x0
    return _d

def reference(L0_attn_x, L0_attn_Wq, L0_attn_bq, L0_attn_Wk, L0_attn_bk, L0_attn_Wv, L0_attn_bv, L0_attn_Wo, L0_attn_bo, L0_attn_ln_g, L0_attn_ln_b, L0_ffn_Wg, L0_ffn_W1, L0_ffn_W2, L1_attn_W_in1, L1_attn_A_log, L1_attn_conv_w, L1_attn_conv_b, L1_attn_prelu_a, L1_attn_W_in2, L1_attn_W_in3, L1_attn_ln_g, L1_attn_ln_b, L1_ffn_shared_w1, L1_ffn_shared_w2, L1_ffn_experts_w1, L1_ffn_experts_w2, L1_ffn_gate_w):

    def _L0_attn_ref(x, Wq, bq, Wk, bk, Wv, bv, Wo, bo, ln_g, ln_b):
        import jax, jax.numpy as jnp
        import numpy as np
        B, N, C, H = (4, 1024, 128, 16)
        D = C // H
        EPS = 1e-05
        b, n, c = x.shape
        q = x @ Wq.T + bq
        k = x @ Wk.T + bk
        v = x @ Wv.T + bv
        split = lambda z: z.reshape(b, n, H, D).transpose(0, 2, 1, 3)
        q, k, v = (split(q), split(k), split(v))
        q = jax.nn.softmax(q, axis=-1)
        k = jax.nn.softmax(k, axis=-2)
        state = jnp.einsum('bhnd,bhne->bhde', k, v)
        out = jnp.einsum('bhnd,bhde->bhne', q, state)
        out = out.transpose(0, 2, 1, 3).reshape(b, n, c)
        mu = out.mean(-1, keepdims=True)
        var = out.var(-1, keepdims=True)
        out = (out - mu) * jax.lax.rsqrt(var + EPS) * ln_g + ln_b
        return out @ Wo.T + bo

    def _L0_ffn_ref(x, Wg, W1, W2):
        import jax, jax.numpy as jnp
        import numpy as np
        B, S, D = x.shape
        E = Wg.shape[1]
        T = B * S
        cap = max(1, T // E)
        xt = x.reshape(T, D)
        logits = xt @ Wg
        probs = jax.nn.softmax(logits, axis=-1)
        pT = probs.T
        _, top_idx = jax.lax.top_k(pT, cap)
        sel = jnp.zeros((E, T), dtype=bool).at[jnp.arange(E)[:, None], top_idx].set(True)
        masked = jnp.where(sel, pT, -jnp.inf)
        assigned = sel.any(axis=0)
        tok2exp = jnp.where(assigned, jnp.argmax(masked, axis=0), jnp.argmax(pT, axis=0))
        weights = jnp.take_along_axis(probs, tok2exp[:, None], axis=1)[:, 0]
        out = jnp.zeros_like(xt)
        for e in range(E):
            gate = jnp.where(tok2exp == e, weights, 0.0)
            h = jax.nn.gelu(xt @ W1[e], approximate=False) @ W2[e]
            out = out + gate[:, None] * h
        return out.reshape(B, S, D)

    def _L1_attn_ref(u, W_in1, A_log, conv_w, conv_b, prelu_a, W_in2, W_in3, ln_g, ln_b):
        import jax, jax.numpy as jnp
        import numpy as np
        D_MODEL = 128
        D_STATE = 64
        HEADDIM = 64
        D_INNER = 2 * D_MODEL
        NHEADS = D_INNER // HEADDIM
        D_IN_PROJ = 2 * D_INNER + 2 * D_STATE + NHEADS
        CHANNELS = D_INNER + 2 * D_STATE
        KSIZE = 4
        LN_EPS = 1e-05

        def _segsum(x):
            T = x.shape[-1]
            cs = jnp.cumsum(x, axis=-1)
            seg = cs[..., :, None] - cs[..., None, :]
            mask = jnp.tril(jnp.ones((T, T), bool))
            return jnp.where(mask, seg, -jnp.inf)

        def _ssd(X, A, B, C, block_len):
            b, Lseq, h, p = X.shape
            c = Lseq // block_len
            X = X.reshape(b, c, block_len, h, p)
            A = A.reshape(b, c, block_len, h).transpose(0, 3, 1, 2)
            B = B.reshape(b, c, block_len, -1)
            C = C.reshape(b, c, block_len, -1)
            A_cumsum = jnp.cumsum(A, axis=-1)
            Lmat = jnp.exp(_segsum(A))
            Y_diag = jnp.einsum('bcln,bcsn,bhcls,bcshp->bclhp', C, B, Lmat, X)
            decay_states = jnp.exp(A_cumsum[..., -1:] - A_cumsum)
            states = jnp.einsum('bcln,bhcl,bclhp->bchpn', B, decay_states, X)
            init = jnp.zeros_like(states[:, :1])
            states = jnp.concatenate([init, states], axis=1)
            A_last = jnp.pad(A_cumsum[..., -1], ((0, 0), (0, 0), (1, 0)))
            decay_chunk = jnp.exp(_segsum(A_last))
            new_states = jnp.einsum('bhzc,bchpn->bzhpn', decay_chunk, states)
            states_off, final_state = (new_states[:, :-1], new_states[:, -1])
            state_decay_out = jnp.exp(A_cumsum)
            Y_off = jnp.einsum('bcln,bchpn,bhcl->bclhp', C, states_off, state_decay_out)
            Y = (Y_diag + Y_off).reshape(b, Lseq, h, p)
            return (Y, final_state)
        Bsz, L, _ = u.shape
        zxbcdt = u @ W_in1.T
        A = -jnp.exp(A_log)
        z = zxbcdt[..., :D_INNER]
        xBC = zxbcdt[..., D_INNER:D_INNER + CHANNELS]
        dt = zxbcdt[..., D_INNER + CHANNELS:]
        dt_safe = jnp.where(dt <= 20.0, dt, 0.0)
        dt = jnp.where(dt <= 20.0, jnp.log1p(jnp.exp(dt_safe)), dt)
        A_t = dt * A[None, None, :]
        xt = xBC.transpose(0, 2, 1)
        conv = jax.lax.conv_general_dilated(xt, conv_w, (1,), [(KSIZE - 1, 0)], dimension_numbers=('NCH', 'OIH', 'NCH'))
        conv = conv + conv_b[None, :, None]
        conv = jnp.maximum(conv, 0) + prelu_a * jnp.minimum(conv, 0)
        xBC_conv = conv.transpose(0, 2, 1)
        x = xBC_conv[..., :D_INNER].reshape(Bsz, L, NHEADS, HEADDIM)
        Bmat = xBC_conv[..., D_INNER:D_INNER + D_STATE]
        Cmat = xBC_conv[..., D_INNER + D_STATE:]
        Y, _ = _ssd(x, A_t, Bmat, Cmat, L // 4)
        out = Y.reshape(Bsz, L, D_INNER)
        u2 = jax.nn.gelu(u @ W_in2.T, approximate=False)
        h = u2 * out
        mu = jnp.mean(h, axis=-1, keepdims=True)
        var = jnp.mean((h - mu) ** 2, axis=-1, keepdims=True)
        hn = (h - mu) / jnp.sqrt(var + LN_EPS) * ln_g + ln_b
        return hn @ W_in3.T

    def _L1_ffn_ref(x, shared_w1, shared_w2, experts_w1, experts_w2, gate_w):
        import jax, jax.numpy as jnp
        import numpy as np
        D_MODEL = 128
        N_EXPERTS = 8
        TOP_K = 2
        HIDDEN = 4 * D_MODEL
        B, S, D = x.shape
        T = B * S
        x_flat = x.reshape(T, D)
        shared = jnp.einsum('td,dh->th', x_flat, shared_w1.T)
        shared = jnp.einsum('th,hd->td', jax.nn.silu(shared), shared_w2.T)
        gate_logits = x_flat @ gate_w.T
        top_k_gates, top_k_idx = jax.lax.top_k(gate_logits, TOP_K)
        top_k_gates = jax.nn.softmax(top_k_gates, axis=1)
        gates = jnp.zeros((T, N_EXPERTS), dtype=x.dtype)
        gates = gates.at[jnp.arange(T)[:, None], top_k_idx].set(top_k_gates)
        h = jnp.einsum('td,ehd->teh', x_flat, experts_w1)
        expert_out = jnp.einsum('teh,edh->ted', jax.nn.silu(h), experts_w2)
        selected = jnp.einsum('ted,te->td', expert_out, gates)
        return (shared + selected).reshape(B, S, D)
    x = L0_attn_x
    x = x + 0.5 * _L0_ffn_ref(_layernorm(x, axis=-1), L0_ffn_Wg, L0_ffn_W1, L0_ffn_W2)
    x = x + _L0_attn_ref(_layernorm(x, axis=-1), L0_attn_Wq, L0_attn_bq, L0_attn_Wk, L0_attn_bk, L0_attn_Wv, L0_attn_bv, L0_attn_Wo, L0_attn_bo, L0_attn_ln_g, L0_attn_ln_b)
    x = x + 0.5 * _L0_ffn_ref(_layernorm(x, axis=-1), L0_ffn_Wg, L0_ffn_W1, L0_ffn_W2)
    x = x + 0.5 * _L1_ffn_ref(_layernorm(x, axis=-1), L1_ffn_shared_w1, L1_ffn_shared_w2, L1_ffn_experts_w1, L1_ffn_experts_w2, L1_ffn_gate_w)
    x = x + _L1_attn_ref(_layernorm(x, axis=-1), L1_attn_W_in1, L1_attn_A_log, L1_attn_conv_w, L1_attn_conv_b, L1_attn_prelu_a, L1_attn_W_in2, L1_attn_W_in3, L1_attn_ln_g, L1_attn_ln_b)
    x = x + 0.5 * _L1_ffn_ref(_layernorm(x, axis=-1), L1_ffn_shared_w1, L1_ffn_shared_w2, L1_ffn_experts_w1, L1_ffn_experts_w2, L1_ffn_gate_w)
    return x

_drawn_inputs = setup_inputs


def setup_inputs(seed=0):
    import zlib

    import numpy as np

    out = dict(_drawn_inputs(seed))
    spreads = {'L0_attn_ln_g': (1.0, 0.2),
     'L0_attn_ln_b': (0.0, 0.1),
     'L1_attn_ln_g': (1.0, 0.2),
     'L1_attn_ln_b': (0.0, 0.306)}
    factors = {'L0_attn_bq': 8.0,
     'L0_attn_bk': 64.0,
     'L0_ffn_Wg': 8.0,
     'L0_ffn_W1': 8.0,
     'L0_ffn_W2': 8.0,
     'L1_attn_A_log': 5.135,
     'L1_attn_conv_b': 4.461,
     'L1_ffn_experts_w1': 2.969,
     'L1_ffn_experts_w2': 2.92,
     'L1_ffn_gate_w': 3.39}
    for name, (base, spread) in spreads.items():
        noise = np.random.default_rng([zlib.crc32(name.encode()), seed]).standard_normal(out[name].shape)
        drawn = base * np.exp(spread * noise) if base else spread * noise
        out[name] = jnp.asarray(drawn.astype(out[name].dtype))
    for name, factor in factors.items():
        out[name] = (out[name] * factor).astype(out[name].dtype)
    return out
```

```python
from contextlib import ExitStack

import numpy as np

import concourse.bass as bass
from concourse import mybir

F32 = mybir.dt.float32
I32 = mybir.dt.int32
ALU = mybir.AluOpType
ACT = mybir.ActivationFunctionType
AX = mybir.AxisListType

P = 128
D = 128
BATCHES, SEQ = 8, 512
TOKENS = BATCHES * SEQ
TILES = TOKENS // P
BT = SEQ // P
E = 8
FA, FB = 256, 512
CAP = TOKENS // E
HEADS = 16
HD = D // HEADS
INNER, STATE, MH = 256, 64, 4
MP = INNER // MH
CH = INNER + 2 * STATE
CC = CH // P
TAPS = 4
EPS = 1e-5
NEG = -3e38
BITS = 30
GROUP = 4
MAX_BLOCKS = 2 * TILES + E
SLOTS = 8

PARTS = dict(ident=P, before=P, upto=P, ones=P, same_expert=P, last_row=P, head_mask=P, causal=P,
             prefer=E * TILES, restart=E * TILES, block_row=MAX_BLOCKS)
AT = {k: sum(list(PARTS.values())[:i]) for i, k in enumerate(PARTS)}
CONST_COLS = sum(PARTS.values())
V_BK, V_LNG, V_LNB, V_CONVB, V_PRELU, V_MG, V_MB, V_END = 0, 1, 2, 3, 6, 7, 9, 11
R_BQ, R_BV, R_BO, R_ALOG, R_END = 0, 128, 256, 384, 388


def wait(eng, semaphore, count):
    if not isinstance(count, int) or count > 0:
        eng.wait_ge(semaphore, count)


def turns(eng, n):
    def run(body):
        body(0)
        with eng.Fori(1, n) as i:
            body(i)
    return run


def program(nc, x, consts, bits, vecs, rows, wqkvo, a_wg, a_w1, a_w2, b_wg, b_w1, b_w2, b_sw1, b_sw2,
            m_in1, m_in2, m_in3, m_conv, out):
    ctx = ExitStack()
    with ctx:
        def sb(scope, name, shape, dt=F32):
            return scope.enter_context(nc.sbuf_tensor(name, shape, dt))

        held, signals = [ctx.enter_context(ExitStack())], [[]]

        def sem(name):
            signals[-1].append(held[-1].enter_context(nc.semaphore(name)))
            return signals[-1][-1]

        def next_phase():
            if len(held) > 2:
                held[-2].close()
            held.append(ctx.enter_context(ExitStack()))
            signals.append([])

        def clear_last_phase(sp):
            nums = sorted(h.num for h in signals[-2])
            while len(signals) > 2 and nums:
                n = 1
                while n < len(nums) and nums[n] == nums[0] + n:
                    n += 1
                sp.sem_clear(range(nums[0], nums[0] + n))
                nums = nums[n:]

        def pair(name):
            return [sem(f"{name}{q}") for q in range(2)]

        X = sb(ctx, "X", [P, TILES, D])
        stats = sb(ctx, "stats", [P, TILES, 6])
        rstd = sb(ctx, "rstd", [P, TILES])
        shift = sb(ctx, "shift", [P, TILES])
        table = sb(ctx, "table", [P, CONST_COLS])
        bit_table = sb(ctx, "bit_table", [P, BITS], I32)
        vec = sb(ctx, "vec", [P, V_END])
        row = sb(ctx, "row", [P, R_END])
        wgB = sb(ctx, "wgB", [P, E])
        w1B, w2B = sb(ctx, "w1B", [P, E, FB]), sb(ctx, "w2B", [P, E, FB // P, D])
        sw1B, sw2B = sb(ctx, "sw1B", [P, FB]), sb(ctx, "sw2B", [P, FB // P, D])
        win1, win2 = sb(ctx, "win1", [P, CH + MH]), sb(ctx, "win2", [P, INNER])
        win3 = sb(ctx, "win3", [P, INNER // P, D])
        wconv = sb(ctx, "wconv", [P, CC, TAPS, CH])
        layer0 = ctx.enter_context(ExitStack())
        wattn = sb(layer0, "wattn", [P, 4, D])
        wgA = sb(layer0, "wgA", [P, E])
        w1A, w2A = sb(layer0, "w1A", [P, E, FA]), sb(layer0, "w2A", [P, E, FA // P, D])
        bank = [ctx.enter_context(nc.psum_tensor(f"bank{i}", [P, 512], F32)) for i in range(8)]
        sorted_x = nc.dram_tensor("sorted_x", [MAX_BLOCKS * P, D], F32, kind="Internal").ap()
        sorted_y = nc.dram_tensor("sorted_y", [MAX_BLOCKS * P, D], F32, kind="Internal").ap()

        def const(which):
            return table[:, AT[which]:AT[which] + PARTS[which]]

        ident = const("ident")

        def one(ap, i):
            return ap[:, bass.ds(i, 1)]

        class Chain:

            def __init__(self, eng, name):
                self.eng, self.sem, self.base, self.n = eng, sem(name), 0, 0

            def __call__(self, ins):
                self.n += 1
                ins.then_inc(self.sem, 1)
                self.eng.wait_ge(self.sem, self.base + self.n)

            def start(self, base):
                self.base, self.n = base, 0

        def row_norm(v, own, st, rs, sh, width, scope, name):
            n = rs.shape[1]
            diff, total, var, t = (sb(scope, f"{name}_{k}", [P, n]) for k in ("diff", "total", "var", "newton"))
            seed = sb(scope, f"{name}_seed", [P, n], I32)
            own(v.tensor_tensor(diff[:], st[:, :, 1], st[:, :, 4], ALU.subtract))
            own(v.tensor_tensor(total[:], st[:, :, 1], st[:, :, 4], ALU.add))
            own(v.tensor_tensor(var[:], st[:, :, 2], st[:, :, 5], ALU.add))
            own(v.scalar_tensor_tensor(t[:], diff[:], 0.25, diff[:], ALU.mult, ALU.mult))
            own(v.scalar_tensor_tensor(var[:], var[:], 1.0 / width, t[:], ALU.mult, ALU.add))
            own(v.tensor_scalar(var[:], var[:], EPS, None, ALU.add))
            own(v.tensor_scalar(seed[:], var[:].bitcast(I32), 1, None, ALU.logical_shift_right))
            own(v.tensor_scalar(seed[:], seed[:], -1.0, float(0x5F3759DF), ALU.mult, ALU.add))
            r = seed[:].bitcast(F32)
            for _ in range(3):
                own(v.tensor_tensor(t[:], r, r, ALU.mult))
                own(v.scalar_tensor_tensor(t[:], t[:], -0.5, var[:], ALU.mult, ALU.mult))
                own(v.scalar_tensor_tensor(rs[:], t[:], 1.5, r, ALU.add, ALU.mult))
                r = rs[:]
            own(v.scalar_tensor_tensor(sh[:], total[:], -0.5, rs[:], ALU.mult, ALU.mult))

        def normed(v, dst, tile, src):
            return v.tensor_scalar(dst, src, one(rstd, tile), one(shift, tile), ALU.mult, ALU.add)

        scattered = sem("scattered")
        y_stored = [sem(f"y_stored{k}") for k in range(GROUP)]
        gathered = [sem(f"gathered{k}") for k in range(SLOTS)]
        done = dict(scattered=0, y_stored=0, gathered=0)

        x_loaded, w_loaded, zeroed, cleared = sem("x_loaded"), sem("w_loaded"), sem("zeroed"), sem("cleared")
        with ExitStack() as scope:
            zeros = sb(scope, "zeros", [P, MAX_BLOCKS // 4, D])
            first = ((table, consts), (bit_table, bits), (vec, vecs), (row, rows), (wattn, wqkvo),
                     (wgA, a_wg), (w1A, a_w1), (w2A, a_w2))
            second = ((wgB, b_wg), (w1B, b_w1), (w2B, b_w2), (sw1B, b_sw1), (sw2B, b_sw2),
                      (win1, m_in1), (win2, m_in2), (win3, m_in3), (wconv, m_conv))
            with nc.Block() as block:
                @block.sync
                def _(sp):
                    sp.dma_start(X[:], x.rearrange("(t p) d -> p t d", p=P)).then_inc(x_loaded, 16)
                    for dst, src in first:
                        sp.dma_start(dst[:], src).then_inc(w_loaded, 16)
                    sp.wait_ge(w_loaded, 16 * len(first + second))
                    sp.wait_ge(cleared, 16 * 4)

                @block.scalar
                def _(act):
                    for dst, src in second:
                        act.dma_start(dst[:], src).then_inc(w_loaded, 16)

                @block.gpsimd
                def _(pool):
                    nc.gpsimd.memset(zeros[:], 0.0).then_inc(zeroed, 1)
                    pool.wait_ge(zeroed, 1)
                    for k in range(4):
                        pool.dma_start(sorted_x.rearrange("(k p t) d -> k p t d", k=4, p=P)[k], zeros[:]) \
                            .then_inc(cleared, 16)

                @block.vector
                def _(v):
                    v.wait_ge(x_loaded, 16)
                    @turns(v, TILES // 4)
                    def _(i):
                        for k in range(4):
                            v.bn_stats(one(stats, 4 * i + k), one(X, 4 * i + k))

        def moe(name, F, choices, func, wg, w1, w2, shared, final):
            NC = F // P
            NB = choices * TILES + E
            TURNS = NB // GROUP
            HALF_BANK = E * TILES
            scope = ExitStack()

            def s(n):
                return sem(f"{name}_{n}")

            def s2(n):
                return pair(f"{name}_{n}")

            def t(n, shape, dt=F32):
                return sb(scope, f"{name}_{n}", shape, dt)

            normed_rows, columns, columns_copied, logits_done = s2("normed_rows"), s2("columns"), s2("columns_copied"), s2("logits_done")
            rows_kept, all_columns = s2("rows_kept"), s2("all_columns")
            centred, exped, prob_ready, prob_turned = s("centred"), s("exped"), s("prob_ready"), s("prob_turned")
            counted, summed, thr_ready, thr_spread = s("counted"), s("summed"), s("thr_ready"), s("thr_spread")
            ties_ready, ties_summed, picked, picks_summed = s("ties_ready"), s("ties_summed"), s("picked"), s("picks_summed")
            pos_ready, experts_known = s("pos_ready"), s("experts_known")
            scattered0, stored0, gathered0 = done["scattered"], done["y_stored"], done["gathered"]
            done["scattered"] += 16 * TILES * choices
            done["y_stored"] += 16 * TURNS
            done["gathered"] += 16 * TILES * choices // SLOTS
            if shared:
                sh_up, sh_act, sh_down, sh_added = s("sh_up"), [s(f"sh_act{c}") for c in range(NC)], s2("sh_down"), s2("sh_added")
            blk_loaded = [s(f"blk_loaded{k}") for k in range(GROUP)]
            turned, xT_copied, up, activated = s2("turned"), s2("xT_copied"), s2("up"), s2("activated")
            h_turned, hT_copied, down, y_copied = s2("h_turned"), s2("hT_copied"), s2("down"), s2("y_copied")
            used, sent = s("used"), s("sent")

            with scope:
                xn = t("xn", [P, TILES, D])
                xw = [t(f"xw{q}", [P, BT, D]) for q in range(2)]
                xT = [t(f"xT{q}", [P, SEQ]) for q in range(2)]
                gate = [t(f"gate{k}", [P, TILES]) for k in range(choices)]
                pos = [t(f"pos{k}", [P, TILES], I32) for k in range(choices)]
                block_expert = t("block_expert", [P, NB + GROUP], I32)
                score, work, pick, pick2 = (t(n, [P, E, TILES]) for n in ("score", "work", "pick", "pick2"))
                best, other = t("best", [P, TILES]), t("other", [P, TILES])
                by_tile = t("by_tile", [P, TILES, E])
                prob_rows, hits = t("prob_rows", [P, 2 * P]), t("hits", [P, 2 * P])
                thr, cand, count = t("thr", [P, 1]), t("cand", [P, 1]), t("count", [P, 1])
                small = [t(f"small{k}", [P, E]) for k in range(4)]
                small_i = t("small_i", [P, E], I32)
                begun, begun_by = t("begun", [P, NB, E]), t("begun_by", [P, NB])
                if shared:
                    xnT = t("xnT", [P, TOKENS])
                    sh = [t(f"sh{q}", [P, NC, SEQ]) for q in range(2)]
                rows_in = [t(f"rows_in{k}", [P, D]) for k in range(GROUP)]
                bxT = [t(f"bxT{q}", [P, P]) for q in range(2)]
                h = [t(f"h{q}", [P, F]) for q in range(2)]
                hT = [t(f"hT{q}", [P, F]) for q in range(2)]
                y = [t(f"y{k}", [P, D]) for k in range(GROUP)]
                got = [t(f"got{k}", [P, D]) for k in range(SLOTS)]

                def per_token(ap):
                    return ap.unsqueeze(1).broadcast_to([P, E, TILES])

                def per_expert(ap):
                    return ap.unsqueeze(2).broadcast_to([P, E, TILES])

                def over_experts(ap):
                    return ap.rearrange("p e t -> p t e")

                def flat(ap):
                    return ap.rearrange("p e t -> p (e t)")

                def routing(b):
                    return bank[b][:, 0:HALF_BANK].rearrange("p (e t) -> p e t", e=E)

                logits, sum_before, sum_tile, sum_above = routing(2), routing(3), routing(4), routing(5)

                def parity(i, k):
                    return k % 2, 2 * i + k // 2

                with nc.Block() as block:
                    @block.tensor
                    def _(pe):
                        @turns(pe, BATCHES // 2)
                        def _(i):
                            for q in range(2):
                                pe.wait_ge(normed_rows[q], i + 1)
                                wait(pe, columns_copied[q], i)
                                for k in range(BT):
                                    last = pe.transpose(bank[q][:, k * P:(k + 1) * P], xw[q][:, k, :], ident)
                                last.then_inc(columns[q], 1)
                            for q in range(2):
                                pe.wait_ge(columns_copied[q], i + 1)
                                for k in range(BT):
                                    last = pe.matmul(logits[:, :, bass.ds(8 * i + BT * q + k, 1)], xT[q][:, k * P:(k + 1) * P],
                                                     wg[:], start=True, stop=True)
                                last.then_inc(logits_done[q], 1)
                        if choices == 1:
                            pe.wait_ge(prob_ready, 1)
                            for half in range(2):
                                last = pe.transpose(bank[0][:, half * P:(half + 1) * P],
                                                    by_tile[:, 16 * half:16 * half + 16, :].rearrange("p t e -> p (t e)"), ident)
                            last.then_inc(prob_turned, 1)
                            with pe.Fori(0, BITS) as i:
                                pe.wait_ge(counted, i + 1)
                                pe.matmul(bank[1][:, 0:1], const("same_expert"), count[:], start=True, stop=True).then_inc(summed, 1)
                            pe.wait_ge(thr_ready, 1)
                            pe.matmul(bank[1][:, 0:E], thr[:].to_broadcast([P, P]), ident[:, 0:E], start=True, stop=True) \
                                .then_inc(thr_spread, 1)
                            pe.wait_ge(ties_ready, 2)
                            pe.matmul(flat(sum_before), const("before"), flat(pick[:]), start=True, stop=True)
                            pe.matmul(flat(sum_tile), const("ones"), flat(pick[:]), start=True, stop=True)
                            pe.matmul(flat(sum_above), const("ones"), flat(work[:]), start=True, stop=True).then_inc(ties_summed, 1)
                        pe.wait_ge(picked, 1)
                        pe.matmul(flat(sum_before), const("before"), flat(work[:]), start=True, stop=True)
                        pe.matmul(flat(sum_tile), const("ones"), flat(work[:]), start=True, stop=True).then_inc(picks_summed, 1)

                        if shared:
                            pe.wait_ge(pos_ready, choices)
                            for q in range(2):
                                pe.wait_ge(all_columns[q], BATCHES // 2)
                            @turns(pe, BATCHES // 2)
                            def _(i):
                                for q in range(2):
                                    for c in range(NC):
                                        wait(pe, sh_act[c], 2 * i + q)
                                        pe.matmul(bank[c][:], sw1B[:, c * P:(c + 1) * P], xnT[:, bass.ds((2 * i + q) * SEQ, SEQ)],
                                                  start=True, stop=True).then_inc(sh_up, 1)
                                for q in range(2):
                                    pe.wait_ge(sh_act[NC - 1], 2 * i + q + 1)
                                    wait(pe, sh_added[q], i)
                                    for k in range(BT):
                                        for c in range(NC):
                                            last = pe.matmul(bank[6 + q][:, k * P:(k + 1) * P], sh[q][:, c, k * P:(k + 1) * P],
                                                             sw2B[:, c, :], start=(c == 0), stop=(c == NC - 1))
                                    last.then_inc(sh_down[q], 1)
                            for q in range(2):
                                pe.wait_ge(sh_added[q], BATCHES // 2)

                        def turn_rows(i, k):
                            q, n = parity(i, k)
                            pe.wait_ge(blk_loaded[k], 16 * (i + 1))
                            wait(pe, xT_copied[q], n)
                            pe.transpose(bank[q][:, 0:P], rows_in[k][:], ident).then_inc(turned[q], 1)

                        def go_up(i, k, e):
                            q, n = parity(i, k)
                            pe.wait_ge(xT_copied[q], n + 1)
                            wait(pe, activated[q], n)
                            pe.matmul(bank[2 + q][:, 0:F], bxT[q][:], w1[:, bass.ds(e, 1), :], start=True, stop=True).then_inc(up[q], 1)

                        def turn_hidden(i, k):
                            q, n = parity(i, k)
                            pe.wait_ge(activated[q], n + 1)
                            wait(pe, hT_copied[q], n)
                            for c in range(NC):
                                last = pe.transpose(bank[4 + q][:, c * P:(c + 1) * P], h[q][:, c * P:(c + 1) * P], ident)
                            last.then_inc(h_turned[q], 1)

                        def come_down(i, k, e):
                            q, n = parity(i, k)
                            pe.wait_ge(hT_copied[q], n + 1)
                            wait(pe, y_copied[q], n)
                            for c in range(NC):
                                last = pe.matmul(bank[6 + q][:, 0:D], hT[q][:, c * P:(c + 1) * P], w2[:, bass.ds(e, 1), c, :],
                                                 start=(c == 0), stop=(c == NC - 1))
                            last.then_inc(down[q], 1)

                        def after(i, k, by):
                            return (i, k + by) if k + by < GROUP else (i + 1, k + by - GROUP)

                        regs = [pe.alloc_register(f"{name}_expert{k}") for k in range(GROUP + 1)]

                        def turn(i, last_turn):
                            pe.reg_load(regs, block_expert[0:1, bass.ds(GROUP * i, GROUP + 1)])
                            e = [pe.snap(r, min_val=0, max_val=E - 1) for r in regs]
                            for k in range(GROUP):
                                turn_hidden(i, k)
                                if not (last_turn and k + 1 >= GROUP):
                                    go_up(*after(i, k, 1), e[k + 1])
                                come_down(i, k, e[k])
                                if not (last_turn and k + 2 >= GROUP):
                                    turn_rows(*after(i, k, 2))

                        pe.wait_ge(experts_known, 1)
                        turn_rows(0, 0)
                        turn_rows(0, 1)
                        pe.reg_load(regs[0:1], block_expert[0:1, 0:1])
                        go_up(0, 0, pe.snap(regs[0], min_val=0, max_val=E - 1))
                        @turns(pe, TURNS - 1)
                        def _(i):
                            turn(i, False)
                        turn(TURNS - 1, True)

                    @block.scalar
                    def _(act):
                        @turns(act, BATCHES // 2)
                        def _(i):
                            for q in range(2):
                                act.wait_ge(columns[q], i + 1)
                                wait(act, logits_done[q], i)
                                if shared:
                                    wait(act, all_columns[q], i)
                                act.activation(xT[q][:], bank[q][:], ACT.Copy).then_inc(columns_copied[q], 1)
                        act.wait_ge(centred, 1)
                        e = flat(work[:]) if choices == 1 else other[:]
                        act.activation(e, e, ACT.Exp).then_inc(exped, 1)
                        if shared:
                            @turns(act, BATCHES // 2)
                            def _(i):
                                for q in range(2):
                                    wait(act, sh_down[q], i)
                                    for c in range(NC):
                                        act.wait_ge(sh_up, 2 * NC * i + NC * q + c + 1)
                                        act.activation(sh[q][:, c, :], bank[c][:], func).then_inc(sh_act[c], 1)

                        def activate(i, k):
                            q, n = parity(i, k)
                            act.wait_ge(up[q], n + 1)
                            wait(act, h_turned[q], n)
                            act.activation(h[q][:], bank[2 + q][:, 0:F], func).then_inc(activated[q], 1)

                        def copy_y(i, k):
                            q, n = parity(i, k)
                            act.wait_ge(down[q], n + 1)
                            wait(act, y_stored[k], 16 * i + stored0)
                            act.activation(y[k][:], bank[6 + q][:, 0:D], ACT.Copy).then_inc(y_copied[q], 1)

                        def turn(i, last_turn):
                            for k in range(GROUP):
                                if not (last_turn and k + 1 >= GROUP):
                                    activate(i if k + 1 < GROUP else i + 1, (k + 1) % GROUP)
                                copy_y(i, k)

                        activate(0, 0)
                        @turns(act, TURNS - 1)
                        def _(i):
                            turn(i, False)
                        turn(TURNS - 1, True)

                    @block.vector
                    def _(v):
                        own = Chain(v, f"{name}_route")
                        row_norm(v, own, stats[:], rstd[:], shift[:], D, scope, name)
                        @turns(v, BATCHES // 2)
                        def _(i):
                            for q in range(2):
                                wait(v, columns[q], i)
                                wait(v, rows_kept[q], i)
                                for k in range(BT):
                                    tile = 8 * i + BT * q + k
                                    last = normed(v, xw[q][:, k, :], tile, one(X, tile))
                                last.then_inc(normed_rows[q], 1)
                            if shared:
                                for q in range(2):
                                    v.wait_ge(columns_copied[q], i + 1)
                                    v.tensor_copy(xnT[:, bass.ds((2 * i + q) * SEQ, SEQ)], xT[q][:]).then_inc(all_columns[q], 1)
                        for q in range(2):
                            v.wait_ge(logits_done[q], BATCHES // 2)
                        prefer = const("prefer").rearrange("p (e t) -> p e t", e=E)

                        def first_of_best(dst, value, top):
                            own(v.tensor_tensor(dst, value, per_token(top), ALU.is_equal))
                            own(v.tensor_tensor(dst, dst, prefer, ALU.mult))
                            own(v.tensor_reduce(other[:], over_experts(dst), AX.X, ALU.max))
                            own(v.tensor_tensor(dst, dst, per_token(other[:]), ALU.is_equal))

                        if choices == 1:
                            own(v.tensor_reduce(best[:], over_experts(logits), AX.X, ALU.max))
                            v.tensor_tensor(work[:], logits, per_token(best[:]), ALU.subtract).then_inc(centred, 1)
                            v.wait_ge(exped, 1)
                            own(v.tensor_reduce(best[:], over_experts(work[:]), AX.X, ALU.add))
                            own(v.reciprocal(best[:], best[:]))
                            own(v.tensor_tensor(score[:], work[:], per_token(best[:]), ALU.mult))
                            own(v.memset(thr[:], 0.0))
                            own(v.tensor_scalar(cand[:].bitcast(I32), thr[:].bitcast(I32), 1 << (BITS - 1), None, ALU.bitwise_or))
                            v.tensor_copy(by_tile[:], over_experts(score[:])).then_inc(prob_ready, 1)
                            v.wait_ge(prob_turned, 1)
                            own(v.tensor_copy(prob_rows[:], bank[0][:, 0:2 * P]))
                            steps = 3
                            bit = Chain(v, f"{name}_bit")
                            with v.Fori(0, BITS) as i:
                                bit.start(steps * i)
                                v.tensor_scalar(hits[:], prob_rows[:], cand[:], None, ALU.is_ge, ALU.add, accum_out=count[:]) \
                                    .then_inc(counted, 1)
                                v.wait_ge(summed, i + 1)
                                bit(v.scalar_tensor_tensor(cand[:], bank[1][:, 0:1], float(CAP), cand[:], ALU.is_ge, ALU.mult))
                                bit(v.tensor_tensor(thr[:], thr[:], cand[:], ALU.max))
                                bit(v.tensor_tensor(cand[:].bitcast(I32), thr[:].bitcast(I32), one(bit_table, i), ALU.bitwise_or))
                                assert bit.n == steps
                            v.tensor_copy(count[:], thr[:]).then_inc(thr_ready, 1)
                            v.wait_ge(thr_spread, 1)
                            own(v.tensor_copy(small[0][:], bank[1][:, 0:E]))
                            v.tensor_tensor(work[:], score[:], per_expert(small[0][:]), ALU.is_gt).then_inc(ties_ready, 1)
                            v.tensor_tensor(pick[:], score[:], per_expert(small[0][:]), ALU.is_equal).then_inc(ties_ready, 1)
                            v.wait_ge(ties_summed, 1)
                            own(v.tensor_reduce(small[1][:], sum_above, AX.X, ALU.add))
                            own(v.tensor_scalar(small[1][:], small[1][:], -1.0, float(CAP), ALU.mult, ALU.add))
                            own(v.tensor_tensor_scan(flat(pick2[:]), const("restart"), flat(sum_tile), 0.0, ALU.mult, ALU.add))
                            own(v.tensor_tensor(pick2[:], pick2[:], sum_tile, ALU.subtract))
                            own(v.tensor_tensor(pick2[:], pick2[:], sum_before, ALU.add))
                            own(v.tensor_tensor(pick2[:], pick2[:], per_expert(small[1][:]), ALU.is_lt))
                            own(v.tensor_tensor(pick2[:], pick2[:], pick[:], ALU.mult))
                            own(v.tensor_tensor(pick2[:], pick2[:], work[:], ALU.add))
                            own(v.tensor_reduce(best[:], over_experts(pick2[:]), AX.X, ALU.max))
                            own(v.tensor_scalar(best[:], best[:], -1.0, 1.0, ALU.mult, ALU.add))
                            own(v.tensor_tensor(pick2[:], pick2[:], per_token(best[:]), ALU.max))
                            own(v.tensor_tensor(score[:], score[:], pick2[:], ALU.mult))
                            own(v.tensor_scalar(pick2[:], pick2[:], -1.0, None, ALU.add))
                            own(v.tensor_tensor(score[:], score[:], pick2[:], ALU.add))
                            own(v.tensor_reduce(gate[0][:], over_experts(score[:]), AX.X, ALU.max))
                            first_of_best(work[:], score[:], gate[0][:])
                            v.tensor_scalar(gate[0][:], gate[0][:], 0.5, None, ALU.mult).then_inc(picked, 1)
                            chosen = [work]
                        else:
                            own(v.tensor_copy(score[:], logits))
                            own(v.tensor_reduce(best[:], over_experts(score[:]), AX.X, ALU.max))
                            first_of_best(pick[:], score[:], best[:])
                            own(v.tensor_scalar(work[:], pick[:], -1.0, 1.0, ALU.mult, ALU.add))
                            own(v.tensor_tensor(score[:], score[:], work[:], ALU.mult))
                            own(v.scalar_tensor_tensor(flat(score[:]), flat(pick[:]), NEG, flat(score[:]), ALU.mult, ALU.add))
                            own(v.tensor_reduce(gate[1][:], over_experts(score[:]), AX.X, ALU.max))
                            first_of_best(pick2[:], score[:], gate[1][:])
                            v.tensor_tensor(work[:], pick[:], pick2[:], ALU.add).then_inc(picked, 1)
                            v.tensor_tensor(other[:], gate[1][:], best[:], ALU.subtract).then_inc(centred, 1)
                            v.wait_ge(exped, 1)
                            own(v.tensor_scalar(best[:], other[:], 1.0, None, ALU.add))
                            own(v.reciprocal(best[:], best[:]))
                            own(v.tensor_scalar(gate[0][:], best[:], 0.5, None, ALU.mult))
                            own(v.tensor_tensor(gate[1][:], gate[0][:], other[:], ALU.mult))
                            chosen = [pick, pick2]
                        v.wait_ge(picks_summed, 1)
                        own(v.tensor_tensor_scan(flat(score[:]), const("ones")[:, 0:1].to_broadcast([P, E * TILES]),
                                                 flat(sum_tile), 0.0, ALU.mult, ALU.add))
                        own(v.tensor_tensor(score[:], score[:], sum_tile, ALU.subtract))
                        own(v.tensor_reduce(small[0][:], sum_tile, AX.X, ALU.add))
                        own(v.tensor_scalar(small_i[:], small[0][:], float(P - 1), None, ALU.add))
                        log_p = P.bit_length() - 1
                        own(v.tensor_scalar(small_i[:], small_i[:], log_p, log_p, ALU.logical_shift_right, ALU.logical_shift_left))
                        own(v.tensor_copy(small[1][:], small_i[:]))
                        own(v.tensor_tensor_scan(small[2][:], const("ones")[:, 0:E], small[1][:], 0.0, ALU.mult, ALU.add))
                        own(v.tensor_tensor(small[2][:], small[2][:], small[1][:], ALU.subtract))
                        own(v.tensor_tensor(small[3][:], small[2][:], score[:, :, 0], ALU.subtract))
                        own(v.tensor_tensor(score[:], score[:], sum_before, ALU.add))
                        own(v.tensor_tensor(score[:], score[:], per_expert(small[3][:]), ALU.add))
                        for k, c in enumerate(chosen):
                            own(v.tensor_tensor(c[:], c[:], score[:], ALU.mult))
                            own(v.tensor_reduce(best[:], over_experts(c[:]), AX.X, ALU.add))
                            v.tensor_copy(pos[k][:], best[:]).then_inc(pos_ready, 1)
                            v.wait_ge(pos_ready, k + 1)
                        own(v.tensor_tensor(begun[:], const("block_row")[:, 0:NB].unsqueeze(2).broadcast_to([P, NB, E]),
                                            small[2][:].unsqueeze(1).broadcast_to([P, NB, E]), ALU.is_ge))
                        own(v.tensor_reduce(begun_by[:], begun[:], AX.X, ALU.add))
                        own(v.memset(block_expert[:], 0))
                        v.tensor_scalar(block_expert[:, 0:NB], begun_by[:], -1.0, None, ALU.add).then_inc(experts_known, 1)

                        if shared:
                            @turns(v, BATCHES // 2)
                            def _(i):
                                for q in range(2):
                                    v.wait_ge(sh_down[q], i + 1)
                                    part = X[:, bass.ds((2 * i + q) * BT, BT), :].rearrange("p t d -> p (t d)")
                                    v.scalar_tensor_tensor(part, bank[6 + q][:], 0.5, part, ALU.mult, ALU.add).then_inc(sh_added[q], 1)

                        def copy_columns(i, k):
                            q, n = parity(i, k)
                            v.wait_ge(turned[q], n + 1)
                            wait(v, up[q], n)
                            v.tensor_copy(bxT[q][:], bank[q][:, 0:P]).then_inc(xT_copied[q], 1)

                        def copy_hidden(i, k):
                            q, n = parity(i, k)
                            v.wait_ge(h_turned[q], n + 1)
                            wait(v, down[q], n)
                            v.tensor_copy(hT[q][:], bank[4 + q][:, 0:F]).then_inc(hT_copied[q], 1)

                        def turn(i, last_turn):
                            for k in range(GROUP):
                                copy_hidden(i, k)
                                if not (last_turn and k + 2 >= GROUP):
                                    copy_columns(i if k + 2 < GROUP else i + 1, (k + 2) % GROUP)

                        copy_columns(0, 0)
                        copy_columns(0, 1)
                        @turns(v, TURNS - 1)
                        def _(i):
                            turn(i, False)
                        turn(TURNS - 1, True)

                        if shared:
                            for q in range(2):
                                v.wait_ge(sh_added[q], BATCHES // 2)
                        @turns(v, choices * TILES // SLOTS)
                        def _(i):
                            for k in range(SLOTS):
                                tile = (SLOTS // choices) * i + k // choices
                                v.wait_ge(gathered[k], 16 * (i + 1) + gathered0)
                                v.scalar_tensor_tensor(one(X, tile), got[k][:].unsqueeze(1), one(gate[k % choices], tile), one(X, tile),
                                                       ALU.mult, ALU.add).then_inc(used, 1)
                                v.wait_ge(used, SLOTS * i + k + 1)
                                if k % choices == choices - 1 and not final:
                                    v.bn_stats(one(stats, tile), one(X, tile))

                    @block.sync
                    def _(sp):
                        clear_last_phase(sp)
                        sp.wait_ge(scattered, 16 * TILES * choices + scattered0)
                        @turns(sp, TURNS)
                        def _(i):
                            for k in range(GROUP):
                                q, n = parity(i, k)
                                wait(sp, turned[q], 2 * i)
                                sp.dma_start(rows_in[k][:], sorted_x[bass.ds((GROUP * i + k) * P, P), :]).then_inc(blk_loaded[k], 16)
                        if final:
                            @turns(sp, choices * TILES // SLOTS)
                            def _(i):
                                sp.wait_ge(used, SLOTS * (i + 1))
                                n = SLOTS // choices
                                sp.dma_start(out[bass.ds(n * P * i, n * P), :].rearrange("(t p) d -> p t d", p=P),
                                             X[:, bass.ds(n * i, n), :]).then_inc(sent, 16)
                            sp.wait_ge(sent, 16 * choices * TILES // SLOTS)

                    @block.gpsimd
                    def _(pool):
                        @turns(pool, BATCHES // 2)
                        def _(i):
                            for q in range(2):
                                pool.wait_ge(normed_rows[q], i + 1)
                                pool.tensor_copy(xn[:, bass.ds((2 * i + q) * BT, BT), :], xw[q][:]).then_inc(rows_kept[q], 1)
                        for q in range(2):
                            pool.wait_ge(rows_kept[q], BATCHES // 2)
                        for k in range(choices):
                            pool.wait_ge(pos_ready, k + 1)
                            for tile in range(TILES):
                                pool.indirect_dma_start(sorted_x, bass.IndirectOffsetOnAxis(ap=pos[k][:, tile:tile + 1], axis=0),
                                                        xn[:, tile, :], None).then_inc(scattered, 16)
                        @turns(pool, TURNS)
                        def _(i):
                            for k in range(GROUP):
                                q, n = parity(i, k)
                                pool.wait_ge(y_copied[q], n + 1)
                                pool.dma_start(sorted_y[bass.ds((GROUP * i + k) * P, P), :], y[k][:]).then_inc(y_stored[k], 16)
                        for k in range(GROUP):
                            pool.wait_ge(y_stored[k], 16 * TURNS + stored0)
                        for n in range(choices * TILES):
                            tile, k, slot = n // choices, n % choices, n % SLOTS
                            if n >= SLOTS:
                                pool.wait_ge(used, n - SLOTS + 1)
                            pool.indirect_dma_start(got[slot][:], None, sorted_y[0:NB * P], bass.IndirectOffsetOnAxis(ap=pos[k][:, tile:tile + 1], axis=0)) \
                                .then_inc(gathered[slot], 16)

        def attention():
            scope = ExitStack()

            def s2(n):
                return pair(f"attn_{n}")

            def t(n, shape, dt=F32):
                return sb(scope, f"attn_{n}", shape, dt)

            normed_rows, columns, columns_copied = s2("normed_rows"), s2("columns"), s2("columns_copied")
            k_done, q_done, v_done, k_max, k_exped = s2("k_done"), s2("q_done"), s2("v_done"), s2("k_max"), s2("k_exped")
            q_centred, q_exped, q_ready, v_ready = s2("q_centred"), s2("q_exped"), s2("q_ready"), s2("v_ready")
            k_turned, k_copied, state_done, state_ready = s2("k_turned"), s2("k_copied"), s2("state_done"), s2("state_ready")
            q_turned, q_copied, mixed, kept = s2("q_turned"), s2("q_copied"), s2("mixed"), s2("kept")
            again, turned, affine, projected, added = s2("again"), s2("turned"), s2("affine"), s2("projected"), s2("added")
            measured, summed_rows = sem("attn_measured"), sem("attn_summed_rows")

            with scope:
                mix = t("mix", [P, TILES, D])
                mix_stats = t("mix_stats", [P, TILES, 6])
                mix_rstd, mix_shift = t("mix_rstd", [P, TILES]), t("mix_shift", [P, TILES])
                xw, xT = [t(f"xw{p}", [P, BT, D]) for p in range(2)], [t(f"xT{p}", [P, SEQ]) for p in range(2)]
                kx, kxT = [t(f"kx{p}", [P, SEQ]) for p in range(2)], [t(f"kxT{p}", [P, SEQ]) for p in range(2)]
                qx, qxT = [t(f"qx{p}", [P, BT, D]) for p in range(2)], [t(f"qxT{p}", [P, SEQ]) for p in range(2)]
                vx = [t(f"vx{p}", [P, BT, D]) for p in range(2)]
                state = [t(f"state{p}", [P, D]) for p in range(2)]
                kmax, kbias, ksum, krec = ([t(f"{n}{p}", [P, 1]) for p in range(2)] for n in ("kmax", "kbias", "ksum", "krec"))
                head = t("head", [P, BT * HEADS])
                sumrow = t("sumrow", [P, BT, D])
                bk = vec[:, V_BK:V_BK + 1]

                def along(which):
                    return row[:, which:which + D].unsqueeze(1).broadcast_to([P, BT, D])

                def tiles(ap):
                    return ap.rearrange("p (t d) -> p t d", t=BT)

                def heads(ap):
                    return ap.rearrange("p t (h d) -> p (t h) d", d=HD)

                def by_head(ap):
                    return ap.unsqueeze(2).broadcast_to([P, BT * HEADS, HD])

                wq, wk, wv, wo = (wattn[:, n, :] for n in range(4))

                with nc.Block() as block:
                    @block.sync
                    def _(sp):
                        clear_last_phase(sp)

                    @block.tensor
                    def _(pe):
                        def project(i, p):
                            pe.wait_ge(normed_rows[p], i + 1)
                            wait(pe, columns_copied[1 - p], i + p)
                            for k in range(BT):
                                last = pe.transpose(bank[0][:, k * P:(k + 1) * P], xw[p][:, k, :], ident)
                            last.then_inc(columns[p], 1)
                            pe.wait_ge(columns_copied[p], i + 1)
                            wait(pe, k_exped[1 - p], i + p)
                            pe.matmul(bank[1][:], wk, xT[p][:], start=True, stop=True).then_inc(k_done[p], 1)
                            wait(pe, q_centred[1 - p], i + p)
                            for k in range(BT):
                                last = pe.matmul(bank[2][:, k * P:(k + 1) * P], xT[p][:, k * P:(k + 1) * P], wq, start=True, stop=True)
                            last.then_inc(q_done[p], 1)
                            wait(pe, v_ready[1 - p], i + p)
                            for k in range(BT):
                                last = pe.matmul(bank[3][:, k * P:(k + 1) * P], xT[p][:, k * P:(k + 1) * P], wv, start=True, stop=True)
                            last.then_inc(v_done[p], 1)

                        def attend(i, p):
                            pe.wait_ge(k_exped[p], i + 1)
                            wait(pe, k_copied[1 - p], i + p)
                            for k in range(BT):
                                last = pe.transpose(bank[4][:, k * P:(k + 1) * P], kx[p][:, k * P:(k + 1) * P], ident)
                            last.then_inc(k_turned[p], 1)
                            pe.wait_ge(q_ready[p], i + 1)
                            wait(pe, q_copied[1 - p], i + p)
                            for k in range(BT):
                                last = pe.transpose(bank[6][:, k * P:(k + 1) * P], qx[p][:, k, :], ident)
                            last.then_inc(q_turned[p], 1)
                            pe.wait_ge(k_copied[p], i + 1)
                            pe.wait_ge(v_ready[p], i + 1)
                            wait(pe, state_ready[1 - p], i + p)
                            for k in range(BT):
                                last = pe.matmul(bank[5][:, 0:D], kxT[p][:, k * P:(k + 1) * P], vx[p][:, k, :],
                                                 start=(k == 0), stop=(k == BT - 1))
                            last.then_inc(state_done[p], 1)
                            pe.wait_ge(state_ready[p], i + 1)
                            pe.wait_ge(q_copied[p], i + 1)
                            wait(pe, kept[1 - p], i + p)
                            for k in range(BT):
                                last = pe.matmul(bank[7][:, k * P:(k + 1) * P], qxT[p][:, k * P:(k + 1) * P], state[p][:], start=True, stop=True)
                            last.then_inc(mixed[p], 1)

                        @turns(pe, BATCHES // 2)
                        def _(i):
                            for p in range(2):
                                project(i, p)
                            for p in range(2):
                                attend(i, p)
                        for p in range(2):
                            pe.wait_ge(kept[p], BATCHES // 2)
                        @turns(pe, BATCHES // 2)
                        def _(i):
                            for p in range(2):
                                pe.wait_ge(again[p], i + 1)
                                wait(pe, affine[p], i)
                                for k in range(BT):
                                    last = pe.transpose(bank[p][:, k * P:(k + 1) * P], xw[p][:, k, :], ident)
                                last.then_inc(turned[p], 1)
                            for p in range(2):
                                pe.wait_ge(affine[p], i + 1)
                                wait(pe, added[p], i)
                                for k in range(BT):
                                    last = pe.matmul(bank[2 + p][:, k * P:(k + 1) * P], xT[p][:, k * P:(k + 1) * P], wo, start=True, stop=True)
                                last.then_inc(projected[p], 1)

                    @block.scalar
                    def _(act):
                        def project(i, p):
                            act.wait_ge(columns[p], i + 1)
                            wait(act, v_done[p], i)
                            act.activation(xT[p][:], bank[0][:], ACT.Copy).then_inc(columns_copied[p], 1)
                            act.wait_ge(k_max[p], i + 1)
                            wait(act, k_turned[p], i)
                            act.activation(kx[p][:], bank[1][:], ACT.Exp, bias=kbias[p][:], accum_out=ksum[p][:]).then_inc(k_exped[p], 1)
                            act.wait_ge(q_centred[p], i + 1)
                            act.activation(qx[p][:], qx[p][:], ACT.Exp).then_inc(q_exped[p], 1)

                        def attend(i, p):
                            act.wait_ge(k_turned[p], i + 1)
                            wait(act, state_done[p], i)
                            act.activation(kxT[p][:], bank[4][:], ACT.Copy).then_inc(k_copied[p], 1)
                            act.wait_ge(q_turned[p], i + 1)
                            wait(act, mixed[p], i)
                            act.activation(qxT[p][:], bank[6][:], ACT.Copy).then_inc(q_copied[p], 1)

                        @turns(act, BATCHES // 2)
                        def _(i):
                            for p in range(2):
                                project(i, p)
                            for p in range(2):
                                attend(i, p)
                        @turns(act, BATCHES // 2)
                        def _(i):
                            for p in range(2):
                                act.wait_ge(turned[p], i + 1)
                                wait(act, projected[p], i)
                                act.activation(xT[p][:], bank[p][:], ACT.Identity, scale=vec[:, V_LNG:V_LNG + 1],
                                               bias=vec[:, V_LNB:V_LNB + 1]).then_inc(affine[p], 1)

                    @block.vector
                    def _(v):
                        own = Chain(v, "attn_own")
                        row_norm(v, own, stats[:], rstd[:], shift[:], D, scope, "attn_in")
                        loop = Chain(v, "attn_loop")
                        per_seq = 7

                        def project(i, p):
                            loop.start(per_seq * (2 * i + p))
                            wait(v, columns[p], i)
                            for k in range(BT):
                                tile = 2 * BT * i + BT * p + k
                                last = normed(v, xw[p][:, k, :], tile, one(X, tile))
                            last.then_inc(normed_rows[p], 1)
                            v.wait_ge(k_done[p], i + 1)
                            loop(v.tensor_reduce(kmax[p][:], bank[1][:], AX.X, ALU.max))
                            loop(v.tensor_scalar(kbias[p][:], kmax[p][:], bk, -1.0, ALU.add, ALU.mult))
                            v.tensor_tensor(kbias[p][:], kbias[p][:], bk, ALU.add).then_inc(k_max[p], 1)
                            v.wait_ge(q_done[p], i + 1)
                            wait(v, q_turned[p], i)
                            loop(v.tensor_tensor(qx[p][:], tiles(bank[2][:]), along(R_BQ), ALU.add))
                            loop(v.tensor_reduce(head[:], heads(qx[p][:]), AX.X, ALU.max))
                            v.tensor_tensor(heads(qx[p][:]), heads(qx[p][:]), by_head(head[:]), ALU.subtract).then_inc(q_centred[p], 1)
                            v.wait_ge(v_done[p], i + 1)
                            wait(v, state_done[p], i)
                            v.tensor_tensor(vx[p][:], tiles(bank[3][:]), along(R_BV), ALU.add).then_inc(v_ready[p], 1)
                            v.wait_ge(q_exped[p], i + 1)
                            loop(v.tensor_reduce(head[:], heads(qx[p][:]), AX.X, ALU.add))
                            loop(v.reciprocal(head[:], head[:]))
                            v.tensor_tensor(heads(qx[p][:]), heads(qx[p][:]), by_head(head[:]), ALU.mult).then_inc(q_ready[p], 1)
                            v.wait_ge(k_exped[p], i + 1)
                            loop(v.reciprocal(krec[p][:], ksum[p][:]))
                            assert loop.n == per_seq

                        def attend(i, p):
                            v.wait_ge(state_done[p], i + 1)
                            wait(v, mixed[p], i)
                            v.scalar_tensor_tensor(state[p][:], bank[5][:, 0:D], krec[p][:], const("head_mask"), ALU.mult, ALU.mult) \
                                .then_inc(state_ready[p], 1)
                            v.wait_ge(mixed[p], i + 1)
                            part = mix[:, bass.ds((2 * i + p) * BT, BT), :]
                            v.tensor_copy(part, tiles(bank[7][:])).then_inc(kept[p], 1)
                            v.wait_ge(kept[p], i + 1)
                            for k in range(BT):
                                tile = 2 * BT * i + BT * p + k
                                v.bn_stats(one(mix_stats, tile), one(mix, tile)).then_inc(measured, 1)

                        @turns(v, BATCHES // 2)
                        def _(i):
                            for p in range(2):
                                project(i, p)
                            for p in range(2):
                                attend(i, p)
                        v.wait_ge(measured, TILES)
                        row_norm(v, own, mix_stats[:], mix_rstd[:], mix_shift[:], D, scope, "attn_mix")
                        @turns(v, BATCHES // 2)
                        def _(i):
                            for p in range(2):
                                wait(v, turned[p], i)
                                for k in range(BT):
                                    tile = 2 * BT * i + BT * p + k
                                    last = v.tensor_scalar(xw[p][:, k, :], one(mix, tile), one(mix_rstd, tile), one(mix_shift, tile), ALU.mult, ALU.add)
                                last.then_inc(again[p], 1)
                            for p in range(2):
                                v.wait_ge(projected[p], i + 1)
                                part = X[:, bass.ds((2 * i + p) * BT, BT), :]
                                v.tensor_tensor(sumrow[:], tiles(bank[2 + p][:]), along(R_BO), ALU.add).then_inc(added[p], 1)
                                v.wait_ge(added[p], i + 1)
                                v.tensor_tensor(part, part, sumrow[:], ALU.add).then_inc(summed_rows, 1)
                                v.wait_ge(summed_rows, 2 * i + p + 1)
                                for k in range(BT):
                                    tile = 2 * BT * i + BT * p + k
                                    v.bn_stats(one(stats, tile), one(X, tile))

        def mamba():
            scope = ExitStack()

            def s(n):
                return sem(f"mamba_{n}")

            def s2(n):
                return pair(f"mamba_{n}")

            def t(n, shape, dt=F32):
                return sb(scope, f"mamba_{n}", shape, dt)

            normed_rows, columns, columns_copied, all_columns = s2("normed_rows"), s2("columns"), s2("columns_copied"), s2("all_columns")
            dt_done, u_done, u_ready = s2("dt_done"), s2("u_done"), s2("u_ready")
            dt_clipped, dt_exped, dt_plus1, dt_logged = s("dt_clipped"), s("dt_exped"), s("dt_plus1"), s("dt_logged")
            rates_ready, cs_done, cs_ready, last_done, dec_ready, decays_ready = (
                s(n) for n in ("rates_ready", "cs_done", "cs_ready", "last_done", "dec_ready", "decays_ready"))
            in_done, in_copied, conv_done, relu_done, conv_ready = s("in_done"), s("in_copied"), s("conv_done"), s("relu_done"), s("conv_ready")
            x_turned, x_copied, seg_done, seg_shifted, seg_exped = s("x_turned"), s("x_copied"), s("seg_done"), s("seg_shifted"), s("seg_exped")
            cb_done, weights_ready, y_done, y_read, state_done, state_ready = (
                s(n) for n in ("cb_done", "weights_ready", "y_done", "y_read", "state_done", "state_ready"))
            again, turned, affine, projected, added = s2("again"), s2("turned"), s2("affine"), s2("projected"), s2("added")
            pads, least_done, cs_here = s("pads"), s("least_done"), s("cs_here")
            u_measured = s("u_measured")

            with scope:
                u = t("u", [P, TILES, INNER])
                xT_all = t("xT_all", [P, TOKENS])
                rates, cs, dec, ecs, elast = (t(n, [P, TILES * MH]) for n in ("rates", "cs", "dec", "ecs", "elast"))
                small = [t(f"small{k}", [P, TILES * MH]) for k in range(4)]
                expA = t("expA", [P, MH])
                out_rstd, out_shift = t("out_rstd", [P, TILES]), t("out_shift", [P, TILES])
                u_stats = t("u_stats", [P, TILES, 6])
                seg, weights = t("seg", [P, MH, P]), t("weights", [P, MH, P])
                xdec, ytmp = t("xdec", [P, INNER]), t("ytmp", [P, INNER])
                carry = t("carry", [STATE, INNER])
                carry_dec = t("carry_dec", [STATE, INNER])

                def tiles(ap):
                    return ap.rearrange("p (t d) -> p t d", t=BT)

                with ExitStack() as inner_scope, nc.Block() as block:
                    xw = [sb(inner_scope, f"mamba_xw{p}", [P, BT, D]) for p in range(2)]
                    xT = [sb(inner_scope, f"mamba_xT{p}", [P, SEQ]) for p in range(2)]
                    dt_bank = bank[6][:, 0:TILES * MH]

                    @block.sync
                    def _(sp):
                        clear_last_phase(sp)

                    @block.tensor
                    def _(pe):
                        @turns(pe, BATCHES // 2)
                        def _(i):
                            for p in range(2):
                                pe.wait_ge(normed_rows[p], i + 1)
                                wait(pe, columns_copied[p], i)
                                for k in range(BT):
                                    last = pe.transpose(bank[p][:, k * P:(k + 1) * P], xw[p][:, k, :], ident)
                                last.then_inc(columns[p], 1)
                            for p in range(2):
                                pe.wait_ge(columns_copied[p], i + 1)
                                for k in range(BT):
                                    last = pe.matmul(bank[6][:, bass.ds(MH * (2 * BT * i + BT * p + k), MH)], xT[p][:, k * P:(k + 1) * P],
                                                     win1[:, CH:CH + MH], start=True, stop=True)
                                last.then_inc(dt_done[p], 1)
                                wait(pe, u_ready[p], i)
                                for k in range(BT):
                                    last = pe.matmul(bank[2 + 2 * p + k // 2][:, (k % 2) * INNER:(k % 2 + 1) * INNER], xT[p][:, k * P:(k + 1) * P],
                                                     win2[:], start=True, stop=True)
                                last.then_inc(u_done[p], 1)
                        pe.wait_ge(rates_ready, 1)
                        pe.wait_ge(u_ready[1], BATCHES // 2)
                        pe.matmul(bank[7][:, 0:TILES * MH], const("upto"), rates[:], start=True, stop=True).then_inc(cs_done, 1)
                        pe.wait_ge(cs_ready, 1)
                        pe.matmul(bank[5][:, 0:TILES * MH], const("last_row"), cs[:], start=True, stop=True).then_inc(last_done, 1)

                    @block.scalar
                    def _(act):
                        @turns(act, BATCHES // 2)
                        def _(i):
                            for p in range(2):
                                act.wait_ge(columns[p], i + 1)
                                wait(act, u_done[p], i)
                                wait(act, all_columns[p], i)
                                act.activation(xT[p][:], bank[p][:], ACT.Copy).then_inc(columns_copied[p], 1)
                            for p in range(2):
                                act.wait_ge(u_done[p], i + 1)
                                for k in range(2):
                                    last = act.activation(u[:, bass.ds((2 * i + p) * BT + 2 * k, 2), :].rearrange("p t d -> p (t d)"),
                                                          bank[2 + 2 * p + k][:], ACT.Gelu)
                                last.then_inc(u_ready[p], 1)
                        act.activation(expA[:], row[:, R_ALOG:R_ALOG + MH], ACT.Exp)
                        act.wait_ge(dt_clipped, 1)
                        act.activation(small[0][:], small[0][:], ACT.Exp).then_inc(dt_exped, 1)
                        act.wait_ge(dt_plus1, 1)
                        act.activation(small[2][:], small[1][:], ACT.Ln).then_inc(dt_logged, 1)
                        act.wait_ge(dec_ready, 1)
                        act.activation(dec[:], dec[:], ACT.Exp)
                        act.activation(ecs[:], cs[:], ACT.Exp)
                        act.activation(elast[:], bank[5][:, 0:TILES * MH], ACT.Exp).then_inc(decays_ready, 1)

                    @block.vector
                    def _(v):
                        own = Chain(v, "mamba_own")
                        row_norm(v, own, stats[:], rstd[:], shift[:], D, inner_scope, "mamba_in")
                        @turns(v, BATCHES // 2)
                        def _(i):
                            for p in range(2):
                                wait(v, columns[p], i)
                                for k in range(BT):
                                    tile = 2 * BT * i + BT * p + k
                                    last = normed(v, xw[p][:, k, :], tile, one(X, tile))
                                last.then_inc(normed_rows[p], 1)
                            for p in range(2):
                                v.wait_ge(columns_copied[p], i + 1)
                                v.tensor_copy(xT_all[:, bass.ds((2 * i + p) * SEQ, SEQ)], xT[p][:]).then_inc(all_columns[p], 1)
                        for p in range(2):
                            v.wait_ge(dt_done[p], BATCHES // 2)
                        y, y1, ln, den = (a[:] for a in small)
                        v.tensor_scalar(y, dt_bank, 20.0, None, ALU.min).then_inc(dt_clipped, 1)
                        v.wait_ge(dt_exped, 1)
                        v.tensor_scalar(y1, y, 1.0, None, ALU.add).then_inc(dt_plus1, 1)
                        v.wait_ge(dt_plus1, 1)
                        own(v.tensor_scalar(den, y1, -1.0, None, ALU.add))
                        own(v.tensor_scalar(rates[:], den, 0.0, None, ALU.is_equal))
                        own(v.tensor_tensor(den, den, rates[:], ALU.add))
                        own(v.reciprocal(den, den))
                        v.wait_ge(dt_logged, 1)
                        own(v.tensor_tensor(ln, ln, rates[:], ALU.add))
                        own(v.tensor_tensor(ln, ln, den, ALU.mult))
                        own(v.tensor_tensor(ln, ln, y, ALU.mult))
                        own(v.scalar_tensor_tensor(ln, dt_bank, 20.0, ln, ALU.is_le, ALU.mult))
                        own(v.tensor_scalar(y, dt_bank, 20.0, None, ALU.is_gt))
                        own(v.tensor_tensor(y, y, dt_bank, ALU.mult))
                        own(v.tensor_tensor(ln, ln, y, ALU.add))
                        by_head = rates[:].rearrange("p (t h) -> p t h", h=MH)
                        v.scalar_tensor_tensor(by_head, ln.rearrange("p (t h) -> p t h", h=MH), -1.0,
                                               expA[:].unsqueeze(1).broadcast_to([P, TILES, MH]), ALU.mult, ALU.mult).then_inc(rates_ready, 1)
                        v.wait_ge(cs_done, 1)
                        v.tensor_copy(cs[:], bank[7][:, 0:TILES * MH]).then_inc(cs_ready, 1)
                        v.wait_ge(last_done, 1)
                        v.wait_ge(cs_ready, 1)
                        v.tensor_tensor(dec[:], bank[5][:, 0:TILES * MH], cs[:], ALU.subtract).then_inc(dec_ready, 1)

                with ExitStack() as inner_scope, nc.Block() as block:
                    def tt(n, shape):
                        return sb(inner_scope, f"mamba_{n}", shape)

                    cs_now = tt("cs_now", [P, BT * MH])
                    padded = tt("padded", [P, CC, TAPS - 1 + SEQ])
                    relu, least = tt("relu", [P, SEQ]), tt("least", [P, SEQ])
                    xconv = tt("xconv", [P, 2, SEQ])
                    bcT = [tt(f"bcT{p}", [P, SEQ]) for p in range(2)]
                    bT = [b[0:STATE] for b in bcT]
                    cT = [tt(f"cT{p}", [STATE, SEQ]) for p in range(2)]
                    xs = [tt(f"xs{p}", [P, BT, INNER]) for p in range(2)]
                    bs = [tt(f"bs{p}", [P, BT, STATE]) for p in range(2)]

                    def stages(eng, stage):
                        stage((0, 0), None)
                        stage((1, 1), (0, 0))
                        with eng.Fori(0, (BATCHES - 2) // 2) as i:
                            stage((2 * i + 2, 0), (2 * i + 1, 1))
                            stage((2 * i + 3, 1), (2 * i + 2, 0))
                        stage(None, (BATCHES - 1, 1))

                    @block.tensor
                    def _(pe):
                        def stage(conv, scan):
                            if conv:
                                j, p = conv
                            if scan:
                                g, r = scan

                            def take_in():
                                for c in range(CC):
                                    wait(pe, in_copied, CC * j + (c == 2))
                                    pe.matmul(bank[c % 2][:], win1[:, c * P:(c + 1) * P], xT_all[:, bass.ds(j * SEQ, SEQ)],
                                              start=True, stop=True).then_inc(in_done, 1)

                            def convolve(o, part):
                                if part == 0:
                                    pe.wait_ge(in_copied, CC * (j + 1))
                                    wait(pe, conv_ready, CC * j + (o == 2))
                                products = [(c, tap) for c in range(CC) for tap in range(TAPS)]
                                n = len(products) // 2
                                for c, tap in products[part * n:(part + 1) * n]:
                                    last = pe.matmul(bank[2 + o % 2][:], wconv[:, c, tap, o * P:(o + 1) * P], padded[:, c, tap:tap + SEQ],
                                                     start=(c, tap) == products[0], stop=(c, tap) == products[-1])
                                if part:
                                    last.then_inc(conv_done, 1)

                            def turn(c):
                                pe.wait_ge(conv_ready, CC * j + c + 1)
                                wait(pe, x_copied, CC * j + c)
                                if scan:
                                    pe.wait_ge(state_ready, (BT - 1) * (g + 1))
                                for k in range(BT):
                                    src = xconv[:, c, k * P:(k + 1) * P] if c < 2 else bcT[p][:, k * P:(k + 1) * P]
                                    last = pe.transpose(bank[4][:, k * P:(k + 1) * P], src, ident)
                                last.then_inc(x_turned, 1)

                            def pairs():
                                pe.wait_ge(conv_ready, CC * (g + 1))
                                wait(pe, weights_ready, BT * g)
                                for c in range(BT):
                                    last = pe.matmul(bank[6][:, c * P:(c + 1) * P], bT[r][:, c * P:(c + 1) * P], cT[r][:, c * P:(c + 1) * P],
                                                     start=True, stop=True)
                                last.then_inc(cb_done, 1)

                            def spread(c):
                                wait(pe, seg_shifted, BT * g + c)
                                for hd in range(MH):
                                    last = pe.matmul(bank[5][:, hd * P:(hd + 1) * P], cs_now[:, c * MH + hd:c * MH + hd + 1].to_broadcast([P, P]), ident,
                                                     start=True, stop=True)
                                last.then_inc(seg_done, 1)

                            def combine(c):
                                wait(pe, y_read, BT * g + c)
                                pe.wait_ge(weights_ready, BT * g + c + 1)
                                for hd in range(MH):
                                    last = pe.matmul(bank[7][:, hd * MP:(hd + 1) * MP], weights[:, hd, :], xs[r][:, c, hd * MP:(hd + 1) * MP],
                                                     start=True, stop=True)
                                if c:
                                    pe.wait_ge(state_ready, (BT - 1) * g + c)
                                    last = pe.matmul(bank[7][:, INNER:2 * INNER], cT[r][:, c * P:(c + 1) * P], carry[:], start=True, stop=True)
                                last.then_inc(y_done, 1)
                                if c < BT - 1:
                                    pe.wait_ge(x_copied, CC * (g + 1))
                                    wait(pe, state_ready, (BT - 1) * g + c)
                                    pe.matmul(bank[4][0:STATE, 0:INNER], bs[r][:, c, :], xdec[:], start=True, stop=True).then_inc(state_done, 1)

                            if conv:
                                take_in()
                            if scan:
                                pe.wait_ge(cs_here, g + 1)
                                pairs()
                                spread(0)
                            for n in range(BT):
                                if conv:
                                    convolve(n // 2, n % 2)
                                if scan:
                                    combine(n)
                                    if n + 1 < BT:
                                        spread(n + 1)
                            if conv:
                                convolve(2, 0)
                                turn(0)
                                turn(1)
                                convolve(2, 1)
                                turn(2)

                        pe.wait_ge(pads, 1)
                        stages(pe, stage)

                    @block.scalar
                    def _(act):
                        def stage(conv, scan):
                            if conv:
                                j, p = conv
                            if scan:
                                g, r = scan

                            def relu_part(o):
                                act.wait_ge(conv_done, CC * j + o + 1)
                                wait(act, conv_ready, CC * j + o)
                                act.activation(relu[:], bank[2 + o % 2][:], ACT.Relu, bias=vec[:, V_CONVB + o:V_CONVB + o + 1]).then_inc(relu_done, 1)

                            if conv:
                                for c in range(CC):
                                    act.wait_ge(in_done, CC * j + c + 1)
                                    wait(act, conv_done, CC * j)
                                    act.activation(padded[:, c, TAPS - 1:], bank[c % 2][:], ACT.Copy).then_inc(in_copied, 1)
                            for n in range(BT):
                                if scan:
                                    act.wait_ge(seg_shifted, BT * g + n + 1)
                                    act.activation(seg[:], seg[:], ACT.Exp).then_inc(seg_exped, 1)
                                if conv and n % 2:
                                    relu_part(n // 2)
                            if conv:
                                relu_part(2)

                        stages(act, stage)

                    @block.vector
                    def _(v):
                        loop = Chain(v, "mamba_scan")
                        per_scan = 3 * (BT - 1)

                        def stage(conv, scan):
                            if conv:
                                j, p = conv
                            if scan:
                                g, r = scan
                                loop.start(per_scan * g)

                            def prelu(o):
                                v.wait_ge(relu_done, CC * j + o + 1)
                                v.tensor_scalar(least[:], bank[2 + o % 2][:], vec[:, V_CONVB + o:V_CONVB + o + 1], 0.0, ALU.add, ALU.min).then_inc(least_done, 1)
                                v.wait_ge(least_done, CC * j + o + 1)
                                if o < 2:
                                    wait(v, x_turned, CC * j)
                                    v.scalar_tensor_tensor(xconv[:, o, :], least[:], vec[:, V_PRELU:V_PRELU + 1], relu[:], ALU.mult, ALU.add) \
                                        .then_inc(conv_ready, 1)
                                else:
                                    if scan:
                                        wait(v, y_done, BT * g)
                                    v.scalar_tensor_tensor(bcT[p][:], least[:], vec[:, V_PRELU:V_PRELU + 1], relu[:], ALU.mult, ALU.add)
                                    v.scalar_tensor_tensor(cT[p][:], least[STATE:], vec[STATE:, V_PRELU:V_PRELU + 1], relu[STATE:], ALU.mult, ALU.add) \
                                        .then_inc(conv_ready, 1)

                            def copy_turned(c):
                                v.wait_ge(x_turned, CC * j + c + 1)
                                if c < 2:
                                    v.tensor_copy(xs[p][:, :, c * P:(c + 1) * P], tiles(bank[4][:])).then_inc(x_copied, 1)
                                else:
                                    v.tensor_copy(bs[p][:], tiles(bank[4][:])[:, :, 0:STATE]).then_inc(x_copied, 1)

                            def heads(ap):
                                return ap.rearrange("p (h d) -> p h d", h=MH)

                            def by_head(tab, c, parts=P):
                                return tab[0:parts, bass.ds((g * BT + c) * MH, MH)].unsqueeze(2).broadcast_to([parts, MH, MP])

                            def decay(c):
                                v.wait_ge(seg_done, BT * g + c + 1)
                                wait(v, weights_ready, BT * g + c)
                                for hd in range(MH):
                                    last = v.scalar_tensor_tensor(seg[:, hd, :], bank[5][:, hd * P:(hd + 1) * P], one(cs, (g * BT + c) * MH + hd),
                                                                  const("causal"), ALU.subtract, ALU.add)
                                last.then_inc(seg_shifted, 1)

                            def weigh(c):
                                wait(v, y_done, BT * g + c)
                                v.wait_ge(x_copied, CC * (g + 1))
                                if c < BT - 1:
                                    wait(v, state_done, (BT - 1) * g + c)
                                    v.tensor_tensor(heads(xdec[:]), heads(xs[r][:, c, :]), by_head(dec, c), ALU.mult)
                                v.wait_ge(seg_exped, BT * g + c + 1)
                                if c == 0:
                                    v.wait_ge(cb_done, g + 1)
                                v.tensor_tensor(weights[:], seg[:], bank[6][:, c * P:(c + 1) * P].unsqueeze(1).broadcast_to([P, MH, P]), ALU.mult) \
                                    .then_inc(weights_ready, 1)

                            def finish(c):
                                tile = g * BT + c
                                v.wait_ge(y_done, BT * g + c + 1)
                                if c:
                                    loop(v.tensor_tensor(heads(ytmp[:]), heads(bank[7][:, INNER:2 * INNER]), by_head(ecs, c), ALU.mult))
                                    v.tensor_tensor(ytmp[:], ytmp[:], bank[7][:, 0:INNER], ALU.add).then_inc(y_read, 1)
                                else:
                                    v.tensor_copy(ytmp[:], bank[7][:, 0:INNER]).then_inc(y_read, 1)
                                v.wait_ge(y_read, BT * g + c + 1)
                                loop(v.tensor_tensor(one(u, tile), one(u, tile), ytmp[:].unsqueeze(1), ALU.mult))
                                v.bn_stats(one(u_stats, tile), one(u, tile)).then_inc(u_measured, 1)
                                if c == BT - 1:
                                    return
                                v.wait_ge(state_done, (BT - 1) * g + c + 1)
                                if c:
                                    loop(v.tensor_tensor(heads(carry_dec[:]), heads(carry[:]), by_head(elast, c, STATE), ALU.mult))
                                    v.tensor_tensor(carry[:], carry_dec[:], bank[4][0:STATE, 0:INNER], ALU.add).then_inc(state_ready, 1)
                                else:
                                    v.tensor_copy(carry[:], bank[4][0:STATE, 0:INNER]).then_inc(state_ready, 1)
                                v.wait_ge(state_ready, (BT - 1) * g + c + 1)

                            if scan:
                                wait(v, seg_done, BT * g)
                                v.tensor_copy(cs_now[:], cs[:, bass.ds(g * BT * MH, BT * MH)]).then_inc(cs_here, 1)
                                decay(0)
                                weigh(0)
                            for n in range(BT):
                                if scan:
                                    finish(n)
                                    if n + 1 < BT:
                                        decay(n + 1)
                                        weigh(n + 1)
                                if conv and n % 2:
                                    prelu(n // 2)
                            if scan:
                                assert loop.n == per_scan
                            if conv:
                                copy_turned(0)
                                copy_turned(1)
                                prelu(2)
                                copy_turned(2)

                        v.memset(padded[:, :, 0:TAPS - 1], 0.0).then_inc(pads, 1)
                        stages(v, stage)

                with ExitStack() as inner_scope, nc.Block() as block:
                    yw = [sb(inner_scope, f"mamba_yw{p}", [P, BT, INNER]) for p in range(2)]
                    yT = [sb(inner_scope, f"mamba_yT{p}", [P, 2, SEQ]) for p in range(2)]

                    @block.tensor
                    def _(pe):
                        @turns(pe, BATCHES // 2)
                        def _(i):
                            for p in range(2):
                                pe.wait_ge(again[p], i + 1)
                                wait(pe, affine[p], i)
                                for c in range(2):
                                    for k in range(BT):
                                        last = pe.transpose(bank[2 * p + c][:, k * P:(k + 1) * P], yw[p][:, k, c * P:(c + 1) * P], ident)
                                last.then_inc(turned[p], 1)
                            for p in range(2):
                                pe.wait_ge(affine[p], i + 1)
                                wait(pe, added[p], i)
                                for k in range(BT):
                                    for c in range(2):
                                        last = pe.matmul(bank[4 + p][:, k * P:(k + 1) * P], yT[p][:, c, k * P:(k + 1) * P], win3[:, c, :],
                                                         start=(c == 0), stop=(c == 1))
                                last.then_inc(projected[p], 1)

                    @block.scalar
                    def _(act):
                        @turns(act, BATCHES // 2)
                        def _(i):
                            for p in range(2):
                                act.wait_ge(turned[p], i + 1)
                                wait(act, projected[p], i)
                                for c in range(2):
                                    last = act.activation(yT[p][:, c, :], bank[2 * p + c][:], ACT.Identity, scale=vec[:, V_MG + c:V_MG + c + 1],
                                                          bias=vec[:, V_MB + c:V_MB + c + 1])
                                last.then_inc(affine[p], 1)

                    @block.vector
                    def _(v):
                        own = Chain(v, "mamba_out")
                        row_norm(v, own, u_stats[:], out_rstd[:], out_shift[:], INNER, inner_scope, "mamba_out")
                        @turns(v, BATCHES // 2)
                        def _(i):
                            for p in range(2):
                                wait(v, turned[p], i)
                                for k in range(BT):
                                    tile = 2 * BT * i + BT * p + k
                                    last = v.tensor_scalar(yw[p][:, k, :], one(u, tile), one(out_rstd, tile), one(out_shift, tile), ALU.mult, ALU.add)
                                last.then_inc(again[p], 1)
                            for p in range(2):
                                v.wait_ge(projected[p], i + 1)
                                part = X[:, bass.ds((2 * i + p) * BT, BT), :]
                                v.tensor_tensor(part, part, tiles(bank[4 + p][:]), ALU.add).then_inc(added[p], 1)
                                v.wait_ge(added[p], i + 1)
                                for k in range(BT):
                                    tile = 2 * BT * i + BT * p + k
                                    v.bn_stats(one(stats, tile), one(X, tile))

        a = (FA, 1, ACT.Gelu, wgA, w1A, w2A, False, False)
        b = (FB, 2, ACT.Silu, wgB, w1B, w2B, True)
        for phase in ("a0", "attention", "a1", "b0", "mamba", "b1"):
            next_phase()
            if phase[0] == "a" and phase != "attention":
                moe(phase, *a)
            elif phase == "attention":
                attention()
            elif phase == "mamba":
                layer0.close()
                mamba()
            else:
                moe(phase, *b, phase == "b1")


def constants():
    k, m = np.arange(P)[:, None], np.arange(P)[None, :]
    e_t = np.arange(E * TILES)
    part = dict(
        ident=k == m, before=k < m, upto=k <= m, ones=k >= 0 * m, same_expert=k % E == m % E,
        last_row=(k == P - 1) & (m >= 0), head_mask=k // HD == m // HD,
        causal=np.where(m >= k, 0.0, NEG),
        prefer=np.broadcast_to(E - e_t // TILES, (P, E * TILES)),
        restart=np.broadcast_to(e_t % TILES != 0, (P, E * TILES)),
        block_row=np.broadcast_to(P * np.arange(MAX_BLOCKS), (P, MAX_BLOCKS)),
    )
    return np.concatenate([part[n].astype(np.float32) for n in PARTS], axis=1)


def layouts(inp):
    g = {k: np.asarray(v) for k, v in inp.items()}
    c = np.ascontiguousarray
    rep = lambda v: np.broadcast_to(v, (P, v.shape[-1]))
    return {
        "x": c(g["L0_attn_x"].reshape(TOKENS, D)),
        "consts": constants(),
        "bits": c(np.broadcast_to(np.array([1 << b for b in range(BITS - 2, -1, -1)] + [0], np.int32), (P, BITS))),
        "vecs": c(np.concatenate([g["L0_attn_bk"][:, None], g["L0_attn_ln_g"][:, None], g["L0_attn_ln_b"][:, None],
                                  g["L1_attn_conv_b"].reshape(CC, P).T, np.broadcast_to(g["L1_attn_prelu_a"], (P, 1)),
                                  g["L1_attn_ln_g"].reshape(2, P).T, g["L1_attn_ln_b"].reshape(2, P).T], axis=1)),
        "rows": c(np.concatenate([rep(g["L0_attn_bq"]), rep(g["L0_attn_bv"]), rep(g["L0_attn_bo"]), rep(g["L1_attn_A_log"])], axis=1)),
        "wqkvo": c(np.stack([g["L0_attn_W" + n].T for n in "qkvo"], axis=1)),
        "a_wg": g["L0_ffn_Wg"],
        "a_w1": c(g["L0_ffn_W1"].transpose(1, 0, 2)),
        "a_w2": c(g["L0_ffn_W2"].reshape(E, FA // P, P, D).transpose(2, 0, 1, 3)),
        "b_wg": c(g["L1_ffn_gate_w"].T),
        "b_w1": c(g["L1_ffn_experts_w1"].transpose(2, 0, 1)),
        "b_w2": c(g["L1_ffn_experts_w2"].transpose(0, 2, 1).reshape(E, FB // P, P, D).transpose(2, 0, 1, 3)),
        "b_sw1": c(g["L1_ffn_shared_w1"].T),
        "b_sw2": c(g["L1_ffn_shared_w2"].T.reshape(FB // P, P, D).transpose(1, 0, 2)),
        "m_in1": c(g["L1_attn_W_in1"][INNER:].T),
        "m_in2": c(g["L1_attn_W_in2"].T),
        "m_in3": c(g["L1_attn_W_in3"].T.reshape(INNER // P, P, D).transpose(1, 0, 2)),
        "m_conv": c(g["L1_attn_conv_w"].transpose(1, 2, 0).reshape(CC, P, TAPS, CH).transpose(1, 0, 2, 3)),
    }


def kernel(**inputs):
    import concourse.bacc as bacc
    from concourse.bass_utils import run_bass_kernel_spmd

    nc = bacc.Bacc("TRN2", target_bir_lowering=False, num_devices=1)
    arrays = layouts(inputs)
    args = {n: nc.dram_tensor(f"in_{n}", a.shape, mybir.dt.from_np(a.dtype), kind="ExternalInput").ap() for n, a in arrays.items()}
    result = nc.dram_tensor("result", (TOKENS, D), F32, kind="ExternalOutput").ap()
    program(nc, **args, out=result)
    r = run_bass_kernel_spmd(nc, [{f"in_{n}": a for n, a in arrays.items()}], core_ids=[0])
    return r.results[0]["result"].reshape(BATCHES, SEQ, D)
```

```python
from contextlib import ExitStack

import numpy as np

import concourse.bass as bass
from concourse import mybir

F32 = mybir.dt.float32
I32 = mybir.dt.int32
ALU = mybir.AluOpType
ACT = mybir.ActivationFunctionType
AX = mybir.AxisListType

P = 128
D = 128
BATCHES, SEQ = 8, 512
TOKENS = BATCHES * SEQ
TILES = TOKENS // P
BT = SEQ // P
E = 8
FA, FB = 256, 512
CAP = TOKENS // E
HEADS = 16
HD = D // HEADS
INNER, STATE, MH = 256, 64, 4
MP = INNER // MH
CH = INNER + 2 * STATE
CC = CH // P
TAPS = 4
EPS = 1e-5
NEG = -3e38
STEPS = 15
UNROLL = 3
DIGITS = 3 * (STEPS + 1)
GROUP = 8
MAX_BLOCKS = 2 * TILES + E
SLOTS = 8
ROW = D + 2

PARTS = dict(ident=P, before=P, upto=P, ones=P, same_expert=P, last_row=P, head_mask=P, causal=P,
             prefer=E * TILES, restart=E * TILES, row_no=MAX_BLOCKS, digits=DIGITS)
AT = {k: sum(list(PARTS.values())[:i]) for i, k in enumerate(PARTS)}
CONST_COLS = sum(PARTS.values())
V_BK, V_LNG, V_LNB, V_CONVB, V_PRELU, V_MG, V_MB, V_END = 0, 1, 2, 3, 6, 7, 9, 11
R_BQ, R_BV, R_BO, R_ALOG, R_END = 0, 128, 256, 384, 388


def wait(eng, semaphore, count):
    if not isinstance(count, int) or count > 0:
        eng.wait_ge(semaphore, count)


def turns(eng, n):
    def run(body):
        body(0)
        if n > 1:
            with eng.Fori(1, n) as i:
                body(i)
    return run


def program(nc, x, consts, ints, vecs, rows, wqkvo, a_wg, a_w1, a_w2, b_wg, b_w1, b_w2, b_sw1, b_sw2,
            m_in1, m_in2, m_in3, m_conv, out):
    ctx = ExitStack()
    with ctx:
        def sb(scope, name, shape, dt=F32):
            return scope.enter_context(nc.sbuf_tensor(name, shape, dt))

        held, signals = [ctx.enter_context(ExitStack())], [[]]

        def sem(name):
            signals[-1].append(held[-1].enter_context(nc.semaphore(name)))
            return signals[-1][-1]

        def next_phase():
            if len(held) > 2:
                held[-2].close()
            held.append(ctx.enter_context(ExitStack()))
            signals.append([])

        def clear_last_phase(sp):
            nums = sorted(h.num for h in signals[-2])
            while len(signals) > 2 and nums:
                n = 1
                while n < len(nums) and nums[n] == nums[0] + n:
                    n += 1
                sp.sem_clear(range(nums[0], nums[0] + n))
                nums = nums[n:]

        def pair(name):
            return [sem(f"{name}{q}") for q in range(2)]

        X = sb(ctx, "X", [P, TILES, D])
        stats = sb(ctx, "stats", [P, TILES, 6])
        rstd = sb(ctx, "rstd", [P, TILES])
        shift = sb(ctx, "shift", [P, TILES])
        table = sb(ctx, "table", [P, CONST_COLS])
        int_table = sb(ctx, "int_table", [P, DIGITS + 2 * TILES], I32)
        vec = sb(ctx, "vec", [P, V_END])
        row = sb(ctx, "row", [P, R_END])
        wgB = sb(ctx, "wgB", [P, E])
        w1B, w2B = sb(ctx, "w1B", [P, E, FB]), sb(ctx, "w2B", [P, E, FB // P, D])
        sw1B, sw2B = sb(ctx, "sw1B", [P, FB]), sb(ctx, "sw2B", [P, FB // P, D])
        win1, win2 = sb(ctx, "win1", [P, CH + MH]), sb(ctx, "win2", [P, INNER])
        win3 = sb(ctx, "win3", [P, INNER // P, D])
        wconv = sb(ctx, "wconv", [P, CC, TAPS, CH])
        layer0 = ctx.enter_context(ExitStack())
        wattn = sb(layer0, "wattn", [P, 4, D])
        wgA = sb(layer0, "wgA", [P, E])
        w1A, w2A = sb(layer0, "w1A", [P, E, FA]), sb(layer0, "w2A", [P, E, FA // P, D])
        bank = [ctx.enter_context(nc.psum_tensor(f"bank{i}", [P, 512], F32)) for i in range(8)]
        sorted_x = nc.dram_tensor("sorted_x", [MAX_BLOCKS * P, ROW], F32, kind="Internal").ap()
        token_y = nc.dram_tensor("token_y", [2 * TOKENS + MAX_BLOCKS * P, D], F32, kind="Internal").ap()

        def const(which):
            return table[:, AT[which]:AT[which] + PARTS[which]]

        ident = const("ident")

        def one(ap, i):
            return ap[:, bass.ds(i, 1)]

        class Chain:

            def __init__(self, eng, name):
                self.eng, self.sem, self.base, self.n = eng, sem(name), 0, 0

            def __call__(self, ins):
                self.n += 1
                ins.then_inc(self.sem, 1)
                self.eng.wait_ge(self.sem, self.base + self.n)

            def start(self, base):
                self.base, self.n = base, 0

        def row_norm(v, own, st, rs, sh, width, scope, name):
            n = rs.shape[1]
            diff, total, var, t = (sb(scope, f"{name}_{k}", [P, n]) for k in ("diff", "total", "var", "newton"))
            seed = sb(scope, f"{name}_seed", [P, n], I32)
            own(v.tensor_tensor(diff[:], st[:, :, 1], st[:, :, 4], ALU.subtract))
            own(v.tensor_tensor(total[:], st[:, :, 1], st[:, :, 4], ALU.add))
            own(v.tensor_tensor(var[:], st[:, :, 2], st[:, :, 5], ALU.add))
            own(v.scalar_tensor_tensor(t[:], diff[:], 0.25, diff[:], ALU.mult, ALU.mult))
            own(v.scalar_tensor_tensor(var[:], var[:], 1.0 / width, t[:], ALU.mult, ALU.add))
            own(v.tensor_scalar(var[:], var[:], EPS, None, ALU.add))
            own(v.tensor_scalar(seed[:], var[:].bitcast(I32), 1, None, ALU.logical_shift_right))
            own(v.tensor_scalar(seed[:], seed[:], -1.0, float(0x5F3759DF), ALU.mult, ALU.add))
            r = seed[:].bitcast(F32)
            for _ in range(3):
                own(v.tensor_tensor(t[:], r, r, ALU.mult))
                own(v.scalar_tensor_tensor(t[:], t[:], -0.5, var[:], ALU.mult, ALU.mult))
                own(v.scalar_tensor_tensor(rs[:], t[:], 1.5, r, ALU.add, ALU.mult))
                r = rs[:]
            own(v.scalar_tensor_tensor(sh[:], total[:], -0.5, rs[:], ALU.mult, ALU.mult))

        def normed(v, dst, tile, src):
            return v.tensor_scalar(dst, src, one(rstd, tile), one(shift, tile), ALU.mult, ALU.add)

        scattered = sem("scattered")
        y_stored = [sem(f"y_stored{k}") for k in range(GROUP)]
        done = dict(scattered=0, y_stored=0)

        x_loaded, zeroed, cleared = sem("x_loaded"), sem("zeroed"), sem("cleared")
        tables_loaded, experts_loaded, others_loaded = sem("tables_loaded"), sem("experts_loaded"), sem("others_loaded")
        tables = ((table, consts), (int_table, ints), (wgA, a_wg))
        experts = ((w1A, a_w1), (w2A, a_w2))
        others = ((vec, vecs), (row, rows), (wattn, wqkvo), (wgB, b_wg), (w1B, b_w1), (w2B, b_w2), (sw1B, b_sw1), (sw2B, b_sw2),
                  (win1, m_in1), (win2, m_in2), (win3, m_in3), (wconv, m_conv))
        zeros = sb(layer0, "zeros", [P, MAX_BLOCKS // 4, ROW])
        with nc.Block(no_gpsimd_drain=True) as block:
            @block.sync
            def _(sp):
                sp.dma_start(X[:], x.rearrange("(t p) d -> p t d", p=P)).then_inc(x_loaded, 16)

            @block.scalar
            def _(act):
                for dst, src in tables:
                    act.dma_start(dst[:], src).then_inc(tables_loaded, 16)
                for dst, src in experts:
                    act.dma_start(dst[:], src).then_inc(experts_loaded, 16)

            @block.gpsimd
            def _(pool):
                nc.gpsimd.memset(zeros[:], 0.0).then_inc(zeroed, 1)
                pool.wait_ge(zeroed, 1)
                for k in range(4):
                    pool.dma_start(sorted_x.rearrange("(k p t) d -> k p t d", k=4, p=P)[k], zeros[:]) \
                        .then_inc(cleared, 16)

            @block.vector
            def _(v):
                v.wait_ge(x_loaded, 16)
                with v.Fori(0, TILES // 4) as i:
                    for k in range(4):
                        v.bn_stats(one(stats, 4 * i + k), one(X, 4 * i + k))

        def load_others(sp):
            for dst, src in others:
                sp.dma_start(dst[:], src).then_inc(others_loaded, 16)

        def moe(name, F, choices, func, wg, w1, w2, shared, final):
            NC = F // P
            NB = choices * TILES + E
            TURNS = NB // GROUP
            HALF_BANK = E * TILES
            first = name == "a0"
            scope = ExitStack()

            def s(n):
                return sem(f"{name}_{n}")

            def s2(n):
                return pair(f"{name}_{n}")

            def t(n, shape, dt=F32):
                return sb(scope, f"{name}_{n}", shape, dt)

            normed_rows, columns, columns_copied, logits_done = s2("normed_rows"), s2("columns"), s2("columns_copied"), s2("logits_done")
            rows_kept, more_rows_kept, all_columns = s2("rows_kept"), s2("more_rows_kept"), s2("all_columns")
            centred, exped, prob_ready, prob_turned = s("centred"), s("exped"), s("prob_ready"), s("prob_turned")
            counted, summed, thr_ready, thr_spread = s("counted"), s("summed"), s("thr_ready"), s("thr_spread")
            ties_ready, ties_summed, picked, picks_summed = s("ties_ready"), s("ties_summed"), s("picked"), s("picks_summed")
            digit = s("digit")
            pos_ready, experts_known = s("pos_ready"), s("experts_known")
            scattered0, stored0 = done["scattered"], done["y_stored"]
            done["scattered"] += 16 * TILES * choices
            done["y_stored"] += 16 * TURNS
            if shared:
                sh_up, sh_act, sh_down, sh_added = s("sh_up"), [s(f"sh_act{c}") for c in range(NC)], s2("sh_down"), s2("sh_added")
            blk_loaded = [s(f"blk_loaded{k}") for k in range(GROUP)]
            turned, xT_copied, up, activated = s2("turned"), s2("xT_copied"), s2("up"), s2("activated")
            tagged, down, y_copied = s2("tagged"), s2("down"), s2("y_copied")
            rows_tagged, used, sent = s("rows_tagged"), s("used"), s("sent")
            result_loaded = [s(f"result_loaded{k}") for k in range(SLOTS)]

            with scope:
                xn = t("xn", [P, TILES, ROW])
                xw = [t(f"xw{q}", [P, BT, D]) for q in range(2)]
                xT = [t(f"xT{q}", [P, SEQ]) for q in range(2)]
                gate = [t(f"gate{k}", [P, TILES]) for k in range(choices)]
                pos = [t(f"pos{k}", [P, TILES], I32) for k in range(choices)]
                block_expert = t("block_expert", [P, NB + GROUP], I32)
                score, work, pick, pick2 = (t(n, [P, E, TILES]) for n in ("score", "work", "pick", "pick2"))
                best, other = t("best", [P, TILES]), t("other", [P, TILES])
                by_tile = t("by_tile", [P, TILES, E])
                prob_rows, hits = t("prob_rows", [P, 2 * P]), t("hits", [P, 3, 2 * P])
                thr, cand, ahead, best_digit = (t(n, [P, w], I32) for n, w in (("thr", 1), ("cand", 3), ("ahead", 3), ("best_digit", 1)))
                count, digit_of, threshold = t("count", [P, 3]), t("digit_of", [P, 3]), t("threshold", [P, 1])
                small = [t(f"small{k}", [P, E]) for k in range(4)]
                small_i = t("small_i", [P, E], I32)
                begun, begun_by, ended_by = t("begun", [P, NB, E]), t("begun_by", [P, NB]), t("ended_by", [P, NB])
                spare = t("spare", [P, NB], I32)
                if shared:
                    xnT = t("xnT", [P, TOKENS])
                    sh = [t(f"sh{q}", [P, NC, SEQ]) for q in range(2)]
                rows_in = [t(f"rows_in{k}", [P, ROW]) for k in range(GROUP)]
                goes_to = [t(f"goes_to{k}", [P, 1], I32) for k in range(GROUP)]
                gate_in = [t(f"gate_in{k}", [P, 1]) for k in range(GROUP)]
                bxT = [t(f"bxT{q}", [P, P]) for q in range(2)]
                bw1 = [t(f"bw1{q}", [P, F]) for q in range(2)]
                hT = [t(f"hT{q}", [P, F]) for q in range(2)]
                y = [t(f"y{k}", [P, D]) for k in range(GROUP)]
                got = [t(f"got{k}", [P, BT, D]) for k in range(SLOTS)]

                def digits(step):
                    return int_table[:, bass.ds(3 * step, 3)]

                def per_token(ap):
                    return ap.unsqueeze(1).broadcast_to([P, E, TILES])

                def per_expert(ap):
                    return ap.unsqueeze(2).broadcast_to([P, E, TILES])

                def over_experts(ap):
                    return ap.rearrange("p e t -> p t e")

                def flat(ap):
                    return ap.rearrange("p e t -> p (e t)")

                def routing(b):
                    return bank[b][:, 0:HALF_BANK].rearrange("p (e t) -> p e t", e=E)

                logits, sum_before, sum_tile, sum_above = routing(2), routing(3), routing(4), routing(5)

                def parity(i, k):
                    return k % 2, GROUP // 2 * i + k // 2

                def after(i, k, by):
                    return (i, k + by) if k + by < GROUP else (i + 1, k + by - GROUP)

                with nc.Block() as block:
                    @block.tensor
                    def _(pe):
                        if first:
                            pe.wait_ge(tables_loaded, 16 * len(tables))
                        @turns(pe, BATCHES // 2)
                        def _(i):
                            for q in range(2):
                                pe.wait_ge(normed_rows[q], i + 1)
                                wait(pe, columns_copied[q], i)
                                for k in range(BT):
                                    last = pe.transpose(bank[q][:, k * P:(k + 1) * P], xw[q][:, k, :], ident)
                                last.then_inc(columns[q], 1)
                            for q in range(2):
                                pe.wait_ge(columns_copied[q], i + 1)
                                for k in range(BT):
                                    last = pe.matmul(logits[:, :, bass.ds(8 * i + BT * q + k, 1)], xT[q][:, k * P:(k + 1) * P],
                                                     wg[:], start=True, stop=True)
                                last.then_inc(logits_done[q], 1)
                        if choices == 1:
                            pe.wait_ge(prob_ready, 1)
                            for half in range(2):
                                last = pe.transpose(bank[0][:, half * P:(half + 1) * P],
                                                    by_tile[:, 16 * half:16 * half + 16, :].rearrange("p t e -> p (t e)"), ident)
                            last.then_inc(prob_turned, 1)
                            with pe.Fori(0, STEPS // UNROLL) as i:
                                for u in range(UNROLL):
                                    pe.wait_ge(counted, UNROLL * i + u + 1)
                                    pe.matmul(bank[1][:, 0:3], const("same_expert"), count[:], start=True, stop=True).then_inc(summed, 1)
                            pe.wait_ge(thr_ready, 1)
                            pe.matmul(bank[1][:, 0:E], threshold[:].to_broadcast([P, P]), ident[:, 0:E], start=True, stop=True) \
                                .then_inc(thr_spread, 1)
                            pe.wait_ge(ties_ready, 2)
                            pe.matmul(flat(sum_before), const("before"), flat(pick[:]), start=True, stop=True)
                            pe.matmul(flat(sum_tile), const("ones"), flat(pick[:]), start=True, stop=True)
                            pe.matmul(flat(sum_above), const("ones"), flat(work[:]), start=True, stop=True).then_inc(ties_summed, 1)
                        pe.wait_ge(picked, 1)
                        pe.matmul(flat(sum_before), const("before"), flat(work[:]), start=True, stop=True)
                        pe.matmul(flat(sum_tile), const("ones"), flat(work[:]), start=True, stop=True).then_inc(picks_summed, 1)

                        if shared:
                            pe.wait_ge(pos_ready, choices)
                            for q in range(2):
                                pe.wait_ge(all_columns[q], BATCHES // 2)
                            @turns(pe, BATCHES // 2)
                            def _(i):
                                for q in range(2):
                                    for c in range(NC):
                                        wait(pe, sh_act[c], 2 * i + q)
                                        pe.matmul(bank[c][:], sw1B[:, c * P:(c + 1) * P], xnT[:, bass.ds((2 * i + q) * SEQ, SEQ)],
                                                  start=True, stop=True).then_inc(sh_up, 1)
                                for q in range(2):
                                    pe.wait_ge(sh_act[NC - 1], 2 * i + q + 1)
                                    wait(pe, sh_added[q], i)
                                    for k in range(BT):
                                        for c in range(NC):
                                            last = pe.matmul(bank[6 + q][:, k * P:(k + 1) * P], sh[q][:, c, k * P:(k + 1) * P],
                                                             sw2B[:, c, :], start=(c == 0), stop=(c == NC - 1))
                                    last.then_inc(sh_down[q], 1)
                            for q in range(2):
                                pe.wait_ge(sh_added[q], BATCHES // 2)

                        def turn_rows(i, k):
                            q, n = parity(i, k)
                            pe.wait_ge(blk_loaded[k], 16 * (i + 1))
                            wait(pe, xT_copied[q], n)
                            pe.transpose(bank[q][:, 0:P], rows_in[k][:, 0:D], ident).then_inc(turned[q], 1)

                        def go_up(i, k):
                            q, n = parity(i, k)
                            pe.wait_ge(xT_copied[q], n + 1)
                            wait(pe, activated[q], n)
                            for c in range(NC):
                                last = pe.matmul(bank[2 + q][:, c * P:(c + 1) * P], bw1[q][:, c * P:(c + 1) * P], bxT[q][:],
                                                 start=True, stop=True)
                            last.then_inc(up[q], 1)

                        def come_down(i, k, e):
                            q, n = parity(i, k)
                            pe.wait_ge(activated[q], n + 1)
                            wait(pe, y_copied[q], n)
                            for c in range(NC):
                                last = pe.matmul(bank[6 + q][:, 0:D], hT[q][:, c * P:(c + 1) * P], w2[:, bass.ds(e, 1), c, :],
                                                 start=(c == 0), stop=(c == NC - 1))
                            last.then_inc(down[q], 1)

                        regs = [pe.alloc_register(f"{name}_expert{k}") for k in range(GROUP)]

                        def turn(i, last_turn):
                            pe.reg_load(regs, block_expert[0:1, bass.ds(GROUP * i, GROUP)])
                            for k in range(GROUP):
                                if not (last_turn and k + 1 >= GROUP):
                                    go_up(*after(i, k, 1))
                                if not (last_turn and k + 2 >= GROUP):
                                    turn_rows(*after(i, k, 2))
                                come_down(i, k, pe.snap(regs[k], min_val=0, max_val=E - 1))

                        if first:
                            pe.wait_ge(experts_loaded, 16 * len(experts))
                        pe.wait_ge(experts_known, 1)
                        turn_rows(0, 0)
                        turn_rows(0, 1)
                        go_up(0, 0)

                        @turns(pe, TURNS - 1)
                        def _(i):
                            turn(i, False)
                        turn(TURNS - 1, True)

                    @block.scalar
                    def _(act):
                        @turns(act, BATCHES // 2)
                        def _(i):
                            for q in range(2):
                                act.wait_ge(columns[q], i + 1)
                                wait(act, logits_done[q], i)
                                if shared:
                                    wait(act, all_columns[q], i)
                                act.activation(xT[q][:], bank[q][:], ACT.Copy).then_inc(columns_copied[q], 1)
                                act.activation(xn[:, bass.ds((2 * i + q) * BT + BT // 2, BT // 2), 0:D], xw[q][:, BT // 2:BT, :], ACT.Copy) \
                                    .then_inc(more_rows_kept[q], 1)
                        act.wait_ge(centred, 1)
                        e = flat(work[:]) if choices == 1 else other[:]
                        act.activation(e, e, ACT.Exp).then_inc(exped, 1)
                        if shared:
                            @turns(act, BATCHES // 2)
                            def _(i):
                                for q in range(2):
                                    wait(act, sh_down[q], i)
                                    for c in range(NC):
                                        act.wait_ge(sh_up, 2 * NC * i + NC * q + c + 1)
                                        act.activation(sh[q][:, c, :], bank[c][:], func).then_inc(sh_act[c], 1)

                        def activate(i, k):
                            q, n = parity(i, k)
                            act.wait_ge(up[q], n + 1)
                            wait(act, down[q], n)
                            act.activation(hT[q][:], bank[2 + q][:, 0:F], func).then_inc(activated[q], 1)

                        def copy_y(i, k):
                            q, n = parity(i, k)
                            act.wait_ge(down[q], n + 1)
                            act.wait_ge(tagged[q], n + 1)
                            act.activation(y[k][:], bank[6 + q][:, 0:D], ACT.Copy, scale=gate_in[k][:]).then_inc(y_copied[q], 1)

                        def turn(i, last_turn):
                            for k in range(GROUP):
                                if not (last_turn and k + 1 >= GROUP):
                                    activate(*after(i, k, 1))
                                copy_y(i, k)

                        activate(0, 0)
                        @turns(act, TURNS - 1)
                        def _(i):
                            turn(i, False)
                        turn(TURNS - 1, True)

                    @block.vector
                    def _(v):
                        own = Chain(v, f"{name}_route")
                        row_norm(v, own, stats[:], rstd[:], shift[:], D, scope, name)
                        @turns(v, BATCHES // 2)
                        def _(i):
                            for q in range(2):
                                wait(v, columns[q], i)
                                wait(v, rows_kept[q], i)
                                wait(v, more_rows_kept[q], i)
                                for k in range(BT):
                                    tile = 8 * i + BT * q + k
                                    last = normed(v, xw[q][:, k, :], tile, one(X, tile))
                                last.then_inc(normed_rows[q], 1)
                            if shared:
                                for q in range(2):
                                    v.wait_ge(columns_copied[q], i + 1)
                                    v.tensor_copy(xnT[:, bass.ds((2 * i + q) * SEQ, SEQ)], xT[q][:]).then_inc(all_columns[q], 1)
                        for q in range(2):
                            v.wait_ge(logits_done[q], BATCHES // 2)
                        if first:
                            v.wait_ge(tables_loaded, 16 * len(tables))
                            v.wait_ge(experts_loaded, 16 * len(experts))
                        prefer = const("prefer").rearrange("p (e t) -> p e t", e=E)

                        def first_of_best(dst, value, top):
                            own(v.tensor_tensor(dst, value, per_token(top), ALU.is_equal))
                            own(v.tensor_tensor(dst, dst, prefer, ALU.mult))
                            own(v.tensor_reduce(other[:], over_experts(dst), AX.X, ALU.max))
                            own(v.tensor_tensor(dst, dst, per_token(other[:]), ALU.is_equal))

                        if choices == 1:
                            own(v.tensor_reduce(best[:], over_experts(logits), AX.X, ALU.max))
                            v.tensor_tensor(work[:], logits, per_token(best[:]), ALU.subtract).then_inc(centred, 1)
                            v.wait_ge(exped, 1)
                            own(v.tensor_reduce(best[:], over_experts(work[:]), AX.X, ALU.add))
                            own(v.reciprocal(best[:], best[:]))
                            own(v.tensor_tensor(score[:], work[:], per_token(best[:]), ALU.mult))
                            own(v.memset(thr[:], 0))
                            own(v.tensor_copy(cand[:], digits(0)))
                            v.tensor_copy(by_tile[:], over_experts(score[:])).then_inc(prob_ready, 1)
                            v.wait_ge(prob_turned, 1)
                            own(v.tensor_copy(prob_rows[:], bank[0][:, 0:2 * P]))
                            with v.Fori(0, STEPS // UNROLL) as i:
                                for u in range(UNROLL):
                                    step = UNROLL * i + u
                                    for c in range(3):
                                        last = v.tensor_scalar(hits[:, c, :], prob_rows[:], cand[:, c:c + 1].bitcast(F32), None, ALU.is_ge, ALU.add,
                                                               accum_out=count[:, c:c + 1])
                                    last.then_inc(counted, 1)
                                    v.tensor_tensor(ahead[:], thr[:].to_broadcast([P, 3]), digits(step + 1), ALU.bitwise_or).then_inc(digit, 1)
                                    v.wait_ge(summed, step + 1)
                                    v.scalar_tensor_tensor(digit_of[:], bank[1][:, 0:3], float(CAP), const("digits")[:, bass.ds(3 * step, 3)],
                                                           ALU.is_ge, ALU.mult).then_inc(digit, 1)
                                    v.wait_ge(digit, 5 * step + 2)
                                    v.tensor_reduce(best_digit[:], digit_of[:], AX.X, ALU.max).then_inc(digit, 1)
                                    v.wait_ge(digit, 5 * step + 3)
                                    v.tensor_tensor(cand[:], ahead[:], best_digit[:].to_broadcast([P, 3]), ALU.bitwise_or).then_inc(digit, 1)
                                    v.tensor_tensor(thr[:], thr[:], best_digit[:], ALU.bitwise_or).then_inc(digit, 1)
                                    v.wait_ge(digit, 5 * step + 5)
                            v.tensor_copy(threshold[:], thr[:].bitcast(F32)).then_inc(thr_ready, 1)
                            v.wait_ge(thr_spread, 1)
                            own(v.tensor_copy(small[0][:], bank[1][:, 0:E]))
                            v.tensor_tensor(work[:], score[:], per_expert(small[0][:]), ALU.is_gt).then_inc(ties_ready, 1)
                            v.tensor_tensor(pick[:], score[:], per_expert(small[0][:]), ALU.is_equal).then_inc(ties_ready, 1)
                            v.wait_ge(ties_summed, 1)
                            own(v.tensor_reduce(small[1][:], sum_above, AX.X, ALU.add))
                            own(v.tensor_scalar(small[1][:], small[1][:], -1.0, float(CAP), ALU.mult, ALU.add))
                            own(v.tensor_tensor_scan(flat(pick2[:]), const("restart"), flat(sum_tile), 0.0, ALU.mult, ALU.add))
                            own(v.tensor_tensor(pick2[:], pick2[:], sum_tile, ALU.subtract))
                            own(v.tensor_tensor(pick2[:], pick2[:], sum_before, ALU.add))
                            own(v.tensor_tensor(pick2[:], pick2[:], per_expert(small[1][:]), ALU.is_lt))
                            own(v.tensor_tensor(pick2[:], pick2[:], pick[:], ALU.mult))
                            own(v.tensor_tensor(pick2[:], pick2[:], work[:], ALU.add))
                            own(v.tensor_reduce(best[:], over_experts(pick2[:]), AX.X, ALU.max))
                            own(v.tensor_scalar(best[:], best[:], -1.0, 1.0, ALU.mult, ALU.add))
                            own(v.tensor_tensor(pick2[:], pick2[:], per_token(best[:]), ALU.max))
                            own(v.tensor_tensor(score[:], score[:], pick2[:], ALU.mult))
                            own(v.tensor_scalar(pick2[:], pick2[:], -1.0, None, ALU.add))
                            own(v.tensor_tensor(score[:], score[:], pick2[:], ALU.add))
                            own(v.tensor_reduce(gate[0][:], over_experts(score[:]), AX.X, ALU.max))
                            first_of_best(work[:], score[:], gate[0][:])
                            v.tensor_scalar(gate[0][:], gate[0][:], 0.5, None, ALU.mult).then_inc(picked, 1)
                            chosen = [work]
                        else:
                            own(v.tensor_copy(score[:], logits))
                            own(v.tensor_reduce(best[:], over_experts(score[:]), AX.X, ALU.max))
                            first_of_best(pick[:], score[:], best[:])
                            own(v.tensor_scalar(work[:], pick[:], -1.0, 1.0, ALU.mult, ALU.add))
                            own(v.tensor_tensor(score[:], score[:], work[:], ALU.mult))
                            own(v.scalar_tensor_tensor(flat(score[:]), flat(pick[:]), NEG, flat(score[:]), ALU.mult, ALU.add))
                            own(v.tensor_reduce(gate[1][:], over_experts(score[:]), AX.X, ALU.max))
                            first_of_best(pick2[:], score[:], gate[1][:])
                            v.tensor_tensor(work[:], pick[:], pick2[:], ALU.add).then_inc(picked, 1)
                            v.tensor_tensor(other[:], gate[1][:], best[:], ALU.subtract).then_inc(centred, 1)
                            v.wait_ge(exped, 1)
                            own(v.tensor_scalar(best[:], other[:], 1.0, None, ALU.add))
                            own(v.reciprocal(best[:], best[:]))
                            own(v.tensor_scalar(gate[0][:], best[:], 0.5, None, ALU.mult))
                            own(v.tensor_tensor(gate[1][:], gate[0][:], other[:], ALU.mult))
                            chosen = [pick, pick2]
                        v.wait_ge(picks_summed, 1)
                        own(v.tensor_tensor_scan(flat(score[:]), const("ones")[:, 0:1].to_broadcast([P, E * TILES]),
                                                 flat(sum_tile), 0.0, ALU.mult, ALU.add))
                        own(v.tensor_tensor(score[:], score[:], sum_tile, ALU.subtract))
                        own(v.tensor_reduce(small[0][:], sum_tile, AX.X, ALU.add))
                        own(v.tensor_scalar(small_i[:], small[0][:], float(P - 1), None, ALU.add))
                        log_p = P.bit_length() - 1
                        own(v.tensor_scalar(small_i[:], small_i[:], log_p, log_p, ALU.logical_shift_right, ALU.logical_shift_left))
                        own(v.tensor_copy(small[1][:], small_i[:]))
                        own(v.tensor_tensor_scan(small[2][:], const("ones")[:, 0:E], small[1][:], 0.0, ALU.mult, ALU.add))
                        own(v.tensor_tensor(small[2][:], small[2][:], small[1][:], ALU.subtract))
                        own(v.tensor_tensor(small[3][:], small[2][:], score[:, :, 0], ALU.subtract))
                        own(v.tensor_tensor(score[:], score[:], sum_before, ALU.add))
                        own(v.tensor_tensor(score[:], score[:], per_expert(small[3][:]), ALU.add))
                        for k, c in enumerate(chosen):
                            own(v.tensor_tensor(c[:], c[:], score[:], ALU.mult))
                            own(v.tensor_reduce(best[:], over_experts(c[:]), AX.X, ALU.add))
                            v.tensor_copy(pos[k][:], best[:]).then_inc(pos_ready, 1)
                            v.wait_ge(pos_ready, k + 1)
                        by_block = [P, NB, E]
                        row_no = const("row_no")[:, 0:NB]
                        own(v.tensor_tensor(begun[:], row_no.unsqueeze(2).broadcast_to(by_block),
                                            small[2][:].unsqueeze(1).broadcast_to(by_block), ALU.is_ge))
                        own(v.tensor_reduce(begun_by[:], begun[:], AX.X, ALU.add))
                        own(v.memset(block_expert[:], 0))
                        own(v.tensor_scalar(block_expert[:, 0:NB], begun_by[:], -1.0, None, ALU.add))
                        own(v.tensor_tensor(small[2][:], small[2][:], small[0][:], ALU.add))
                        own(v.tensor_tensor(begun[:], row_no.unsqueeze(2).broadcast_to(by_block),
                                            small[2][:].unsqueeze(1).broadcast_to(by_block), ALU.is_ge))
                        own(v.tensor_reduce(ended_by[:], begun[:], AX.X, ALU.add))
                        own(v.tensor_tensor(ended_by[:], ended_by[:], begun_by[:], ALU.subtract))
                        own(v.tensor_scalar(begun_by[:], row_no, float(choices * TOKENS), None, ALU.add))
                        v.scalar_tensor_tensor(spare[:], ended_by[:], 1.0, begun_by[:], ALU.add, ALU.mult).then_inc(experts_known, 1)

                        if shared:
                            @turns(v, BATCHES // 2)
                            def _(i):
                                for q in range(2):
                                    v.wait_ge(sh_down[q], i + 1)
                                    part = X[:, bass.ds((2 * i + q) * BT, BT), :].rearrange("p t d -> p (t d)")
                                    v.scalar_tensor_tensor(part, bank[6 + q][:], 0.5, part, ALU.mult, ALU.add).then_inc(sh_added[q], 1)

                        def copy_columns(i, k, e):
                            q, n = parity(i, k)
                            wait(v, up[q], n)
                            v.tensor_copy(bw1[q][:].unsqueeze(1), w1[:, bass.ds(e, 1), :])
                            v.wait_ge(turned[q], n + 1)
                            v.tensor_copy(bxT[q][:], bank[q][:, 0:P]).then_inc(xT_copied[q], 1)
                            wait(v, y_stored[k], 16 * i + stored0)
                            v.tensor_tensor(goes_to[k][:], rows_in[k][:, D:D + 1].bitcast(I32), one(spare, GROUP * i + k), ALU.max)
                            v.tensor_copy(gate_in[k][:], rows_in[k][:, D + 1:D + 2]).then_inc(tagged[q], 1)

                        regs = [v.alloc_register(f"{name}_expert{k}") for k in range(GROUP)]

                        def turn(i, last_turn):
                            v.reg_load(regs, block_expert[0:1, bass.ds(GROUP * i + 2, GROUP)])
                            for k in range(GROUP):
                                if not (last_turn and k + 2 >= GROUP):
                                    copy_columns(*after(i, k, 2), v.snap(regs[k], min_val=0, max_val=E - 1))

                        v.wait_ge(experts_known, 1)
                        v.reg_load(regs[0:2], block_expert[0:1, 0:2])
                        for k in range(2):
                            copy_columns(0, k, v.snap(regs[k], min_val=0, max_val=E - 1))

                        @turns(v, TURNS - 1)
                        def _(i):
                            turn(i, False)
                        turn(TURNS - 1, True)

                        if shared:
                            for q in range(2):
                                v.wait_ge(sh_added[q], BATCHES // 2)

                        @turns(v, choices * BATCHES // SLOTS)
                        def _(i):
                            for k in range(SLOTS):
                                b = (SLOTS // choices) * i + k // choices
                                part = X[:, bass.ds(BT * b, BT), :]
                                v.wait_ge(result_loaded[k], 16 * (i + 1))
                                v.tensor_tensor(part, part, got[k][:], ALU.add).then_inc(used, 1)
                                v.wait_ge(used, SLOTS * i + k + 1)
                                for n in range(BT):
                                    if k % choices == choices - 1 and not final:
                                        v.bn_stats(one(stats, BT * b + n), one(X, BT * b + n))

                    @block.sync
                    def _(sp):
                        clear_last_phase(sp)
                        if first:
                            load_others(sp)
                        sp.wait_ge(scattered, 16 * TILES * choices + scattered0)
                        @turns(sp, TURNS)
                        def _(i):
                            for k in range(GROUP):
                                q, n = parity(i, k)
                                wait(sp, tagged[q], n + 1 - GROUP // 2)
                                sp.dma_start(rows_in[k][:], sorted_x[bass.ds((GROUP * i + k) * P, P), :]).then_inc(blk_loaded[k], 16)
                        for k in range(GROUP):
                            sp.wait_ge(y_stored[k], 16 * TURNS + stored0)
                        if first:
                            sp.wait_ge(others_loaded, 16 * len(others))

                        def send(b):
                            sp.dma_start(out[bass.ds(SEQ * b, SEQ), :].rearrange("(t p) d -> p t d", p=P),
                                         X[:, bass.ds(BT * b, BT), :]).then_inc(sent, 16)

                        for n in range(choices * BATCHES):
                            if n >= SLOTS:
                                sp.wait_ge(used, n - SLOTS + 1)
                            b, c = n // choices, n % choices
                            sp.dma_start(got[n % SLOTS][:], token_y[c * TOKENS + b * SEQ:c * TOKENS + (b + 1) * SEQ, :]
                                         .rearrange("(t p) d -> p t d", p=P)).then_inc(result_loaded[n % SLOTS], 16)
                        if final:
                            @turns(sp, BATCHES)
                            def _(b):
                                sp.wait_ge(used, choices * (b + 1))
                                send(b)
                            sp.wait_ge(sent, 16 * BATCHES)

                    @block.gpsimd
                    def _(pool):
                        @turns(pool, BATCHES // 2)
                        def _(i):
                            for q in range(2):
                                pool.wait_ge(normed_rows[q], i + 1)
                                pool.tensor_copy(xn[:, bass.ds((2 * i + q) * BT, BT // 2), 0:D], xw[q][:, 0:BT // 2, :]).then_inc(rows_kept[q], 1)
                        for q in range(2):
                            pool.wait_ge(rows_kept[q], BATCHES // 2)
                            pool.wait_ge(more_rows_kept[q], BATCHES // 2)
                        if first:
                            pool.wait_ge(tables_loaded, 16 * len(tables))
                            pool.wait_ge(cleared, 16 * 4)
                        for k in range(choices):
                            pool.wait_ge(pos_ready, k + 1)
                            if k > 0:
                                pool.wait_ge(scattered, 16 * TILES * k + scattered0)
                            ids = int_table[:, DIGITS + k * TILES:DIGITS + (k + 1) * TILES]
                            pool.tensor_copy(xn[:, :, D].bitcast(I32), ids).then_inc(rows_tagged, 1)
                            pool.tensor_copy(xn[:, :, D + 1], gate[k][:]).then_inc(rows_tagged, 1)
                            pool.wait_ge(rows_tagged, 2 * (k + 1))
                            for tile in range(TILES):
                                pool.indirect_dma_start(sorted_x, bass.IndirectOffsetOnAxis(ap=pos[k][:, tile:tile + 1], axis=0),
                                                        xn[:, tile, :], None).then_inc(scattered, 16)

                        for i in range(TURNS):
                            for k in range(GROUP):
                                q, n = parity(i, k)
                                pool.wait_ge(y_copied[q], n + 1)
                                pool.indirect_dma_start(token_y, bass.IndirectOffsetOnAxis(ap=goes_to[k][:], axis=0), y[k][:], None) \
                                    .then_inc(y_stored[k], 16)

        def attention():
            scope = ExitStack()

            def s2(n):
                return pair(f"attn_{n}")

            def t(n, shape, dt=F32):
                return sb(scope, f"attn_{n}", shape, dt)

            normed_rows, columns, columns_copied = s2("normed_rows"), s2("columns"), s2("columns_copied")
            k_done, q_done, v_done, k_max, k_exped = s2("k_done"), s2("q_done"), s2("v_done"), s2("k_max"), s2("k_exped")
            q_centred, q_exped, q_ready, v_ready = s2("q_centred"), s2("q_exped"), s2("q_ready"), s2("v_ready")
            k_turned, k_copied, state_done, state_ready = s2("k_turned"), s2("k_copied"), s2("state_done"), s2("state_ready")
            q_turned, q_copied, mixed, kept = s2("q_turned"), s2("q_copied"), s2("mixed"), s2("kept")
            again, turned, affine, projected, added = s2("again"), s2("turned"), s2("affine"), s2("projected"), s2("added")
            measured, summed_rows = sem("attn_measured"), sem("attn_summed_rows")

            with scope:
                mix = t("mix", [P, TILES, D])
                mix_stats = t("mix_stats", [P, TILES, 6])
                mix_rstd, mix_shift = t("mix_rstd", [P, TILES]), t("mix_shift", [P, TILES])
                xw, xT = [t(f"xw{p}", [P, BT, D]) for p in range(2)], [t(f"xT{p}", [P, SEQ]) for p in range(2)]
                kx, kxT = [t(f"kx{p}", [P, SEQ]) for p in range(2)], [t(f"kxT{p}", [P, SEQ]) for p in range(2)]
                qx, qxT = [t(f"qx{p}", [P, BT, D]) for p in range(2)], [t(f"qxT{p}", [P, SEQ]) for p in range(2)]
                vx = [t(f"vx{p}", [P, BT, D]) for p in range(2)]
                state = [t(f"state{p}", [P, D]) for p in range(2)]
                kmax, kbias, ksum, krec = ([t(f"{n}{p}", [P, 1]) for p in range(2)] for n in ("kmax", "kbias", "ksum", "krec"))
                head = t("head", [P, BT * HEADS])
                sumrow = t("sumrow", [P, BT, D])
                bk = vec[:, V_BK:V_BK + 1]

                def along(which):
                    return row[:, which:which + D].unsqueeze(1).broadcast_to([P, BT, D])

                def tiles(ap):
                    return ap.rearrange("p (t d) -> p t d", t=BT)

                def heads(ap):
                    return ap.rearrange("p t (h d) -> p (t h) d", d=HD)

                def by_head(ap):
                    return ap.unsqueeze(2).broadcast_to([P, BT * HEADS, HD])

                wq, wk, wv, wo = (wattn[:, n, :] for n in range(4))

                with nc.Block() as block:
                    @block.sync
                    def _(sp):
                        clear_last_phase(sp)

                    @block.tensor
                    def _(pe):
                        def project(i, p):
                            pe.wait_ge(normed_rows[p], i + 1)
                            wait(pe, columns_copied[1 - p], i + p)
                            for k in range(BT):
                                last = pe.transpose(bank[0][:, k * P:(k + 1) * P], xw[p][:, k, :], ident)
                            last.then_inc(columns[p], 1)
                            pe.wait_ge(columns_copied[p], i + 1)
                            wait(pe, k_exped[1 - p], i + p)
                            pe.matmul(bank[1][:], wk, xT[p][:], start=True, stop=True).then_inc(k_done[p], 1)
                            wait(pe, q_centred[1 - p], i + p)
                            for k in range(BT):
                                last = pe.matmul(bank[2][:, k * P:(k + 1) * P], xT[p][:, k * P:(k + 1) * P], wq, start=True, stop=True)
                            last.then_inc(q_done[p], 1)
                            wait(pe, v_ready[1 - p], i + p)
                            for k in range(BT):
                                last = pe.matmul(bank[3][:, k * P:(k + 1) * P], xT[p][:, k * P:(k + 1) * P], wv, start=True, stop=True)
                            last.then_inc(v_done[p], 1)

                        def attend(i, p):
                            pe.wait_ge(k_exped[p], i + 1)
                            wait(pe, k_copied[1 - p], i + p)
                            for k in range(BT):
                                last = pe.transpose(bank[4][:, k * P:(k + 1) * P], kx[p][:, k * P:(k + 1) * P], ident)
                            last.then_inc(k_turned[p], 1)
                            pe.wait_ge(q_ready[p], i + 1)
                            wait(pe, q_copied[1 - p], i + p)
                            for k in range(BT):
                                last = pe.transpose(bank[6][:, k * P:(k + 1) * P], qx[p][:, k, :], ident)
                            last.then_inc(q_turned[p], 1)
                            pe.wait_ge(k_copied[p], i + 1)
                            pe.wait_ge(v_ready[p], i + 1)
                            wait(pe, state_ready[1 - p], i + p)
                            for k in range(BT):
                                last = pe.matmul(bank[5][:, 0:D], kxT[p][:, k * P:(k + 1) * P], vx[p][:, k, :],
                                                 start=(k == 0), stop=(k == BT - 1))
                            last.then_inc(state_done[p], 1)
                            pe.wait_ge(state_ready[p], i + 1)
                            pe.wait_ge(q_copied[p], i + 1)
                            wait(pe, kept[1 - p], i + p)
                            for k in range(BT):
                                last = pe.matmul(bank[7][:, k * P:(k + 1) * P], qxT[p][:, k * P:(k + 1) * P], state[p][:], start=True, stop=True)
                            last.then_inc(mixed[p], 1)

                        @turns(pe, BATCHES // 2)
                        def _(i):
                            for p in range(2):
                                project(i, p)
                            for p in range(2):
                                attend(i, p)
                        for p in range(2):
                            pe.wait_ge(kept[p], BATCHES // 2)
                        @turns(pe, BATCHES // 2)
                        def _(i):
                            for p in range(2):
                                pe.wait_ge(again[p], i + 1)
                                wait(pe, affine[p], i)
                                for k in range(BT):
                                    last = pe.transpose(bank[p][:, k * P:(k + 1) * P], xw[p][:, k, :], ident)
                                last.then_inc(turned[p], 1)
                            for p in range(2):
                                pe.wait_ge(affine[p], i + 1)
                                wait(pe, added[p], i)
                                for k in range(BT):
                                    last = pe.matmul(bank[2 + p][:, k * P:(k + 1) * P], xT[p][:, k * P:(k + 1) * P], wo, start=True, stop=True)
                                last.then_inc(projected[p], 1)

                    @block.scalar
                    def _(act):
                        def project(i, p):
                            act.wait_ge(columns[p], i + 1)
                            wait(act, v_done[p], i)
                            act.activation(xT[p][:], bank[0][:], ACT.Copy).then_inc(columns_copied[p], 1)
                            act.wait_ge(k_max[p], i + 1)
                            wait(act, k_turned[p], i)
                            act.activation(kx[p][:], bank[1][:], ACT.Exp, bias=kbias[p][:], accum_out=ksum[p][:]).then_inc(k_exped[p], 1)
                            act.wait_ge(q_centred[p], i + 1)
                            act.activation(qx[p][:], qx[p][:], ACT.Exp).then_inc(q_exped[p], 1)

                        def attend(i, p):
                            act.wait_ge(k_turned[p], i + 1)
                            wait(act, state_done[p], i)
                            act.activation(kxT[p][:], bank[4][:], ACT.Copy).then_inc(k_copied[p], 1)
                            act.wait_ge(q_turned[p], i + 1)
                            wait(act, mixed[p], i)
                            act.activation(qxT[p][:], bank[6][:], ACT.Copy).then_inc(q_copied[p], 1)

                        @turns(act, BATCHES // 2)
                        def _(i):
                            for p in range(2):
                                project(i, p)
                            for p in range(2):
                                attend(i, p)
                        @turns(act, BATCHES // 2)
                        def _(i):
                            for p in range(2):
                                act.wait_ge(turned[p], i + 1)
                                wait(act, projected[p], i)
                                act.activation(xT[p][:], bank[p][:], ACT.Identity, scale=vec[:, V_LNG:V_LNG + 1],
                                               bias=vec[:, V_LNB:V_LNB + 1]).then_inc(affine[p], 1)

                    @block.vector
                    def _(v):
                        own = Chain(v, "attn_own")
                        row_norm(v, own, stats[:], rstd[:], shift[:], D, scope, "attn_in")
                        loop = Chain(v, "attn_loop")
                        per_seq = 7

                        def project(i, p):
                            loop.start(per_seq * (2 * i + p))
                            wait(v, columns[p], i)
                            for k in range(BT):
                                tile = 2 * BT * i + BT * p + k
                                last = normed(v, xw[p][:, k, :], tile, one(X, tile))
                            last.then_inc(normed_rows[p], 1)
                            v.wait_ge(k_done[p], i + 1)
                            loop(v.tensor_reduce(kmax[p][:], bank[1][:], AX.X, ALU.max))
                            loop(v.tensor_scalar(kbias[p][:], kmax[p][:], bk, -1.0, ALU.add, ALU.mult))
                            v.tensor_tensor(kbias[p][:], kbias[p][:], bk, ALU.add).then_inc(k_max[p], 1)
                            v.wait_ge(q_done[p], i + 1)
                            wait(v, q_turned[p], i)
                            loop(v.tensor_tensor(qx[p][:], tiles(bank[2][:]), along(R_BQ), ALU.add))
                            loop(v.tensor_reduce(head[:], heads(qx[p][:]), AX.X, ALU.max))
                            v.tensor_tensor(heads(qx[p][:]), heads(qx[p][:]), by_head(head[:]), ALU.subtract).then_inc(q_centred[p], 1)
                            v.wait_ge(v_done[p], i + 1)
                            wait(v, state_done[p], i)
                            v.tensor_tensor(vx[p][:], tiles(bank[3][:]), along(R_BV), ALU.add).then_inc(v_ready[p], 1)
                            v.wait_ge(q_exped[p], i + 1)
                            loop(v.tensor_reduce(head[:], heads(qx[p][:]), AX.X, ALU.add))
                            loop(v.reciprocal(head[:], head[:]))
                            v.tensor_tensor(heads(qx[p][:]), heads(qx[p][:]), by_head(head[:]), ALU.mult).then_inc(q_ready[p], 1)
                            v.wait_ge(k_exped[p], i + 1)
                            loop(v.reciprocal(krec[p][:], ksum[p][:]))
                            assert loop.n == per_seq

                        def attend(i, p):
                            v.wait_ge(state_done[p], i + 1)
                            wait(v, mixed[p], i)
                            v.scalar_tensor_tensor(state[p][:], bank[5][:, 0:D], krec[p][:], const("head_mask"), ALU.mult, ALU.mult) \
                                .then_inc(state_ready[p], 1)
                            v.wait_ge(mixed[p], i + 1)
                            part = mix[:, bass.ds((2 * i + p) * BT, BT), :]
                            v.tensor_copy(part, tiles(bank[7][:])).then_inc(kept[p], 1)
                            v.wait_ge(kept[p], i + 1)
                            for k in range(BT):
                                tile = 2 * BT * i + BT * p + k
                                v.bn_stats(one(mix_stats, tile), one(mix, tile)).then_inc(measured, 1)

                        @turns(v, BATCHES // 2)
                        def _(i):
                            for p in range(2):
                                project(i, p)
                            for p in range(2):
                                attend(i, p)
                        v.wait_ge(measured, TILES)
                        row_norm(v, own, mix_stats[:], mix_rstd[:], mix_shift[:], D, scope, "attn_mix")
                        @turns(v, BATCHES // 2)
                        def _(i):
                            for p in range(2):
                                wait(v, turned[p], i)
                                for k in range(BT):
                                    tile = 2 * BT * i + BT * p + k
                                    last = v.tensor_scalar(xw[p][:, k, :], one(mix, tile), one(mix_rstd, tile), one(mix_shift, tile), ALU.mult, ALU.add)
                                last.then_inc(again[p], 1)
                            for p in range(2):
                                v.wait_ge(projected[p], i + 1)
                                part = X[:, bass.ds((2 * i + p) * BT, BT), :]
                                v.tensor_tensor(sumrow[:], tiles(bank[2 + p][:]), along(R_BO), ALU.add).then_inc(added[p], 1)
                                v.wait_ge(added[p], i + 1)
                                v.tensor_tensor(part, part, sumrow[:], ALU.add).then_inc(summed_rows, 1)
                                v.wait_ge(summed_rows, 2 * i + p + 1)
                                for k in range(BT):
                                    tile = 2 * BT * i + BT * p + k
                                    v.bn_stats(one(stats, tile), one(X, tile))

        def mamba():
            scope = ExitStack()

            def s(n):
                return sem(f"mamba_{n}")

            def s2(n):
                return pair(f"mamba_{n}")

            def t(n, shape, dt=F32):
                return sb(scope, f"mamba_{n}", shape, dt)

            normed_rows, columns, columns_copied, all_columns = s2("normed_rows"), s2("columns"), s2("columns_copied"), s2("all_columns")
            dt_done, u_done, u_ready = s2("dt_done"), s2("u_done"), s2("u_ready")
            dt_clipped, dt_exped, dt_plus1, dt_logged = s("dt_clipped"), s("dt_exped"), s("dt_plus1"), s("dt_logged")
            rates_ready, cs_done, cs_ready, last_done, dec_ready, decays_ready = (
                s(n) for n in ("rates_ready", "cs_done", "cs_ready", "last_done", "dec_ready", "decays_ready"))
            in_done, in_copied, conv_done, relu_done, conv_ready = s("in_done"), s("in_copied"), s("conv_done"), s("relu_done"), s("conv_ready")
            x_turned, x_copied, seg_done, seg_shifted, seg_exped = s("x_turned"), s("x_copied"), s("seg_done"), s("seg_shifted"), s("seg_exped")
            cb_done, weights_ready, y_done, y_read, state_done, state_ready = (
                s(n) for n in ("cb_done", "weights_ready", "y_done", "y_read", "state_done", "state_ready"))
            again, turned, affine, projected, added = s2("again"), s2("turned"), s2("affine"), s2("projected"), s2("added")
            pads, least_done, cs_here = s("pads"), s("least_done"), s("cs_here")
            u_measured = s("u_measured")

            with scope:
                u = t("u", [P, TILES, INNER])
                xT_all = t("xT_all", [P, TOKENS])
                rates, cs, dec, ecs, elast = (t(n, [P, TILES * MH]) for n in ("rates", "cs", "dec", "ecs", "elast"))
                small = [t(f"small{k}", [P, TILES * MH]) for k in range(4)]
                expA = t("expA", [P, MH])
                out_rstd, out_shift = t("out_rstd", [P, TILES]), t("out_shift", [P, TILES])
                u_stats = t("u_stats", [P, TILES, 6])
                seg, weights = t("seg", [P, MH, P]), t("weights", [P, MH, P])
                xdec, ytmp = t("xdec", [P, INNER]), t("ytmp", [P, INNER])
                carry = t("carry", [STATE, INNER])
                carry_dec = t("carry_dec", [STATE, INNER])

                def tiles(ap):
                    return ap.rearrange("p (t d) -> p t d", t=BT)

                with ExitStack() as inner_scope, nc.Block() as block:
                    xw = [sb(inner_scope, f"mamba_xw{p}", [P, BT, D]) for p in range(2)]
                    xT = [sb(inner_scope, f"mamba_xT{p}", [P, SEQ]) for p in range(2)]
                    dt_bank = bank[6][:, 0:TILES * MH]

                    @block.sync
                    def _(sp):
                        clear_last_phase(sp)

                    @block.tensor
                    def _(pe):
                        @turns(pe, BATCHES // 2)
                        def _(i):
                            for p in range(2):
                                pe.wait_ge(normed_rows[p], i + 1)
                                wait(pe, columns_copied[p], i)
                                for k in range(BT):
                                    last = pe.transpose(bank[p][:, k * P:(k + 1) * P], xw[p][:, k, :], ident)
                                last.then_inc(columns[p], 1)
                            for p in range(2):
                                pe.wait_ge(columns_copied[p], i + 1)
                                for k in range(BT):
                                    last = pe.matmul(bank[6][:, bass.ds(MH * (2 * BT * i + BT * p + k), MH)], xT[p][:, k * P:(k + 1) * P],
                                                     win1[:, CH:CH + MH], start=True, stop=True)
                                last.then_inc(dt_done[p], 1)
                                wait(pe, u_ready[p], i)
                                for k in range(BT):
                                    last = pe.matmul(bank[2 + 2 * p + k // 2][:, (k % 2) * INNER:(k % 2 + 1) * INNER], xT[p][:, k * P:(k + 1) * P],
                                                     win2[:], start=True, stop=True)
                                last.then_inc(u_done[p], 1)
                        pe.wait_ge(rates_ready, 1)
                        pe.wait_ge(u_ready[1], BATCHES // 2)
                        pe.matmul(bank[7][:, 0:TILES * MH], const("upto"), rates[:], start=True, stop=True).then_inc(cs_done, 1)
                        pe.wait_ge(cs_ready, 1)
                        pe.matmul(bank[5][:, 0:TILES * MH], const("last_row"), cs[:], start=True, stop=True).then_inc(last_done, 1)

                    @block.scalar
                    def _(act):
                        @turns(act, BATCHES // 2)
                        def _(i):
                            for p in range(2):
                                act.wait_ge(columns[p], i + 1)
                                wait(act, u_done[p], i)
                                wait(act, all_columns[p], i)
                                act.activation(xT[p][:], bank[p][:], ACT.Copy).then_inc(columns_copied[p], 1)
                            for p in range(2):
                                act.wait_ge(u_done[p], i + 1)
                                for k in range(2):
                                    last = act.activation(u[:, bass.ds((2 * i + p) * BT + 2 * k, 2), :].rearrange("p t d -> p (t d)"),
                                                          bank[2 + 2 * p + k][:], ACT.Gelu)
                                last.then_inc(u_ready[p], 1)
                        act.activation(expA[:], row[:, R_ALOG:R_ALOG + MH], ACT.Exp)
                        act.wait_ge(dt_clipped, 1)
                        act.activation(small[0][:], small[0][:], ACT.Exp).then_inc(dt_exped, 1)
                        act.wait_ge(dt_plus1, 1)
                        act.activation(small[2][:], small[1][:], ACT.Ln).then_inc(dt_logged, 1)
                        act.wait_ge(dec_ready, 1)
                        act.activation(dec[:], dec[:], ACT.Exp)
                        act.activation(ecs[:], cs[:], ACT.Exp)
                        act.activation(elast[:], bank[5][:, 0:TILES * MH], ACT.Exp).then_inc(decays_ready, 1)

                    @block.vector
                    def _(v):
                        own = Chain(v, "mamba_own")
                        row_norm(v, own, stats[:], rstd[:], shift[:], D, inner_scope, "mamba_in")
                        @turns(v, BATCHES // 2)
                        def _(i):
                            for p in range(2):
                                wait(v, columns[p], i)
                                for k in range(BT):
                                    tile = 2 * BT * i + BT * p + k
                                    last = normed(v, xw[p][:, k, :], tile, one(X, tile))
                                last.then_inc(normed_rows[p], 1)
                            for p in range(2):
                                v.wait_ge(columns_copied[p], i + 1)
                                v.tensor_copy(xT_all[:, bass.ds((2 * i + p) * SEQ, SEQ)], xT[p][:]).then_inc(all_columns[p], 1)
                        for p in range(2):
                            v.wait_ge(dt_done[p], BATCHES // 2)
                        y, y1, ln, den = (a[:] for a in small)
                        v.tensor_scalar(y, dt_bank, 20.0, None, ALU.min).then_inc(dt_clipped, 1)
                        v.wait_ge(dt_exped, 1)
                        v.tensor_scalar(y1, y, 1.0, None, ALU.add).then_inc(dt_plus1, 1)
                        v.wait_ge(dt_plus1, 1)
                        own(v.tensor_scalar(den, y1, -1.0, None, ALU.add))
                        own(v.tensor_scalar(rates[:], den, 0.0, None, ALU.is_equal))
                        own(v.tensor_tensor(den, den, rates[:], ALU.add))
                        own(v.reciprocal(den, den))
                        v.wait_ge(dt_logged, 1)
                        own(v.tensor_tensor(ln, ln, rates[:], ALU.add))
                        own(v.tensor_tensor(ln, ln, den, ALU.mult))
                        own(v.tensor_tensor(ln, ln, y, ALU.mult))
                        own(v.scalar_tensor_tensor(ln, dt_bank, 20.0, ln, ALU.is_le, ALU.mult))
                        own(v.tensor_scalar(y, dt_bank, 20.0, None, ALU.is_gt))
                        own(v.tensor_tensor(y, y, dt_bank, ALU.mult))
                        own(v.tensor_tensor(ln, ln, y, ALU.add))
                        by_head = rates[:].rearrange("p (t h) -> p t h", h=MH)
                        v.scalar_tensor_tensor(by_head, ln.rearrange("p (t h) -> p t h", h=MH), -1.0,
                                               expA[:].unsqueeze(1).broadcast_to([P, TILES, MH]), ALU.mult, ALU.mult).then_inc(rates_ready, 1)
                        v.wait_ge(cs_done, 1)
                        v.tensor_copy(cs[:], bank[7][:, 0:TILES * MH]).then_inc(cs_ready, 1)
                        v.wait_ge(last_done, 1)
                        v.wait_ge(cs_ready, 1)
                        v.tensor_tensor(dec[:], bank[5][:, 0:TILES * MH], cs[:], ALU.subtract).then_inc(dec_ready, 1)

                with ExitStack() as inner_scope, nc.Block() as block:
                    def tt(n, shape):
                        return sb(inner_scope, f"mamba_{n}", shape)

                    cs_now = tt("cs_now", [P, BT * MH])
                    padded = tt("padded", [P, CC, TAPS - 1 + SEQ])
                    relu, least = tt("relu", [P, SEQ]), tt("least", [P, SEQ])
                    xconv = tt("xconv", [P, 2, SEQ])
                    bcT = [tt(f"bcT{p}", [P, SEQ]) for p in range(2)]
                    bT = [b[0:STATE] for b in bcT]
                    cT = [tt(f"cT{p}", [STATE, SEQ]) for p in range(2)]
                    xs = [tt(f"xs{p}", [P, BT, INNER]) for p in range(2)]
                    bs = [tt(f"bs{p}", [P, BT, STATE]) for p in range(2)]

                    def stages(eng, stage):
                        stage((0, 0), None)
                        stage((1, 1), (0, 0))
                        with eng.Fori(0, (BATCHES - 2) // 2) as i:
                            stage((2 * i + 2, 0), (2 * i + 1, 1))
                            stage((2 * i + 3, 1), (2 * i + 2, 0))
                        stage(None, (BATCHES - 1, 1))

                    @block.tensor
                    def _(pe):
                        def stage(conv, scan):
                            if conv:
                                j, p = conv
                            if scan:
                                g, r = scan

                            def take_in():
                                for c in range(CC):
                                    wait(pe, in_copied, CC * j + (c == 2))
                                    pe.matmul(bank[c % 2][:], win1[:, c * P:(c + 1) * P], xT_all[:, bass.ds(j * SEQ, SEQ)],
                                              start=True, stop=True).then_inc(in_done, 1)

                            def convolve(o, part):
                                if part == 0:
                                    pe.wait_ge(in_copied, CC * (j + 1))
                                    wait(pe, conv_ready, CC * j + (o == 2))
                                products = [(c, tap) for c in range(CC) for tap in range(TAPS)]
                                n = len(products) // 2
                                for c, tap in products[part * n:(part + 1) * n]:
                                    last = pe.matmul(bank[2 + o % 2][:], wconv[:, c, tap, o * P:(o + 1) * P], padded[:, c, tap:tap + SEQ],
                                                     start=(c, tap) == products[0], stop=(c, tap) == products[-1])
                                if part:
                                    last.then_inc(conv_done, 1)

                            def turn(c):
                                pe.wait_ge(conv_ready, CC * j + c + 1)
                                wait(pe, x_copied, CC * j + c)
                                if scan:
                                    pe.wait_ge(state_ready, (BT - 1) * (g + 1))
                                for k in range(BT):
                                    src = xconv[:, c, k * P:(k + 1) * P] if c < 2 else bcT[p][:, k * P:(k + 1) * P]
                                    last = pe.transpose(bank[4][:, k * P:(k + 1) * P], src, ident)
                                last.then_inc(x_turned, 1)

                            def pairs():
                                pe.wait_ge(conv_ready, CC * (g + 1))
                                wait(pe, weights_ready, BT * g)
                                for c in range(BT):
                                    last = pe.matmul(bank[6][:, c * P:(c + 1) * P], bT[r][:, c * P:(c + 1) * P], cT[r][:, c * P:(c + 1) * P],
                                                     start=True, stop=True)
                                last.then_inc(cb_done, 1)

                            def spread(c):
                                wait(pe, seg_shifted, BT * g + c)
                                for hd in range(MH):
                                    last = pe.matmul(bank[5][:, hd * P:(hd + 1) * P], cs_now[:, c * MH + hd:c * MH + hd + 1].to_broadcast([P, P]), ident,
                                                     start=True, stop=True)
                                last.then_inc(seg_done, 1)

                            def combine(c):
                                wait(pe, y_read, BT * g + c)
                                pe.wait_ge(weights_ready, BT * g + c + 1)
                                for hd in range(MH):
                                    last = pe.matmul(bank[7][:, hd * MP:(hd + 1) * MP], weights[:, hd, :], xs[r][:, c, hd * MP:(hd + 1) * MP],
                                                     start=True, stop=True)
                                if c:
                                    pe.wait_ge(state_ready, (BT - 1) * g + c)
                                    last = pe.matmul(bank[7][:, INNER:2 * INNER], cT[r][:, c * P:(c + 1) * P], carry[:], start=True, stop=True)
                                last.then_inc(y_done, 1)
                                if c < BT - 1:
                                    pe.wait_ge(x_copied, CC * (g + 1))
                                    wait(pe, state_ready, (BT - 1) * g + c)
                                    pe.matmul(bank[4][0:STATE, 0:INNER], bs[r][:, c, :], xdec[:], start=True, stop=True).then_inc(state_done, 1)

                            if conv:
                                take_in()
                            if scan:
                                pe.wait_ge(cs_here, g + 1)
                                pairs()
                                spread(0)
                            for n in range(BT):
                                if conv:
                                    convolve(n // 2, n % 2)
                                if scan:
                                    combine(n)
                                    if n + 1 < BT:
                                        spread(n + 1)
                            if conv:
                                convolve(2, 0)
                                turn(0)
                                turn(1)
                                convolve(2, 1)
                                turn(2)

                        pe.wait_ge(pads, 1)
                        stages(pe, stage)

                    @block.scalar
                    def _(act):
                        def stage(conv, scan):
                            if conv:
                                j, p = conv
                            if scan:
                                g, r = scan

                            def relu_part(o):
                                act.wait_ge(conv_done, CC * j + o + 1)
                                wait(act, conv_ready, CC * j + o)
                                act.activation(relu[:], bank[2 + o % 2][:], ACT.Relu, bias=vec[:, V_CONVB + o:V_CONVB + o + 1]).then_inc(relu_done, 1)

                            if conv:
                                for c in range(CC):
                                    act.wait_ge(in_done, CC * j + c + 1)
                                    wait(act, conv_done, CC * j)
                                    act.activation(padded[:, c, TAPS - 1:], bank[c % 2][:], ACT.Copy).then_inc(in_copied, 1)
                            for n in range(BT):
                                if scan:
                                    act.wait_ge(seg_shifted, BT * g + n + 1)
                                    act.activation(seg[:], seg[:], ACT.Exp).then_inc(seg_exped, 1)
                                if conv and n % 2:
                                    relu_part(n // 2)
                            if conv:
                                relu_part(2)

                        stages(act, stage)

                    @block.vector
                    def _(v):
                        loop = Chain(v, "mamba_scan")
                        per_scan = 3 * (BT - 1)

                        def stage(conv, scan):
                            if conv:
                                j, p = conv
                            if scan:
                                g, r = scan
                                loop.start(per_scan * g)

                            def prelu(o):
                                v.wait_ge(relu_done, CC * j + o + 1)
                                v.tensor_scalar(least[:], bank[2 + o % 2][:], vec[:, V_CONVB + o:V_CONVB + o + 1], 0.0, ALU.add, ALU.min).then_inc(least_done, 1)
                                v.wait_ge(least_done, CC * j + o + 1)
                                if o < 2:
                                    wait(v, x_turned, CC * j)
                                    v.scalar_tensor_tensor(xconv[:, o, :], least[:], vec[:, V_PRELU:V_PRELU + 1], relu[:], ALU.mult, ALU.add) \
                                        .then_inc(conv_ready, 1)
                                else:
                                    if scan:
                                        wait(v, y_done, BT * g)
                                    v.scalar_tensor_tensor(bcT[p][:], least[:], vec[:, V_PRELU:V_PRELU + 1], relu[:], ALU.mult, ALU.add)
                                    v.scalar_tensor_tensor(cT[p][:], least[STATE:], vec[STATE:, V_PRELU:V_PRELU + 1], relu[STATE:], ALU.mult, ALU.add) \
                                        .then_inc(conv_ready, 1)

                            def copy_turned(c):
                                v.wait_ge(x_turned, CC * j + c + 1)
                                if c < 2:
                                    v.tensor_copy(xs[p][:, :, c * P:(c + 1) * P], tiles(bank[4][:])).then_inc(x_copied, 1)
                                else:
                                    v.tensor_copy(bs[p][:], tiles(bank[4][:])[:, :, 0:STATE]).then_inc(x_copied, 1)

                            def heads(ap):
                                return ap.rearrange("p (h d) -> p h d", h=MH)

                            def by_head(tab, c, parts=P):
                                return tab[0:parts, bass.ds((g * BT + c) * MH, MH)].unsqueeze(2).broadcast_to([parts, MH, MP])

                            def decay(c):
                                v.wait_ge(seg_done, BT * g + c + 1)
                                wait(v, weights_ready, BT * g + c)
                                for hd in range(MH):
                                    last = v.scalar_tensor_tensor(seg[:, hd, :], bank[5][:, hd * P:(hd + 1) * P], one(cs, (g * BT + c) * MH + hd),
                                                                  const("causal"), ALU.subtract, ALU.add)
                                last.then_inc(seg_shifted, 1)

                            def weigh(c):
                                wait(v, y_done, BT * g + c)
                                v.wait_ge(x_copied, CC * (g + 1))
                                if c < BT - 1:
                                    wait(v, state_done, (BT - 1) * g + c)
                                    v.tensor_tensor(heads(xdec[:]), heads(xs[r][:, c, :]), by_head(dec, c), ALU.mult)
                                v.wait_ge(seg_exped, BT * g + c + 1)
                                if c == 0:
                                    v.wait_ge(cb_done, g + 1)
                                v.tensor_tensor(weights[:], seg[:], bank[6][:, c * P:(c + 1) * P].unsqueeze(1).broadcast_to([P, MH, P]), ALU.mult) \
                                    .then_inc(weights_ready, 1)

                            def finish(c):
                                tile = g * BT + c
                                v.wait_ge(y_done, BT * g + c + 1)
                                if c:
                                    loop(v.tensor_tensor(heads(ytmp[:]), heads(bank[7][:, INNER:2 * INNER]), by_head(ecs, c), ALU.mult))
                                    v.tensor_tensor(ytmp[:], ytmp[:], bank[7][:, 0:INNER], ALU.add).then_inc(y_read, 1)
                                else:
                                    v.tensor_copy(ytmp[:], bank[7][:, 0:INNER]).then_inc(y_read, 1)
                                v.wait_ge(y_read, BT * g + c + 1)
                                loop(v.tensor_tensor(one(u, tile), one(u, tile), ytmp[:].unsqueeze(1), ALU.mult))
                                v.bn_stats(one(u_stats, tile), one(u, tile)).then_inc(u_measured, 1)
                                if c == BT - 1:
                                    return
                                v.wait_ge(state_done, (BT - 1) * g + c + 1)
                                if c:
                                    loop(v.tensor_tensor(heads(carry_dec[:]), heads(carry[:]), by_head(elast, c, STATE), ALU.mult))
                                    v.tensor_tensor(carry[:], carry_dec[:], bank[4][0:STATE, 0:INNER], ALU.add).then_inc(state_ready, 1)
                                else:
                                    v.tensor_copy(carry[:], bank[4][0:STATE, 0:INNER]).then_inc(state_ready, 1)
                                v.wait_ge(state_ready, (BT - 1) * g + c + 1)

                            if scan:
                                wait(v, seg_done, BT * g)
                                v.tensor_copy(cs_now[:], cs[:, bass.ds(g * BT * MH, BT * MH)]).then_inc(cs_here, 1)
                                decay(0)
                                weigh(0)
                            for n in range(BT):
                                if scan:
                                    finish(n)
                                    if n + 1 < BT:
                                        decay(n + 1)
                                        weigh(n + 1)
                                if conv and n % 2:
                                    prelu(n // 2)
                            if scan:
                                assert loop.n == per_scan
                            if conv:
                                copy_turned(0)
                                copy_turned(1)
                                prelu(2)
                                copy_turned(2)

                        v.memset(padded[:, :, 0:TAPS - 1], 0.0).then_inc(pads, 1)
                        stages(v, stage)

                with ExitStack() as inner_scope, nc.Block() as block:
                    yw = [sb(inner_scope, f"mamba_yw{p}", [P, BT, INNER]) for p in range(2)]
                    yT = [sb(inner_scope, f"mamba_yT{p}", [P, 2, SEQ]) for p in range(2)]

                    @block.tensor
                    def _(pe):
                        @turns(pe, BATCHES // 2)
                        def _(i):
                            for p in range(2):
                                pe.wait_ge(again[p], i + 1)
                                wait(pe, affine[p], i)
                                for c in range(2):
                                    for k in range(BT):
                                        last = pe.transpose(bank[2 * p + c][:, k * P:(k + 1) * P], yw[p][:, k, c * P:(c + 1) * P], ident)
                                last.then_inc(turned[p], 1)
                            for p in range(2):
                                pe.wait_ge(affine[p], i + 1)
                                wait(pe, added[p], i)
                                for k in range(BT):
                                    for c in range(2):
                                        last = pe.matmul(bank[4 + p][:, k * P:(k + 1) * P], yT[p][:, c, k * P:(k + 1) * P], win3[:, c, :],
                                                         start=(c == 0), stop=(c == 1))
                                last.then_inc(projected[p], 1)

                    @block.scalar
                    def _(act):
                        @turns(act, BATCHES // 2)
                        def _(i):
                            for p in range(2):
                                act.wait_ge(turned[p], i + 1)
                                wait(act, projected[p], i)
                                for c in range(2):
                                    last = act.activation(yT[p][:, c, :], bank[2 * p + c][:], ACT.Identity, scale=vec[:, V_MG + c:V_MG + c + 1],
                                                          bias=vec[:, V_MB + c:V_MB + c + 1])
                                last.then_inc(affine[p], 1)

                    @block.vector
                    def _(v):
                        own = Chain(v, "mamba_out")
                        row_norm(v, own, u_stats[:], out_rstd[:], out_shift[:], INNER, inner_scope, "mamba_out")
                        @turns(v, BATCHES // 2)
                        def _(i):
                            for p in range(2):
                                wait(v, turned[p], i)
                                for k in range(BT):
                                    tile = 2 * BT * i + BT * p + k
                                    last = v.tensor_scalar(yw[p][:, k, :], one(u, tile), one(out_rstd, tile), one(out_shift, tile), ALU.mult, ALU.add)
                                last.then_inc(again[p], 1)
                            for p in range(2):
                                v.wait_ge(projected[p], i + 1)
                                part = X[:, bass.ds((2 * i + p) * BT, BT), :]
                                v.tensor_tensor(part, part, tiles(bank[4 + p][:]), ALU.add).then_inc(added[p], 1)
                                v.wait_ge(added[p], i + 1)
                                for k in range(BT):
                                    tile = 2 * BT * i + BT * p + k
                                    v.bn_stats(one(stats, tile), one(X, tile))

        a = (FA, 1, ACT.Gelu, wgA, w1A, w2A, False, False)
        b = (FB, 2, ACT.Silu, wgB, w1B, w2B, True)
        for phase in ("a0", "attention", "a1", "b0", "mamba", "b1"):
            next_phase()
            if phase[0] == "a" and phase != "attention":
                moe(phase, *a)
            elif phase == "attention":
                attention()
            elif phase == "mamba":
                mamba()
            else:
                layer0.close()
                moe(phase, *b, phase == "b1")


def digits():
    return np.array([c << 2 * (STEPS - 1 - step) for step in range(STEPS) for c in (1, 2, 3)] + [0] * 3)


def constants():
    k, m = np.arange(P)[:, None], np.arange(P)[None, :]
    e_t = np.arange(E * TILES)
    part = dict(
        ident=k == m, before=k < m, upto=k <= m, ones=k >= 0 * m, same_expert=k % E == m % E,
        last_row=(k == P - 1) & (m >= 0), head_mask=k // HD == m // HD,
        causal=np.where(m >= k, 0.0, NEG),
        prefer=np.broadcast_to(E - e_t // TILES, (P, E * TILES)),
        restart=np.broadcast_to(e_t % TILES != 0, (P, E * TILES)),
        row_no=P * np.arange(MAX_BLOCKS)[None, :] + k,
        digits=np.broadcast_to(digits(), (P, DIGITS)),
    )
    return np.concatenate([part[n].astype(np.float32) for n in PARTS], axis=1)


def layouts(inp):
    g = {k: np.asarray(v) for k, v in inp.items()}
    c = np.ascontiguousarray
    rep = lambda v: np.broadcast_to(v, (P, v.shape[-1]))
    return {
        "x": c(g["L0_attn_x"].reshape(TOKENS, D)),
        "consts": constants(),
        "ints": c(np.concatenate([np.broadcast_to(digits(), (P, DIGITS)),
                                  P * np.arange(2 * TILES)[None, :] + np.arange(P)[:, None]], axis=1).astype(np.int32)),
        "vecs": c(np.concatenate([g["L0_attn_bk"][:, None], g["L0_attn_ln_g"][:, None], g["L0_attn_ln_b"][:, None],
                                  g["L1_attn_conv_b"].reshape(CC, P).T, np.broadcast_to(g["L1_attn_prelu_a"], (P, 1)),
                                  g["L1_attn_ln_g"].reshape(2, P).T, g["L1_attn_ln_b"].reshape(2, P).T], axis=1)),
        "rows": c(np.concatenate([rep(g["L0_attn_bq"]), rep(g["L0_attn_bv"]), rep(g["L0_attn_bo"]), rep(g["L1_attn_A_log"])], axis=1)),
        "wqkvo": c(np.stack([g["L0_attn_W" + n].T for n in "qkvo"], axis=1)),
        "a_wg": g["L0_ffn_Wg"],
        "a_w1": c(g["L0_ffn_W1"].transpose(1, 0, 2)),
        "a_w2": c(g["L0_ffn_W2"].reshape(E, FA // P, P, D).transpose(2, 0, 1, 3)),
        "b_wg": c(g["L1_ffn_gate_w"].T),
        "b_w1": c(g["L1_ffn_experts_w1"].transpose(2, 0, 1)),
        "b_w2": c(g["L1_ffn_experts_w2"].transpose(0, 2, 1).reshape(E, FB // P, P, D).transpose(2, 0, 1, 3)),
        "b_sw1": c(g["L1_ffn_shared_w1"].T),
        "b_sw2": c(g["L1_ffn_shared_w2"].T.reshape(FB // P, P, D).transpose(1, 0, 2)),
        "m_in1": c(g["L1_attn_W_in1"][INNER:].T),
        "m_in2": c(g["L1_attn_W_in2"].T),
        "m_in3": c(g["L1_attn_W_in3"].T.reshape(INNER // P, P, D).transpose(1, 0, 2)),
        "m_conv": c(g["L1_attn_conv_w"].transpose(1, 2, 0).reshape(CC, P, TAPS, CH).transpose(1, 0, 2, 3)),
    }


def kernel(**inputs):
    import concourse.bacc as bacc
    from concourse.bass_utils import run_bass_kernel_spmd

    nc = bacc.Bacc("TRN2", target_bir_lowering=False, num_devices=1)
    arrays = layouts(inputs)
    args = {n: nc.dram_tensor(f"in_{n}", a.shape, mybir.dt.from_np(a.dtype), kind="ExternalInput").ap() for n, a in arrays.items()}
    result = nc.dram_tensor("result", (TOKENS, D), F32, kind="ExternalOutput").ap()
    program(nc, **args, out=result)
    r = run_bass_kernel_spmd(nc, [{f"in_{n}": a for n, a in arrays.items()}], core_ids=[0])
    return r.results[0]["result"].reshape(BATCHES, SEQ, D)
```

```python
from contextlib import ExitStack

import numpy as np

import concourse.bass as bass
from concourse import mybir

F32 = mybir.dt.float32
I32 = mybir.dt.int32
BF16 = mybir.dt.bfloat16
F32R = mybir.dt.float32r
ALU = mybir.AluOpType
ACT = mybir.ActivationFunctionType
AX = mybir.AxisListType

P = 128
D = 128
BATCHES, SEQ = 8, 512
TOKENS = BATCHES * SEQ
TILES = TOKENS // P
BT = SEQ // P
E = 8
FA, FB = 256, 512
CAP = TOKENS // E
HEADS = 16
HD = D // HEADS
INNER, STATE, MH = 256, 64, 4
MP = INNER // MH
CH = INNER + 2 * STATE
CC = CH // P
TAPS = 4
IN_BANK = (0, 1, 3)
EPS = 1e-5
NEG = -3e38
STEPS = 15
UNROLL = 5
DIGITS = 3 * (STEPS + 1)
GROUP = 8
MAX_BLOCKS = 2 * TILES + E
SLOTS = 8
ROW = D + 2

PARTS = dict(ident=P, not_before=P, upto=P, ones=P, same_expert=P, last_row=P, head_mask=P, causal=P,
             prefer=E * TILES, restart=E * TILES, row_no=MAX_BLOCKS, digits=DIGITS)
AT = {k: sum(list(PARTS.values())[:i]) for i, k in enumerate(PARTS)}
CONST_COLS = sum(PARTS.values())
V_BK, V_LNG, V_LNB, V_CONVB, V_PRELU, V_MG, V_MB, V_END = 0, 1, 2, 3, 6, 7, 9, 11
R_BQ, R_BV, R_BO, R_ALOG, R_END = 0, 128, 256, 384, 388


def wait(eng, semaphore, count):
    if not isinstance(count, int) or count > 0:
        eng.wait_ge(semaphore, count)


def turns(eng, n):
    def run(body):
        body(0)
        if n > 1:
            with eng.Fori(1, n) as i:
                body(i)
    return run


def program(nc, x, consts, ints, vecs, rows, wqkvo, a_wg, a_w1, a_w2, b_wg, b_w1, b_w2, b_sw1, b_sw2,
            m_in1, m_in2, m_in3, m_conv, out):
    ctx = ExitStack()
    with ctx:
        def sb(scope, name, shape, dt=F32):
            return scope.enter_context(nc.sbuf_tensor(name, shape, dt))

        held, signals = [ctx.enter_context(ExitStack())], [[]]

        def sem(name):
            signals[-1].append(held[-1].enter_context(nc.semaphore(name)))
            return signals[-1][-1]

        def next_phase():
            if len(held) > 2:
                held[-2].close()
            held.append(ctx.enter_context(ExitStack()))
            signals.append([])

        def clear_last_phase(sp):
            nums = sorted(h.num for h in signals[-2])
            while len(signals) > 2 and nums:
                n = 1
                while n < len(nums) and nums[n] == nums[0] + n:
                    n += 1
                sp.sem_clear(range(nums[0], nums[0] + n))
                nums = nums[n:]

        def pair(name):
            return [sem(f"{name}{q}") for q in range(2)]

        X = sb(ctx, "X", [P, TILES, D])
        stats = sb(ctx, "stats", [P, TILES, 6])
        rstd = sb(ctx, "rstd", [P, TILES])
        shift = sb(ctx, "shift", [P, TILES])
        table = sb(ctx, "table", [P, CONST_COLS])
        int_table = sb(ctx, "int_table", [P, DIGITS + 2 * TILES], I32)
        vec = sb(ctx, "vec", [P, V_END])
        row = sb(ctx, "row", [P, R_END])
        wgB = sb(ctx, "wgB", [P, E])
        w1B, w2B = sb(ctx, "w1B", [P, E, FB]), sb(ctx, "w2B", [P, E, FB // P, D])
        sw1B, sw2B = sb(ctx, "sw1B", [P, FB]), sb(ctx, "sw2B", [P, FB // P, D])
        win1, win2 = sb(ctx, "win1", [P, CH + MH]), sb(ctx, "win2", [P, INNER])
        win3 = sb(ctx, "win3", [P, INNER // P, D])
        layer0 = ctx.enter_context(ExitStack())
        wattn = sb(layer0, "wattn", [P, 4, D])
        wgA = sb(layer0, "wgA", [P, E])
        w1A, w2A = sb(layer0, "w1A", [P, E, FA]), sb(layer0, "w2A", [P, E, FA // P, D])
        bank = [ctx.enter_context(nc.psum_tensor(f"bank{i}", [P, 512], F32)) for i in range(8)]
        sorted_x = nc.dram_tensor("sorted_x", [MAX_BLOCKS * P, ROW], F32, kind="Internal").ap()
        token_y = nc.dram_tensor("token_y", [2 * TOKENS + MAX_BLOCKS * P, D], F32, kind="Internal").ap()

        def const(which):
            return table[:, AT[which]:AT[which] + PARTS[which]]

        ident = const("ident")

        def one(ap, i):
            return ap[:, bass.ds(i, 1)]

        class Chain:

            def __init__(self, eng, name):
                self.eng, self.sem, self.base, self.n = eng, sem(name), 0, 0

            def go(self, ins):
                self.n += 1
                ins.then_inc(self.sem, 1)

            def __call__(self, ins):
                self.go(ins)
                self.eng.wait_ge(self.sem, self.base + self.n)

            def start(self, base):
                self.base, self.n = base, 0

        def row_norm(v, own, st, rs, sh, width, scope, name):
            n = rs.shape[1]
            diff, total, var, t = (sb(scope, f"{name}_{k}", [P, n]) for k in ("diff", "total", "var", "newton"))
            seed = sb(scope, f"{name}_seed", [P, n], I32)
            own.go(v.tensor_tensor(diff[:], st[:, :, 1], st[:, :, 4], ALU.subtract))
            own.go(v.tensor_tensor(total[:], st[:, :, 1], st[:, :, 4], ALU.add))
            own(v.tensor_tensor(var[:], st[:, :, 2], st[:, :, 5], ALU.add))
            own(v.scalar_tensor_tensor(t[:], diff[:], 0.25, diff[:], ALU.mult, ALU.mult))
            own(v.scalar_tensor_tensor(var[:], var[:], 1.0 / width, t[:], ALU.mult, ALU.add))
            own(v.tensor_scalar(var[:], var[:], EPS, None, ALU.add))
            own(v.tensor_scalar(seed[:], var[:].bitcast(I32), 1, None, ALU.logical_shift_right))
            own(v.tensor_scalar(seed[:], seed[:], -1.0, float(0x5F3759DF), ALU.mult, ALU.add))
            r = seed[:].bitcast(F32)
            for _ in range(3):
                own(v.tensor_tensor(t[:], r, r, ALU.mult))
                own(v.scalar_tensor_tensor(t[:], t[:], -0.5, var[:], ALU.mult, ALU.mult))
                own(v.scalar_tensor_tensor(rs[:], t[:], 1.5, r, ALU.add, ALU.mult))
                r = rs[:]
            own(v.scalar_tensor_tensor(sh[:], total[:], -0.5, rs[:], ALU.mult, ALU.mult))

        def normed(v, dst, tile, src):
            return v.tensor_scalar(dst, src, one(rstd, tile), one(shift, tile), ALU.mult, ALU.add)

        def stages(eng, stage):
            stage((0, 0), None)
            stage((1, 1), (0, 0))
            with eng.Fori(0, (BATCHES - 4) // 2) as i:
                stage((2 * i + 2, 0), (2 * i + 1, 1))
                stage((2 * i + 3, 1), (2 * i + 2, 0))
            stage((BATCHES - 2, 0), (BATCHES - 3, 1))
            stage((BATCHES - 1, 1), (BATCHES - 2, 0))
            stage(None, (BATCHES - 1, 1))

        def ahead_of(front):
            j, p = front
            return None if isinstance(j, int) and j == BATCHES - 1 else (j + 1, 1 - p)

        scattered = [sem(f"scattered{h}") for h in range(2)]
        y_stored = [sem(f"y_stored{k}") for k in range(GROUP)]
        done = dict(scattered=0, y_stored=[0] * GROUP)

        x_loaded, zeroed, cleared = [sem(f"x_loaded{k}") for k in range(4)], sem("zeroed"), sem("cleared")
        tables_loaded, experts_loaded, others_loaded = sem("tables_loaded"), sem("experts_loaded"), sem("others_loaded")
        tables = ((table, consts), (int_table, ints), (wgA, a_wg))
        experts = ((w1A, a_w1), (w2A, a_w2))
        others = ((vec, vecs), (row, rows), (wattn, wqkvo), (wgB, b_wg), (w1B, b_w1), (w2B, b_w2), (sw1B, b_sw1), (sw2B, b_sw2),
                  (win1, m_in1), (win2, m_in2), (win3, m_in3))
        zeros = sb(layer0, "zeros", [P, MAX_BLOCKS // 4, ROW])
        with nc.Block(no_gpsimd_drain=True) as block:
            @block.sync
            def _(sp):
                for k in range(4):
                    part = slice(k * TILES // 4, (k + 1) * TILES // 4)
                    sp.dma_start(X[:, part, :], x.rearrange("(t p) d -> p t d", p=P)[:, part, :]).then_inc(x_loaded[k], 16)
                for dst, src in tables:
                    sp.dma_start(dst[:], src).then_inc(tables_loaded, 16)
                for dst, src in experts:
                    sp.dma_start(dst[:], src).then_inc(experts_loaded, 16)

            @block.gpsimd
            def _(pool):
                nc.gpsimd.memset(zeros[:], 0.0).then_inc(zeroed, 1)
                pool.wait_ge(zeroed, 1)
                for k in range(4):
                    pool.dma_start(sorted_x.rearrange("(k p t) d -> k p t d", k=4, p=P)[k], zeros[:]) \
                        .then_inc(cleared, 16)

            @block.vector
            def _(v):
                for k in range(4):
                    v.wait_ge(x_loaded[k], 16)
                    for tile in range(k * TILES // 4, (k + 1) * TILES // 4):
                        v.bn_stats(one(stats, tile), one(X, tile))

        def load_others(sp):
            for dst, src in others:
                sp.dma_start(dst[:], src).then_inc(others_loaded, 16)

        def moe(name, F, choices, func, wg, w1, w2, shared, final):
            NC = F // P
            NB = choices * TILES + E - 1
            TURNS = -(-NB // GROUP)
            LAST = NB - GROUP * (TURNS - 1)
            HALF_BANK, HALF = E * TILES, TILES // 2
            first = name == "a0"
            scope = ExitStack()

            def s(n):
                return sem(f"{name}_{n}")

            def s2(n):
                return pair(f"{name}_{n}")

            def t(n, shape, dt=F32):
                return sb(scope, f"{name}_{n}", shape, dt)

            normed_rows, columns, columns_copied, logits_done = s("normed_rows"), s("columns"), s("columns_copied"), s("logits_done")
            rows_kept, more_rows_kept, all_columns = s("rows_kept"), s("more_rows_kept"), s("all_columns")
            centred, exped, prob_ready, prob_turned = s("centred"), s("exped"), s("prob_ready"), s("prob_turned")
            counted, summed, thr_ready, thr_spread = s("counted"), s("summed"), s("thr_ready"), s("thr_spread")
            ties_ready, ties_summed, picked, picks_summed = s("ties_ready"), s("ties_summed"), s("picked"), s("picks_summed")
            digit = s("digit")
            pos_ready, experts_known = s("pos_ready"), s("experts_known")
            scattered0, stored0 = done["scattered"], done["y_stored"]
            done["scattered"] += 16 * HALF * choices
            stores = [16 * (TURNS if k < LAST else TURNS - 1) for k in range(GROUP)]
            done["y_stored"] = [a + b for a, b in zip(stored0, stores)]
            if shared:
                sh_up, sh_act, sh_down, sh_added = s("sh_up"), [s(f"sh_act{c}") for c in range(NC)], s2("sh_down"), s2("sh_added")
            blk_loaded = [s(f"blk_loaded{k}") for k in range(GROUP)]
            turned, xT_copied, up, activated = s2("turned"), s2("xT_copied"), s2("up"), s2("activated")
            tagged, down, y_copied = s2("tagged"), s2("down"), s2("y_copied")
            rows_tagged, used, used_by_pool, sent = s("rows_tagged"), s("used"), s("used_by_pool"), s("sent")
            result_loaded = [s(f"result_loaded{k}") for k in range(SLOTS)]

            with scope:
                xn = t("xn", [P, TILES, ROW])
                xw = [t(f"xw{q}", [P, BT, D]) for q in range(2)]
                xT = [t(f"xT{q}", [P, SEQ]) for q in range(2)]
                gate = [t(f"gate{k}", [P, TILES]) for k in range(choices)]
                pos = [t(f"pos{k}", [P, TILES], I32) for k in range(choices)]
                block_expert = t("block_expert", [P, NB + GROUP], I32)
                score, work = t("score", [P, E, TILES]), t("work", [P, E, TILES])
                above, pick, pick2 = (t(n, [P, E, TILES], BF16) for n in ("above", "pick", "pick2"))
                best, other = t("best", [P, TILES]), t("other", [P, TILES])
                by_tile = t("by_tile", [P, TILES, E])
                prob_rows, hits = t("prob_rows", [P, 2 * P]), t("hits", [P, 3, 2 * P])
                thr, cand, ahead, best_digit = (t(n, [P, w], I32) for n, w in (("thr", 1), ("cand", 3), ("ahead", 3), ("best_digit", 1)))
                count, digit_of, threshold = t("count", [P, 3], BF16), t("digit_of", [P, 3]), t("threshold", [P, 1])
                small = [t(f"small{k}", [P, E]) for k in range(3)]
                same_expert, not_before, ones = (t(n, [P, P], BF16) for n in ("same_expert", "not_before", "ones"))
                small_i = t("small_i", [P, E], I32)
                begun, begun_by, ended_by = t("begun", [P, NB, E]), t("begun_by", [P, NB]), t("ended_by", [P, NB])
                spare = t("spare", [P, NB], I32)
                if shared:
                    xnT = t("xnT", [P, TOKENS])
                    sh = [t(f"sh{q}", [P, NC, SEQ]) for q in range(2)]
                rows_in = [t(f"rows_in{k}", [P, ROW]) for k in range(GROUP)]
                goes_to = [t(f"goes_to{k}", [P, 1], I32) for k in range(GROUP)]
                gate_in = [t(f"gate_in{k}", [P, 1]) for k in range(GROUP)]
                bxT = [t(f"bxT{q}", [P, P]) for q in range(2)]
                bw1 = [t(f"bw1{q}", [P, F]) for q in range(2)]
                hT = [t(f"hT{q}", [P, F]) for q in range(2)]
                y = [t(f"y{k}", [P, D]) for k in range(GROUP)]
                got = [t(f"got{k}", [P, BT, D]) for k in range(SLOTS)]

                def digits(step):
                    return int_table[:, bass.ds(3 * step, 3)]

                def per_token(ap):
                    return ap.unsqueeze(1).broadcast_to([P, E, TILES])

                def per_expert(ap):
                    return ap.unsqueeze(2).broadcast_to([P, E, TILES])

                def over_experts(ap):
                    return ap.rearrange("p e t -> p t e")

                def flat(ap):
                    return ap.rearrange("p e t -> p (e t)")

                def routing(b):
                    return bank[b][:, 0:HALF_BANK].rearrange("p (e t) -> p e t", e=E)

                logits, sum_from, sum_tile, sum_above = routing(2), routing(3), routing(4), routing(5)

                def parity(i, k):
                    return k % 2, GROUP // 2 * i + k // 2

                def after(i, k, by):
                    return (i, k + by) if k + by < GROUP else (i + 1, k + by - GROUP)

                with nc.Block() as block:
                    @block.tensor
                    def _(pe):
                        if first:
                            pe.wait_ge(tables_loaded, 16 * len(tables))
                        def route(front, back):
                            if front:
                                j, p = front
                                pe.wait_ge(normed_rows, j + 1)
                                wait(pe, columns_copied, j - 1)
                                for k in range(BT):
                                    last = pe.transpose(bank[p][:, k * P:(k + 1) * P], xw[p][:, k, :], ident)
                                last.then_inc(columns, 1)
                            if back:
                                b, r = back
                                pe.wait_ge(columns_copied, b + 1)
                                for k in range(BT):
                                    last = pe.matmul(logits[:, :, bass.ds(BT * b + k, 1)], xT[r][:, k * P:(k + 1) * P],
                                                     wg[:], start=True, stop=True)
                                last.then_inc(logits_done, 1)

                        stages(pe, route)
                        if choices == 1:
                            pe.wait_ge(prob_ready, 1)
                            for half in range(2):
                                last = pe.transpose(bank[0][:, half * P:(half + 1) * P],
                                                    by_tile[:, 16 * half:16 * half + 16, :].rearrange("p t e -> p (t e)"), ident)
                            last.then_inc(prob_turned, 1)
                            with pe.Fori(0, STEPS // UNROLL) as i:
                                for u in range(UNROLL):
                                    pe.wait_ge(counted, UNROLL * i + u + 1)
                                    pe.matmul(bank[1][:, 0:3], same_expert[:], count[:], start=True, stop=True).then_inc(summed, 1)
                            pe.wait_ge(thr_ready, 1)
                            pe.matmul(bank[1][:, 0:E], threshold[:].to_broadcast([P, P]), ident[:, 0:E], start=True, stop=True) \
                                .then_inc(thr_spread, 1)
                            pe.wait_ge(ties_ready, 2)
                            pe.matmul(flat(sum_from), not_before[:], flat(pick[:]), start=True, stop=True)
                            pe.matmul(flat(sum_tile), ones[:], flat(pick[:]), start=True, stop=True)
                            pe.matmul(flat(sum_above), ones[:], flat(above[:]), start=True, stop=True).then_inc(ties_summed, 1)
                        pe.wait_ge(picked, 1)
                        pe.matmul(flat(sum_from), not_before[:], flat(above[:]), start=True, stop=True)
                        pe.matmul(flat(sum_tile), ones[:], flat(above[:]), start=True, stop=True).then_inc(picks_summed, 1)

                        if shared:
                            pe.wait_ge(pos_ready, choices)
                            pe.wait_ge(all_columns, BATCHES)
                            @turns(pe, BATCHES // 2)
                            def _(i):
                                for q in range(2):
                                    for c in range(NC):
                                        wait(pe, sh_act[c], 2 * i + q)
                                        pe.matmul(bank[c][:], sw1B[:, c * P:(c + 1) * P], xnT[:, bass.ds((2 * i + q) * SEQ, SEQ)],
                                                  start=True, stop=True).then_inc(sh_up, 1)
                                for q in range(2):
                                    pe.wait_ge(sh_act[NC - 1], 2 * i + q + 1)
                                    wait(pe, sh_added[q], i)
                                    for k in range(BT):
                                        for c in range(NC):
                                            last = pe.matmul(bank[6 + q][:, k * P:(k + 1) * P], sh[q][:, c, k * P:(k + 1) * P],
                                                             sw2B[:, c, :], start=(c == 0), stop=(c == NC - 1))
                                    last.then_inc(sh_down[q], 1)
                            for q in range(2):
                                pe.wait_ge(sh_added[q], BATCHES // 2)

                        def turn_rows(i, k):
                            q, n = parity(i, k)
                            pe.wait_ge(blk_loaded[k], 16 * (i + 1))
                            wait(pe, xT_copied[q], n)
                            pe.transpose(bank[q][:, 0:P], rows_in[k][:, 0:D], ident).then_inc(turned[q], 1)

                        def go_up(i, k):
                            q, n = parity(i, k)
                            pe.wait_ge(xT_copied[q], n + 1)
                            wait(pe, activated[q], n)
                            for c in range(NC):
                                last = pe.matmul(bank[2 + q][:, c * P:(c + 1) * P], bw1[q][:, c * P:(c + 1) * P], bxT[q][:],
                                                 start=True, stop=True)
                            last.then_inc(up[q], 1)

                        def come_down(i, k, e):
                            q, n = parity(i, k)
                            pe.wait_ge(activated[q], n + 1)
                            wait(pe, y_copied[q], n)
                            for c in range(NC):
                                last = pe.matmul(bank[6 + q][:, 0:D], hT[q][:, c * P:(c + 1) * P], w2[:, bass.ds(e, 1), c, :],
                                                 start=(c == 0), stop=(c == NC - 1))
                            last.then_inc(down[q], 1)

                        regs = [pe.alloc_register(f"{name}_expert{k}") for k in range(GROUP)]

                        def turn(i, last_turn):
                            pe.reg_load(regs, block_expert[0:1, bass.ds(GROUP * i, GROUP)])
                            for k in range(LAST if last_turn else GROUP):
                                if not (last_turn and k + 1 >= LAST):
                                    go_up(*after(i, k, 1))
                                if not (last_turn and k + 2 >= LAST):
                                    turn_rows(*after(i, k, 2))
                                come_down(i, k, pe.snap(regs[k], min_val=0, max_val=E - 1))

                        if first:
                            pe.wait_ge(experts_loaded, 16 * len(experts))
                        pe.wait_ge(experts_known, 1)
                        turn_rows(0, 0)
                        turn_rows(0, 1)
                        go_up(0, 0)

                        @turns(pe, TURNS - 1)
                        def _(i):
                            turn(i, False)
                        turn(TURNS - 1, True)

                    @block.scalar
                    def _(act):
                        def route(front, back):
                            if front:
                                j, p = front
                                act.wait_ge(columns, j + 1)
                                wait(act, logits_done, j - 1)
                                if shared:
                                    wait(act, all_columns, j - 1)
                                act.activation(xT[p][:], bank[p][:], ACT.Copy).then_inc(columns_copied, 1)
                                act.activation(xn[:, bass.ds(BT * j + BT // 2, BT // 2), 0:D], xw[p][:, BT // 2:BT, :], ACT.Copy) \
                                    .then_inc(more_rows_kept, 1)

                        stages(act, route)
                        act.wait_ge(centred, 1)
                        e = flat(work[:]) if choices == 1 else other[:]
                        act.activation(e, e, ACT.Exp).then_inc(exped, 1)
                        if shared:
                            @turns(act, BATCHES // 2)
                            def _(i):
                                for q in range(2):
                                    wait(act, sh_down[q], i)
                                    for c in range(NC):
                                        act.wait_ge(sh_up, 2 * NC * i + NC * q + c + 1)
                                        act.activation(sh[q][:, c, :], bank[c][:], func).then_inc(sh_act[c], 1)

                        def activate(i, k):
                            q, n = parity(i, k)
                            act.wait_ge(up[q], n + 1)
                            wait(act, down[q], n)
                            act.activation(hT[q][:], bank[2 + q][:, 0:F], func).then_inc(activated[q], 1)

                        def copy_y(i, k):
                            q, n = parity(i, k)
                            act.wait_ge(down[q], n + 1)
                            act.wait_ge(tagged[q], n + 1)
                            act.activation(y[k][:], bank[6 + q][:, 0:D], ACT.Copy, scale=gate_in[k][:]).then_inc(y_copied[q], 1)

                        def turn(i, last_turn):
                            for k in range(LAST if last_turn else GROUP):
                                if not (last_turn and k + 1 >= LAST):
                                    activate(*after(i, k, 1))
                                copy_y(i, k)

                        activate(0, 0)
                        @turns(act, TURNS - 1)
                        def _(i):
                            turn(i, False)
                        turn(TURNS - 1, True)

                    @block.vector
                    def _(v):
                        own = Chain(v, f"{name}_route")
                        row_norm(v, own, stats[:], rstd[:], shift[:], D, scope, name)
                        def route(front, back):
                            if front:
                                j, p = front
                                wait(v, columns, j - 1)
                                wait(v, rows_kept, j - 1)
                                wait(v, more_rows_kept, j - 1)
                                for k in range(BT):
                                    last = normed(v, xw[p][:, k, :], BT * j + k, one(X, BT * j + k))
                                last.then_inc(normed_rows, 1)
                            if back and shared:
                                b, r = back
                                v.wait_ge(columns_copied, b + 1)
                                v.tensor_copy(xnT[:, bass.ds(b * SEQ, SEQ)], xT[r][:]).then_inc(all_columns, 1)

                        stages(v, route)
                        if first:
                            v.wait_ge(tables_loaded, 16 * len(tables))
                        for n, tab in (("same_expert", same_expert), ("not_before", not_before), ("ones", ones)):
                            own.go(v.tensor_copy(tab[:], const(n)))
                        v.wait_ge(logits_done, BATCHES)
                        if first:
                            v.wait_ge(experts_loaded, 16 * len(experts))
                        prefer = const("prefer").rearrange("p (e t) -> p e t", e=E)

                        def first_of_best(dst, value, top):
                            own(v.tensor_tensor(dst, value, per_token(top), ALU.is_equal))
                            own(v.tensor_tensor(dst, dst, prefer, ALU.mult))
                            own(v.tensor_reduce(other[:], over_experts(dst), AX.X, ALU.max))
                            own(v.tensor_tensor(dst, dst, per_token(other[:]), ALU.is_equal))

                        if choices == 1:
                            own(v.tensor_reduce(best[:], over_experts(logits), AX.X, ALU.max))
                            v.tensor_tensor(work[:], logits, per_token(best[:]), ALU.subtract).then_inc(centred, 1)
                            v.wait_ge(exped, 1)
                            own(v.tensor_reduce(best[:], over_experts(work[:]), AX.X, ALU.add))
                            own(v.reciprocal(best[:], best[:]))
                            own(v.tensor_tensor(score[:], work[:], per_token(best[:]), ALU.mult))
                            own(v.memset(thr[:], 0))
                            own(v.tensor_copy(cand[:], digits(0)))
                            v.tensor_copy(by_tile[:], over_experts(score[:])).then_inc(prob_ready, 1)
                            v.wait_ge(prob_turned, 1)
                            own(v.tensor_copy(prob_rows[:], bank[0][:, 0:2 * P]))
                            with v.Fori(0, STEPS // UNROLL) as i:
                                for u in range(UNROLL):
                                    step = UNROLL * i + u
                                    for c in range(3):
                                        last = v.tensor_scalar(hits[:, c, :], prob_rows[:], cand[:, c:c + 1].bitcast(F32), None, ALU.is_ge, ALU.add,
                                                               accum_out=count[:, c:c + 1])
                                    last.then_inc(counted, 1)
                                    v.tensor_tensor(ahead[:], thr[:].to_broadcast([P, 3]), digits(step + 1), ALU.bitwise_or).then_inc(digit, 1)
                                    v.wait_ge(summed, step + 1)
                                    v.scalar_tensor_tensor(digit_of[:], bank[1][:, 0:3], float(CAP), const("digits")[:, bass.ds(3 * step, 3)],
                                                           ALU.is_ge, ALU.mult).then_inc(digit, 1)
                                    v.wait_ge(digit, 5 * step + 2)
                                    v.tensor_reduce(best_digit[:], digit_of[:], AX.X, ALU.max).then_inc(digit, 1)
                                    v.wait_ge(digit, 5 * step + 3)
                                    v.tensor_tensor(cand[:], ahead[:], best_digit[:].to_broadcast([P, 3]), ALU.bitwise_or).then_inc(digit, 1)
                                    v.tensor_tensor(thr[:], thr[:], best_digit[:], ALU.bitwise_or).then_inc(digit, 1)
                                    v.wait_ge(digit, 5 * step + 5)
                            v.tensor_copy(threshold[:], thr[:].bitcast(F32)).then_inc(thr_ready, 1)
                            v.wait_ge(thr_spread, 1)
                            own(v.tensor_copy(small[0][:], bank[1][:, 0:E]))
                            v.tensor_tensor(above[:], score[:], per_expert(small[0][:]), ALU.is_gt).then_inc(ties_ready, 1)
                            v.tensor_tensor(pick[:], score[:], per_expert(small[0][:]), ALU.is_equal).then_inc(ties_ready, 1)
                            v.wait_ge(ties_summed, 1)
                            own.go(v.tensor_tensor_scan(flat(work[:]), const("restart"), flat(sum_tile), 0.0, ALU.mult, ALU.add))
                            own(v.tensor_reduce(small[1][:], sum_above, AX.X, ALU.add))
                            own.go(v.tensor_tensor(work[:], work[:], sum_from, ALU.add))
                            own(v.tensor_scalar(small[1][:], small[1][:], -1.0, float(CAP), ALU.mult, ALU.add))
                            own(v.tensor_tensor(pick2[:], work[:], per_expert(small[1][:]), ALU.is_lt))
                            own(v.tensor_tensor(pick2[:], pick2[:], pick[:], ALU.mult))
                            own(v.tensor_tensor(pick2[:], pick2[:], above[:], ALU.add))
                            own(v.tensor_reduce(best[:], over_experts(pick2[:]), AX.X, ALU.max))
                            own(v.tensor_tensor(pick2[:], pick2[:], per_token(best[:]), ALU.is_ge))
                            own(v.tensor_tensor(score[:], score[:], pick2[:], ALU.mult))
                            own(v.scalar_tensor_tensor(score[:], pick2[:], -1.0, score[:], ALU.add, ALU.add))
                            own(v.tensor_reduce(gate[0][:], over_experts(score[:]), AX.X, ALU.max))
                            first_of_best(above[:], score[:], gate[0][:])
                            v.tensor_scalar(gate[0][:], gate[0][:], 0.5, None, ALU.mult).then_inc(picked, 1)
                            chosen = [above]
                        else:
                            own(v.tensor_copy(score[:], logits))
                            own(v.tensor_reduce(best[:], over_experts(score[:]), AX.X, ALU.max))
                            first_of_best(pick[:], score[:], best[:])
                            own(v.tensor_scalar(work[:], pick[:], -1.0, 1.0, ALU.mult, ALU.add))
                            own(v.tensor_tensor(score[:], score[:], work[:], ALU.mult))
                            own(v.scalar_tensor_tensor(flat(score[:]), flat(pick[:]), NEG, flat(score[:]), ALU.mult, ALU.add))
                            own(v.tensor_reduce(gate[1][:], over_experts(score[:]), AX.X, ALU.max))
                            first_of_best(pick2[:], score[:], gate[1][:])
                            v.tensor_tensor(above[:], pick[:], pick2[:], ALU.add).then_inc(picked, 1)
                            v.tensor_tensor(other[:], gate[1][:], best[:], ALU.subtract).then_inc(centred, 1)
                            v.wait_ge(exped, 1)
                            own(v.tensor_scalar(best[:], other[:], 1.0, None, ALU.add))
                            own(v.reciprocal(best[:], best[:]))
                            own(v.tensor_scalar(gate[0][:], best[:], 0.5, None, ALU.mult))
                            own(v.tensor_tensor(gate[1][:], gate[0][:], other[:], ALU.mult))
                            chosen = [pick, pick2]
                        v.wait_ge(picks_summed, 1)
                        own.go(v.tensor_tensor_scan(flat(score[:]), const("restart"), flat(sum_tile), 0.0, ALU.mult, ALU.add))
                        own(v.tensor_reduce(small[0][:], sum_tile, AX.X, ALU.add))
                        own.go(v.tensor_tensor(score[:], score[:], sum_from, ALU.add))
                        own(v.tensor_scalar(small_i[:], small[0][:], float(P - 1), None, ALU.add))
                        log_p = P.bit_length() - 1
                        own(v.tensor_scalar(small_i[:], small_i[:], log_p, log_p, ALU.logical_shift_right, ALU.logical_shift_left))
                        own(v.tensor_copy(small[1][:], small_i[:]))
                        own(v.tensor_tensor_scan(small[2][:], const("ones")[:, 0:E], small[1][:], 0.0, ALU.mult, ALU.add))
                        own(v.tensor_tensor(small[2][:], small[2][:], small[1][:], ALU.subtract))
                        own(v.tensor_tensor(score[:], score[:], per_expert(small[2][:]), ALU.add))
                        for k, c in enumerate(chosen):
                            own(v.tensor_tensor(work[:], c[:], score[:], ALU.mult))
                            own(v.tensor_reduce(best[:], over_experts(work[:]), AX.X, ALU.add))
                            v.tensor_copy(pos[k][:], best[:]).then_inc(pos_ready, 1)
                            v.wait_ge(pos_ready, k + 1)
                        by_block = [P, NB, E]
                        row_no = const("row_no")[:, 0:NB]
                        own(v.tensor_tensor(begun[:], row_no.unsqueeze(2).broadcast_to(by_block),
                                            small[2][:].unsqueeze(1).broadcast_to(by_block), ALU.is_ge))
                        own(v.tensor_reduce(begun_by[:], begun[:], AX.X, ALU.add))
                        own(v.memset(block_expert[:], 0))
                        own(v.tensor_scalar(block_expert[:, 0:NB], begun_by[:], -1.0, None, ALU.add))
                        own(v.tensor_tensor(small[2][:], small[2][:], small[0][:], ALU.add))
                        own(v.tensor_tensor(begun[:], row_no.unsqueeze(2).broadcast_to(by_block),
                                            small[2][:].unsqueeze(1).broadcast_to(by_block), ALU.is_ge))
                        own(v.tensor_reduce(ended_by[:], begun[:], AX.X, ALU.add))
                        own(v.tensor_tensor(ended_by[:], ended_by[:], begun_by[:], ALU.subtract))
                        own(v.tensor_scalar(begun_by[:], row_no, float(choices * TOKENS), None, ALU.add))
                        v.scalar_tensor_tensor(spare[:], ended_by[:], 1.0, begun_by[:], ALU.add, ALU.mult).then_inc(experts_known, 1)

                        if shared:
                            @turns(v, BATCHES // 2)
                            def _(i):
                                for q in range(2):
                                    v.wait_ge(sh_down[q], i + 1)
                                    part = X[:, bass.ds((2 * i + q) * BT, BT), :].rearrange("p t d -> p (t d)")
                                    v.scalar_tensor_tensor(part, bank[6 + q][:], 0.5, part, ALU.mult, ALU.add).then_inc(sh_added[q], 1)

                        def copy_columns(i, k, e):
                            q, n = parity(i, k)
                            wait(v, up[q], n)
                            v.tensor_copy(bw1[q][:].unsqueeze(1), w1[:, bass.ds(e, 1), :])
                            v.wait_ge(turned[q], n + 1)
                            v.tensor_copy(bxT[q][:], bank[q][:, 0:P]).then_inc(xT_copied[q], 1)
                            wait(v, y_stored[k], 16 * i + stored0[k])
                            v.tensor_tensor(goes_to[k][:], rows_in[k][:, D:D + 1].bitcast(I32), one(spare, GROUP * i + k), ALU.max)
                            v.tensor_copy(gate_in[k][:], rows_in[k][:, D + 1:D + 2]).then_inc(tagged[q], 1)

                        regs = [v.alloc_register(f"{name}_expert{k}") for k in range(GROUP)]

                        def turn(i, last_turn):
                            v.reg_load(regs, block_expert[0:1, bass.ds(GROUP * i + 2, GROUP)])
                            for k in range(LAST if last_turn else GROUP):
                                if not (last_turn and k + 2 >= LAST):
                                    copy_columns(*after(i, k, 2), v.snap(regs[k], min_val=0, max_val=E - 1))

                        v.wait_ge(experts_known, 1)
                        v.reg_load(regs[0:2], block_expert[0:1, 0:2])
                        for k in range(2):
                            copy_columns(0, k, v.snap(regs[k], min_val=0, max_val=E - 1))

                        @turns(v, TURNS - 1)
                        def _(i):
                            turn(i, False)
                        turn(TURNS - 1, True)

                        @turns(v, choices * BATCHES // SLOTS)
                        def _(i):
                            for k in range(SLOTS):
                                b, n = (SLOTS // choices) * i + k // choices, SLOTS // 2 * i + k // 2 + 1
                                if k % 2:
                                    part = X[:, bass.ds(BT * b, BT), :]
                                    if shared:
                                        v.wait_ge(used_by_pool, n)
                                    v.wait_ge(result_loaded[k], 16 * (i + 1))
                                    v.tensor_tensor(part, part, got[k][:], ALU.add).then_inc(used, 1)
                                    v.wait_ge(used, n)
                                else:
                                    v.wait_ge(used_by_pool, n)
                                if k % choices == choices - 1 and not final:
                                    for t_ in range(BT):
                                        v.bn_stats(one(stats, BT * b + t_), one(X, BT * b + t_))

                    @block.sync
                    def _(sp):
                        clear_last_phase(sp)
                        if first:
                            load_others(sp)
                        for h in range(2):
                            sp.wait_ge(scattered[h], 16 * HALF * choices + scattered0)

                        def turn(i, last_turn):
                            for k in range(LAST if last_turn else GROUP):
                                q, n = parity(i, k)
                                wait(sp, tagged[q], n + 1 - GROUP // 2)
                                sp.dma_start(rows_in[k][:], sorted_x[bass.ds((GROUP * i + k) * P, P), :]).then_inc(blk_loaded[k], 16)

                        @turns(sp, TURNS - 1)
                        def _(i):
                            turn(i, False)
                        turn(TURNS - 1, True)
                        for k in range(GROUP):
                            sp.wait_ge(y_stored[k], stored0[k] + stores[k])
                        if first:
                            sp.wait_ge(others_loaded, 16 * len(others))

                        def send(b):
                            sp.dma_start(out[bass.ds(SEQ * b, SEQ), :].rearrange("(t p) d -> p t d", p=P),
                                         X[:, bass.ds(BT * b, BT), :]).then_inc(sent, 16)

                        for n in range(choices * BATCHES):
                            if n >= SLOTS:
                                sp.wait_ge(used if n % 2 else used_by_pool, (n - SLOTS) // 2 + 1)
                            b, c = n // choices, n % choices
                            sp.dma_start(got[n % SLOTS][:], token_y[c * TOKENS + b * SEQ:c * TOKENS + (b + 1) * SEQ, :]
                                         .rearrange("(t p) d -> p t d", p=P)).then_inc(result_loaded[n % SLOTS], 16)
                        if final:
                            @turns(sp, BATCHES)
                            def _(b):
                                sp.wait_ge(used, b + 1)
                                send(b)
                            sp.wait_ge(sent, 16 * BATCHES)

                    @block.gpsimd
                    def _(pool):
                        def route(front, back):
                            if front:
                                j, p = front
                                pool.wait_ge(normed_rows, j + 1)
                                pool.tensor_copy(xn[:, bass.ds(BT * j, BT // 2), 0:D], xw[p][:, 0:BT // 2, :]).then_inc(rows_kept, 1)

                        stages(pool, route)
                        pool.wait_ge(rows_kept, BATCHES)
                        pool.wait_ge(more_rows_kept, BATCHES)
                        if first:
                            pool.wait_ge(tables_loaded, 16 * len(tables))
                            pool.wait_ge(cleared, 16 * 4)
                        for k in range(choices):
                            pool.wait_ge(pos_ready, k + 1)
                            for h in range(2):
                                part = slice(h * HALF, (h + 1) * HALF)
                                if k > 0:
                                    pool.wait_ge(scattered[h], 16 * HALF * k + scattered0)
                                ids = int_table[:, DIGITS + k * TILES + h * HALF:DIGITS + k * TILES + (h + 1) * HALF]
                                pool.tensor_copy(xn[:, part, D].bitcast(I32), ids).then_inc(rows_tagged, 1)
                                pool.tensor_copy(xn[:, part, D + 1], gate[k][:, part]).then_inc(rows_tagged, 1)
                                pool.wait_ge(rows_tagged, 2 * (2 * k + h + 1))
                                for tile in range(h * HALF, (h + 1) * HALF):
                                    pool.indirect_dma_start(sorted_x, bass.IndirectOffsetOnAxis(ap=pos[k][:, tile:tile + 1], axis=0),
                                                            xn[:, tile, :], None).then_inc(scattered[h], 16)

                        for i in range(TURNS):
                            for k in range(GROUP if i < TURNS - 1 else LAST):
                                q, n = parity(i, k)
                                pool.wait_ge(y_copied[q], n + 1)
                                pool.indirect_dma_start(token_y, bass.IndirectOffsetOnAxis(ap=goes_to[k][:], axis=0), y[k][:], None) \
                                    .then_inc(y_stored[k], 16)

                        if shared:
                            for q in range(2):
                                pool.wait_ge(sh_added[q], BATCHES // 2)

                        @turns(pool, choices * BATCHES // SLOTS)
                        def _(i):
                            for k in range(0, SLOTS, 2):
                                b = (SLOTS // choices) * i + k // choices
                                part = X[:, bass.ds(BT * b, BT), :]
                                pool.wait_ge(result_loaded[k], 16 * (i + 1))
                                pool.tensor_tensor(part, part, got[k][:], ALU.add).then_inc(used_by_pool, 1)

        def attention():
            scope = ExitStack()

            def s(n):
                return sem(f"attn_{n}")

            def t(n, shape, dt=F32):
                return sb(scope, f"attn_{n}", shape, dt)

            normed_rows, bias_added, columns, columns_copied = s("normed_rows"), s("bias_added"), s("columns"), s("columns_copied")
            k_done, q_done, v_done, k_max, k_exped = s("k_done"), s("q_done"), s("v_done"), s("k_max"), s("k_exped")
            q_centred, q_exped, q_ready, v_copied = s("q_centred"), s("q_exped"), s("q_ready"), s("v_copied")
            k_turned, k_copied, state_done, state_ready = s("k_turned"), s("k_copied"), s("state_done"), s("state_ready")
            q_turned, q_copied, mixed, kept = s("q_turned"), s("q_copied"), s("mixed"), s("kept")
            again, turned, affine, projected, added = s("again"), s("turned"), s("affine"), s("projected"), s("added")
            scales_ready, measured = s("scales_ready"), s("measured")

            with scope:
                mix = t("mix", [P, TILES, D])
                mix_stats = t("mix_stats", [P, TILES, 6])
                mix_rstd, mix_shift = t("mix_rstd", [P, TILES]), t("mix_shift", [P, TILES])
                xw, xT = [t(f"xw{p}", [P, BT, D]) for p in range(2)], [t(f"xT{p}", [P, SEQ]) for p in range(2)]
                kx, kxT = [t(f"kx{p}", [P, SEQ]) for p in range(2)], [t(f"kxT{p}", [P, SEQ]) for p in range(2)]
                qx, qxT = [t(f"qx{p}", [P, BT, D]) for p in range(2)], [t(f"qxT{p}", [P, SEQ]) for p in range(2)]
                vx = [t(f"vx{p}", [P, SEQ]) for p in range(2)]
                state = [t(f"state{p}", [P, D]) for p in range(2)]
                kbias, ksum, krec = ([t(f"{n}{p}", [P, 1]) for p in range(2)] for n in ("kbias", "ksum", "krec"))
                kmax, head, means = t("kmax", [P, 1]), t("head", [P, BT * HEADS]), t("means", [P, D])
                bk = vec[:, V_BK:V_BK + 1]

                def along(which):
                    return row[:, which:which + D].unsqueeze(1).broadcast_to([P, BT, D])

                def tiles(ap):
                    return ap.rearrange("p (t d) -> p t d", t=BT)

                def cut(ap, k):
                    return ap[:, k * P:(k + 1) * P]

                def heads(ap):
                    return ap.rearrange("p t (h d) -> p (t h) d", d=HD)

                def by_head(ap):
                    return ap.unsqueeze(2).broadcast_to([P, BT * HEADS, HD])

                def sequence(ap, j):
                    return ap[:, bass.ds(BT * j, BT), :]

                wq, wk, wv, wo = (wattn[:, n, :] for n in range(4))

                with nc.Block() as block:
                    @block.sync
                    def _(sp):
                        clear_last_phase(sp)

                    @block.tensor
                    def _(pe):
                        def stage(front, back):
                            if front:
                                j, p = front
                                pe.wait_ge(normed_rows, j + 1)
                                wait(pe, columns_copied, j)
                                for k in range(BT):
                                    last = pe.transpose(cut(bank[0], k), xw[p][:, k, :], ident)
                                last.then_inc(columns, 1)
                            if back:
                                b, r = back
                                pe.wait_ge(k_exped, b + 1)
                                wait(pe, k_copied, b)
                                for k in range(BT):
                                    last = pe.transpose(cut(bank[4], k), cut(kx[r], k), ident)
                                last.then_inc(k_turned, 1)
                            if front:
                                pe.wait_ge(columns_copied, j + 1)
                                wait(pe, k_exped, j)
                                pe.matmul(bank[1][:], wk, xT[p][:], start=True, stop=True).then_inc(k_done, 1)
                            if back:
                                pe.wait_ge(q_ready, b + 1)
                                wait(pe, q_copied, b)
                                for k in range(BT):
                                    last = pe.transpose(cut(bank[6], k), qx[r][:, k, :], ident)
                                last.then_inc(q_turned, 1)
                                pe.wait_ge(k_copied, b + 1)
                                pe.wait_ge(v_copied, b + 1)
                                wait(pe, state_ready, b)
                                for k in range(BT):
                                    last = pe.matmul(bank[5][:, 0:D], cut(kxT[r], k), cut(vx[r], k), start=(k == 0), stop=(k == BT - 1))
                                last.then_inc(state_done, 1)
                            if front:
                                wait(pe, q_centred, j)
                                for k in range(BT):
                                    last = pe.matmul(cut(bank[2], k), cut(xT[p], k), wq, start=True, stop=True)
                                last.then_inc(q_done, 1)
                            if back:
                                pe.wait_ge(state_ready, b + 1)
                                pe.wait_ge(q_copied, b + 1)
                                wait(pe, kept, b)
                                for k in range(BT):
                                    last = pe.matmul(cut(bank[7], k), cut(qxT[r], k), state[r][:], start=True, stop=True)
                                last.then_inc(mixed, 1)
                            if front:
                                wait(pe, v_copied, j)
                                for k in range(BT):
                                    last = pe.matmul(cut(bank[3], k), cut(xT[p], k), wv, start=True, stop=True)
                                last.then_inc(v_done, 1)

                        stages(pe, stage)

                        def project(front, back):
                            if front:
                                j, p = front
                                pe.wait_ge(again, j + 1)
                                wait(pe, affine, j - 1)
                                for k in range(BT):
                                    last = pe.transpose(cut(bank[p], k), xw[p][:, k, :], ident)
                                last.then_inc(turned, 1)
                            if back:
                                b, r = back
                                pe.wait_ge(affine, b + 1)
                                wait(pe, added, b)
                                for k in range(BT):
                                    last = pe.matmul(cut(bank[2 + r], k), cut(xT[r], k), wo, start=True, stop=True)
                                last.then_inc(projected, 1)

                        pe.wait_ge(kept, BATCHES)
                        stages(pe, project)

                    @block.scalar
                    def _(act):
                        def norm(which):
                            j, p = which
                            wait(act, columns, j - 1)
                            for k in range(BT):
                                tile = BT * j + k
                                last = act.activation(xw[p][:, k, :], one(X, tile), ACT.Identity, scale=one(rstd, tile), bias=one(shift, tile))
                            last.then_inc(normed_rows, 1)

                        act.wait_ge(scales_ready, 1)
                        norm((0, 0))

                        def stage(front, back):
                            if front:
                                j, p = front
                                act.wait_ge(columns, j + 1)
                                wait(act, v_done, j - 1)
                                act.activation(xT[p][:], bank[0][:], ACT.Copy).then_inc(columns_copied, 1)
                            if back:
                                b, r = back
                                act.wait_ge(k_turned, b + 1)
                                wait(act, state_done, b)
                                act.activation(kxT[r][:], bank[4][:], ACT.Copy).then_inc(k_copied, 1)
                                act.wait_ge(q_turned, b + 1)
                                wait(act, mixed, b)
                                act.activation(qxT[r][:], bank[6][:], ACT.Copy).then_inc(q_copied, 1)
                            if front and ahead_of(front):
                                norm(ahead_of(front))
                            if front:
                                act.wait_ge(k_max, j + 1)
                                wait(act, k_turned, j - 1)
                                act.activation(kx[p][:], bank[1][:], ACT.Exp, bias=kbias[p][:], accum_out=ksum[p][:]).then_inc(k_exped, 1)
                            if back:
                                act.wait_ge(mixed, b + 1)
                                act.activation(sequence(mix, b), tiles(bank[7][:]), ACT.Copy).then_inc(kept, 1)
                            if front:
                                act.wait_ge(q_centred, j + 1)
                                act.activation(qx[p][:], qx[p][:], ACT.Exp).then_inc(q_exped, 1)
                                act.wait_ge(v_done, j + 1)
                                wait(act, state_done, j - 1)
                                act.activation(vx[p][:], bank[3][:], ACT.Copy).then_inc(v_copied, 1)

                        stages(act, stage)

                        def project(front, back):
                            if front:
                                j, p = front
                                act.wait_ge(turned, j + 1)
                                wait(act, projected, j - 1)
                                act.activation(xT[p][:], bank[p][:], ACT.Identity, scale=vec[:, V_LNG:V_LNG + 1],
                                               bias=vec[:, V_LNB:V_LNB + 1]).then_inc(affine, 1)

                        stages(act, project)

                    @block.vector
                    def _(v):
                        own = Chain(v, "attn_own")
                        row_norm(v, own, stats[:], rstd[:], shift[:], D, scope, "attn_in")
                        v.tensor_copy(kmax[:], rstd[:, 0:1]).then_inc(scales_ready, 1)
                        v.wait_ge(scales_ready, 1)
                        front_own, back_own = Chain(v, "attn_front"), Chain(v, "attn_back")

                        def stage(front, back):
                            if front:
                                j, p = front
                                front_own.start(7 * j)
                                v.wait_ge(k_done, j + 1)
                                front_own(v.tensor_reduce(kmax[:], bank[1][:], AX.X, ALU.max))
                                front_own(v.tensor_scalar(kbias[p][:], kmax[:], bk, -1.0, ALU.add, ALU.mult))
                                v.tensor_tensor(kbias[p][:], kbias[p][:], bk, ALU.add).then_inc(k_max, 1)
                            if back:
                                b, r = back
                                back_own.start(b)
                                v.wait_ge(state_done, b + 1)
                                back_own(v.scalar_tensor_tensor(means[:], bank[5][:, 0:D], krec[r][:], row[:, R_BV:R_BV + D], ALU.mult, ALU.add))
                                wait(v, mixed, b)
                                v.tensor_tensor(state[r][:], means[:], const("head_mask"), ALU.mult).then_inc(state_ready, 1)
                            if front:
                                v.wait_ge(q_done, j + 1)
                                wait(v, q_turned, j - 1)
                                front_own(v.tensor_tensor(qx[p][:], tiles(bank[2][:]), along(R_BQ), ALU.add))
                                front_own(v.tensor_reduce(head[:], heads(qx[p][:]), AX.X, ALU.max))
                                v.tensor_tensor(heads(qx[p][:]), heads(qx[p][:]), by_head(head[:]), ALU.subtract).then_inc(q_centred, 1)
                            if back:
                                v.wait_ge(kept, b + 1)
                                for k in range(BT):
                                    last = v.bn_stats(one(mix_stats, BT * b + k), one(mix, BT * b + k))
                                last.then_inc(measured, 1)
                            if front:
                                v.wait_ge(k_exped, j + 1)
                                front_own(v.reciprocal(krec[p][:], ksum[p][:]))
                                v.wait_ge(q_exped, j + 1)
                                front_own(v.tensor_reduce(head[:], heads(qx[p][:]), AX.X, ALU.add))
                                front_own(v.reciprocal(head[:], head[:]))
                                v.tensor_tensor(heads(qx[p][:]), heads(qx[p][:]), by_head(head[:]), ALU.mult).then_inc(q_ready, 1)
                                assert front_own.n == 7

                        stages(v, stage)
                        v.wait_ge(measured, BATCHES)
                        row_norm(v, own, mix_stats[:], mix_rstd[:], mix_shift[:], D, scope, "attn_mix")
                        v.wait_ge(bias_added, BATCHES)

                        def norm(which):
                            j, p = which
                            wait(v, turned, j - 1)
                            for k in range(BT):
                                tile = BT * j + k
                                last = v.tensor_scalar(xw[p][:, k, :], one(mix, tile), one(mix_rstd, tile), one(mix_shift, tile), ALU.mult, ALU.add)
                            last.then_inc(again, 1)

                        def project(front, back):
                            if front and ahead_of(front):
                                norm(ahead_of(front))
                            if back:
                                b, r = back
                                v.wait_ge(projected, b + 1)
                                part = sequence(X, b)
                                v.tensor_tensor(part, part, tiles(bank[2 + r][:]), ALU.add).then_inc(added, 1)
                                v.wait_ge(added, b + 1)
                                for k in range(BT):
                                    v.bn_stats(one(stats, BT * b + k), one(X, BT * b + k))

                        norm((0, 0))
                        stages(v, project)

                    @block.gpsimd
                    def _(pool):
                        @turns(pool, BATCHES)
                        def _(i):
                            pool.wait_ge(normed_rows, i + 1)
                            part = sequence(X, i)
                            pool.tensor_tensor(part, part, along(R_BO), ALU.add).then_inc(bias_added, 1)

        def mamba():
            scope = ExitStack()

            def s(n):
                return sem(f"mamba_{n}")

            def s2(n):
                return pair(f"mamba_{n}")

            def t(n, shape, dt=F32):
                return sb(scope, f"mamba_{n}", shape, dt)

            normed_rows, columns, columns_copied, all_columns = s("normed_rows"), s("columns"), s("columns_copied"), s("all_columns")
            dt_done, u_done, u_ready = s("dt_done"), s("u_done"), s("u_ready")
            dt_clipped, dt_exped, dt_plus1, dt_logged = s("dt_clipped"), s("dt_exped"), s("dt_plus1"), s("dt_logged")
            rates_ready, cs_done, cs_ready, last_done, dec_ready, decays_ready = (
                s(n) for n in ("rates_ready", "cs_done", "cs_ready", "last_done", "dec_ready", "decays_ready"))
            in_done, high_ready, low_ready, odd_ready, conv_done, relu_done, conv_ready = s("in_done"), s("high_ready"), s("low_ready"), s("odd_ready"), s("conv_done"), s("relu_done"), s("conv_ready")
            x_turned, x_copied, seg_done, seg_shifted, seg_exped = s("x_turned"), s("x_copied"), s("seg_done"), s("seg_shifted"), s("seg_exped")
            cb_done, weights_ready, y_done, y_read, state_done, state_ready = (
                s(n) for n in ("cb_done", "weights_ready", "y_done", "y_read", "state_done", "state_ready"))
            again, turned, affine, projected, added = s("again"), s("turned"), s("affine"), s("projected"), s("added")
            pads, least_done, cs_here, diagonal_ready = s("pads"), s("least_done"), s("cs_here"), s("diagonal_ready")
            u_measured, wconv_loaded, w_split, reloaded = s("u_measured"), s("wconv_loaded"), s("w_split"), s("reloaded")

            with scope:
                u = t("u", [P, TILES, INNER])
                xT_all = w1B[:].rearrange("p e f -> p (e f)")
                rates, cs, dec, ecs, elast = (t(n, [P, TILES * MH]) for n in ("rates", "cs", "dec", "ecs", "elast"))
                small = [t(f"small{k}", [P, TILES * MH]) for k in range(4)]
                expA = t("expA", [P, MH])
                out_rstd, out_shift = t("out_rstd", [P, TILES]), t("out_shift", [P, TILES])
                u_stats = t("u_stats", [P, TILES, 6])
                seg, weights = t("seg", [P, MH, P]), t("weights", [P, MH, P])
                xdec, ytmp = t("xdec", [P, INNER]), t("ytmp", [P, INNER])
                carry = t("carry", [STATE, INNER])
                carry_dec = t("carry_dec", [STATE, INNER])
                high_w, low_w = (t(n, [P, CC, TAPS, CH], F32R) for n in ("high_w", "low_w"))

                def tiles(ap):
                    return ap.rearrange("p (t d) -> p t d", t=BT)

                with ExitStack() as inner_scope, nc.Block() as block:
                    xw = [sb(inner_scope, f"mamba_xw{p}", [P, BT, D]) for p in range(2)]
                    xT = [sb(inner_scope, f"mamba_xT{p}", [P, SEQ]) for p in range(2)]
                    dt_bank = bank[6][:, 0:TILES * MH]

                    wconv = sb(inner_scope, "wconv", [P, CC, TAPS, CH])

                    @block.sync
                    def _(sp):
                        sp.dma_start(wconv[:], m_conv).then_inc(wconv_loaded, 16)
                        clear_last_phase(sp)

                    @block.gpsimd
                    def _(pool):
                        pool.wait_ge(wconv_loaded, 16)
                        pool.tensor_copy(high_w[:], wconv[:]).then_inc(w_split, 1)
                        pool.wait_ge(w_split, 1)
                        pool.tensor_tensor(low_w[:], wconv[:], high_w[:].bitcast(F32), ALU.subtract).then_inc(w_split, 1)

                    @block.tensor
                    def _(pe):
                        def stage(front, back):
                            if front:
                                j, p = front
                                pe.wait_ge(normed_rows, j + 1)
                                wait(pe, columns_copied, j - 1)
                                for k in range(BT):
                                    last = pe.transpose(bank[p][:, k * P:(k + 1) * P], xw[p][:, k, :], ident)
                                last.then_inc(columns, 1)
                            if back:
                                b, r = back
                                pe.wait_ge(columns_copied, b + 1)
                                for k in range(BT):
                                    last = pe.matmul(bank[6][:, bass.ds(MH * (BT * b + k), MH)], xT[r][:, k * P:(k + 1) * P],
                                                     win1[:, CH:CH + MH], start=True, stop=True)
                                last.then_inc(dt_done, 1)
                                wait(pe, u_ready, b)
                                for k in range(BT):
                                    last = pe.matmul(bank[2 + 2 * r + k // 2][:, (k % 2) * INNER:(k % 2 + 1) * INNER], xT[r][:, k * P:(k + 1) * P],
                                                     win2[:], start=True, stop=True)
                                last.then_inc(u_done, 1)

                        stages(pe, stage)
                        pe.wait_ge(rates_ready, 1)
                        pe.wait_ge(u_ready, BATCHES)
                        pe.matmul(bank[7][:, 0:TILES * MH], const("upto"), rates[:], start=True, stop=True).then_inc(cs_done, 1)
                        pe.wait_ge(cs_ready, 1)
                        pe.matmul(bank[5][:, 0:TILES * MH], const("last_row"), cs[:], start=True, stop=True).then_inc(last_done, 1)

                    @block.scalar
                    def _(act):
                        def stage(front, back):
                            if front:
                                j, p = front
                                act.wait_ge(columns, j + 1)
                                wait(act, u_done, j - 1)
                                wait(act, all_columns, j - 1)
                                act.activation(xT[p][:], bank[p][:], ACT.Copy).then_inc(columns_copied, 1)
                            if back:
                                b, r = back
                                act.wait_ge(u_done, b + 1)
                                for k in range(2):
                                    last = act.activation(u[:, bass.ds(b * BT + 2 * k, 2), :].rearrange("p t d -> p (t d)"),
                                                          bank[2 + 2 * r + k][:], ACT.Gelu)
                                last.then_inc(u_ready, 1)

                        stages(act, stage)
                        act.activation(expA[:], row[:, R_ALOG:R_ALOG + MH], ACT.Exp)
                        act.wait_ge(dt_clipped, 1)
                        act.activation(small[0][:], small[0][:], ACT.Exp).then_inc(dt_exped, 1)
                        act.wait_ge(dt_plus1, 1)
                        act.activation(small[2][:], small[1][:], ACT.Ln).then_inc(dt_logged, 1)
                        act.wait_ge(dec_ready, 1)
                        act.activation(dec[:], dec[:], ACT.Exp)
                        act.activation(ecs[:], cs[:], ACT.Exp)
                        act.activation(elast[:], bank[5][:, 0:TILES * MH], ACT.Exp).then_inc(decays_ready, 1)

                    @block.vector
                    def _(v):
                        own = Chain(v, "mamba_own")
                        row_norm(v, own, stats[:], rstd[:], shift[:], D, inner_scope, "mamba_in")
                        def stage(front, back):
                            if front:
                                j, p = front
                                wait(v, columns, j - 1)
                                for k in range(BT):
                                    last = normed(v, xw[p][:, k, :], BT * j + k, one(X, BT * j + k))
                                last.then_inc(normed_rows, 1)
                            if back:
                                b, r = back
                                v.wait_ge(columns_copied, b + 1)
                                v.tensor_copy(xT_all[:, bass.ds(b * SEQ, SEQ)], xT[r][:]).then_inc(all_columns, 1)

                        stages(v, stage)
                        v.wait_ge(dt_done, BATCHES)
                        y, y1, ln, den = (a[:] for a in small)
                        v.tensor_scalar(y, dt_bank, 20.0, None, ALU.min).then_inc(dt_clipped, 1)
                        v.wait_ge(dt_exped, 1)
                        v.tensor_scalar(y1, y, 1.0, None, ALU.add).then_inc(dt_plus1, 1)
                        v.wait_ge(dt_plus1, 1)
                        own(v.tensor_scalar(den, y1, -1.0, None, ALU.add))
                        own(v.tensor_scalar(rates[:], den, 0.0, None, ALU.is_equal))
                        own(v.tensor_tensor(den, den, rates[:], ALU.add))
                        own(v.reciprocal(den, den))
                        v.wait_ge(dt_logged, 1)
                        own(v.tensor_tensor(ln, ln, rates[:], ALU.add))
                        own(v.tensor_tensor(ln, ln, den, ALU.mult))
                        own(v.tensor_tensor(ln, ln, y, ALU.mult))
                        own(v.scalar_tensor_tensor(ln, dt_bank, 20.0, ln, ALU.is_le, ALU.mult))
                        own(v.tensor_scalar(y, dt_bank, 20.0, None, ALU.is_gt))
                        own(v.tensor_tensor(y, y, dt_bank, ALU.mult))
                        own(v.tensor_tensor(ln, ln, y, ALU.add))
                        by_head = rates[:].rearrange("p (t h) -> p t h", h=MH)
                        v.scalar_tensor_tensor(by_head, ln.rearrange("p (t h) -> p t h", h=MH), -1.0,
                                               expA[:].unsqueeze(1).broadcast_to([P, TILES, MH]), ALU.mult, ALU.mult).then_inc(rates_ready, 1)
                        v.wait_ge(cs_done, 1)
                        v.tensor_copy(cs[:], bank[7][:, 0:TILES * MH]).then_inc(cs_ready, 1)
                        v.wait_ge(last_done, 1)
                        v.wait_ge(cs_ready, 1)
                        v.tensor_tensor(dec[:], bank[5][:, 0:TILES * MH], cs[:], ALU.subtract).then_inc(dec_ready, 1)

                with ExitStack() as inner_scope, nc.Block() as block:
                    def tt(n, shape, dt=F32):
                        return sb(inner_scope, f"mamba_{n}", shape, dt)

                    cs_high, cs_low = (tt(n, [P, BT * MH], F32R) for n in ("cs_high", "cs_low"))
                    diagonals = [tt(f"diagonals{k}", [P, 2, MH, P], F32R) for k in range(2)]
                    all_ones = tt("all_ones", [P, P], F32R)
                    inputs = {(part, odd): tt(f"inputs_{part}{odd}", [P, CC, TAPS + SEQ], F32R) for part in ("high", "low") for odd in (0, 1)}
                    data = slice(TAPS - 1, TAPS - 1 + SEQ)
                    relu, least = tt("relu", [P, SEQ]), tt("least", [P, SEQ])
                    xconv = tt("xconv", [P, 2, SEQ])
                    bcT = [tt(f"bcT{p}", [P, SEQ]) for p in range(2)]
                    bT = [b[0:STATE] for b in bcT]
                    cT = [tt(f"cT{p}", [STATE, SEQ]) for p in range(2)]
                    xs = [tt(f"xs{p}", [P, BT, INNER]) for p in range(2)]
                    bs = [tt(f"bs{p}", [P, BT, STATE]) for p in range(2)]

                    @block.tensor
                    def _(pe):
                        def stage(conv, scan):
                            if conv:
                                j, p = conv
                            if scan:
                                g, r = scan

                            def take_in():
                                for c in range(CC):
                                    if c < 2:
                                        wait(pe, low_ready, CC * j)
                                    else:
                                        wait(pe, conv_ready, CC * j - 1)
                                    pe.matmul(bank[IN_BANK[c]][:], win1[:, c * P:(c + 1) * P], xT_all[:, bass.ds(j * SEQ, SEQ)],
                                              start=True, stop=True).then_inc(in_done, 1)

                            def convolve(o, part):
                                if part == 0:
                                    pe.wait_ge(low_ready, CC * (j + 1))
                                    wait(pe, conv_ready, CC * j + (o == 2))
                                else:
                                    pe.wait_ge(odd_ready, CC * (j + 1))
                                products = [(c, tap, w, x) for c in range(CC) for tap in range(part, TAPS, 2)
                                            for w, x in ((low_w, "high"), (high_w, "low"), (high_w, "high"))]
                                for n, (c, tap, w, x) in enumerate(products):
                                    last = pe.matmul(bank[2 + o % 2][:], w[:, c, tap, o * P:(o + 1) * P], inputs[x, part][:, c, tap - part:tap - part + SEQ],
                                                     start=part == 0 and n == 0, stop=part == 1 and n == len(products) - 1)
                                if part:
                                    last.then_inc(conv_done, 1)

                            def turn(c):
                                pe.wait_ge(conv_ready, CC * j + c + 1)
                                wait(pe, x_copied, CC * j + c)
                                if scan:
                                    pe.wait_ge(state_ready, (BT - 1) * (g + 1))
                                for k in range(BT):
                                    last = pe.transpose(bank[4][:, k * P:(k + 1) * P], xconv[:, c, k * P:(k + 1) * P], ident)
                                last.then_inc(x_turned, 1)

                            def turn_b():
                                pe.wait_ge(conv_ready, CC * (g + 1))
                                pe.wait_ge(x_copied, CC * g + 2)
                                for k in range(BT):
                                    src = bcT[r][:, k * P:(k + 1) * P]
                                    last = pe.transpose(bank[4][:, k * P:(k + 1) * P], src, ident)
                                last.then_inc(x_turned, 1)

                            def pairs():
                                pe.wait_ge(conv_ready, CC * (g + 1))
                                wait(pe, weights_ready, BT * g)
                                for c in range(BT):
                                    last = pe.matmul(bank[6][:, c * P:(c + 1) * P], bT[r][:, c * P:(c + 1) * P], cT[r][:, c * P:(c + 1) * P],
                                                     start=True, stop=True)
                                last.then_inc(cb_done, 1)

                            def spread(c):
                                pe.wait_ge(diagonal_ready, BT * g + c + 1)
                                wait(pe, seg_shifted, BT * g + c)
                                pe.matmul(bank[5][:], all_ones[:], diagonals[c % 2][:, 1].rearrange("p h l -> p (h l)"), start=True, stop=False)
                                pe.matmul(bank[5][:], all_ones[:], diagonals[c % 2][:, 0].rearrange("p h l -> p (h l)"), start=False, stop=True) \
                                    .then_inc(seg_done, 1)

                            def combine(c):
                                wait(pe, y_read, BT * g + c)
                                pe.wait_ge(weights_ready, BT * g + c + 1)
                                for hd in range(MH):
                                    last = pe.matmul(bank[7][:, hd * MP:(hd + 1) * MP], weights[:, hd, :], xs[r][:, c, hd * MP:(hd + 1) * MP],
                                                     start=True, stop=True)
                                if c:
                                    pe.wait_ge(state_ready, (BT - 1) * g + c)
                                    last = pe.matmul(bank[7][:, INNER:2 * INNER], cT[r][:, c * P:(c + 1) * P], carry[:], start=True, stop=True)
                                last.then_inc(y_done, 1)
                                if c < BT - 1:
                                    pe.wait_ge(x_copied, CC * (g + 1))
                                    wait(pe, state_ready, (BT - 1) * g + c)
                                    pe.matmul(bank[4][0:STATE, 0:INNER], bs[r][:, c, :], xdec[:], start=True, stop=True).then_inc(state_done, 1)

                            if conv:
                                take_in()
                            if scan:
                                turn_b()
                                pairs()
                                spread(0)
                            for n in range(BT):
                                if conv:
                                    convolve(n // 2, n % 2)
                                if scan:
                                    if n + 1 < BT:
                                        spread(n + 1)
                                    combine(n)
                            if conv:
                                convolve(2, 0)
                                turn(0)
                                convolve(2, 1)
                                turn(1)

                        pe.wait_ge(pads, 3)
                        stages(pe, stage)

                    @block.scalar
                    def _(act):
                        def stage(conv, scan):
                            if conv:
                                j, p = conv
                            if scan:
                                g, r = scan

                            def relu_part(o):
                                act.wait_ge(conv_done, CC * j + o + 1)
                                wait(act, conv_ready, CC * j + o)
                                act.activation(relu[:], bank[2 + o % 2][:], ACT.Relu, bias=vec[:, V_CONVB + o:V_CONVB + o + 1]).then_inc(relu_done, 1)

                            if conv:
                                for c in range(CC):
                                    act.wait_ge(in_done, CC * j + c + 1)
                                    wait(act, conv_done, CC * j)
                                    act.activation(inputs["high", 0][:, c, data], bank[IN_BANK[c]][:], ACT.Copy).then_inc(high_ready, 1)
                            for n in range(BT):
                                if scan:
                                    act.wait_ge(seg_shifted, BT * g + n + 1)
                                    act.activation(seg[:], seg[:], ACT.Exp).then_inc(seg_exped, 1)
                                if conv and n == 0:
                                    for c in range(CC):
                                        act.wait_ge(low_ready, CC * j + c + 1)
                                        for part in ("high", "low"):
                                            last = act.activation(inputs[part, 1][:, c, 0:SEQ + 2], inputs[part, 0][:, c, 1:SEQ + 3], ACT.Copy)
                                        last.then_inc(odd_ready, 1)
                                if conv and n % 2:
                                    relu_part(n // 2)
                            if conv:
                                relu_part(2)

                        act.wait_ge(pads, 3)
                        stages(act, stage)

                    @block.vector
                    def _(v):
                        loop = Chain(v, "mamba_scan")
                        per_scan = 3 * (BT - 1)

                        def stage(conv, scan):
                            if conv:
                                j, p = conv
                            if scan:
                                g, r = scan
                                loop.start(per_scan * g)

                            def prelu(o):
                                v.wait_ge(relu_done, CC * j + o + 1)
                                v.tensor_scalar(least[:], bank[2 + o % 2][:], vec[:, V_CONVB + o:V_CONVB + o + 1], 0.0, ALU.add, ALU.min).then_inc(least_done, 1)
                                v.wait_ge(least_done, CC * j + o + 1)
                                if o < 2:
                                    wait(v, x_turned, CC * j)
                                    v.scalar_tensor_tensor(xconv[:, o, :], least[:], vec[:, V_PRELU:V_PRELU + 1], relu[:], ALU.mult, ALU.add) \
                                        .then_inc(conv_ready, 1)
                                else:
                                    if scan:
                                        wait(v, y_done, BT * g)
                                    v.scalar_tensor_tensor(bcT[p][:], least[:], vec[:, V_PRELU:V_PRELU + 1], relu[:], ALU.mult, ALU.add)
                                    v.scalar_tensor_tensor(cT[p][:], least[STATE:], vec[STATE:, V_PRELU:V_PRELU + 1], relu[STATE:], ALU.mult, ALU.add) \
                                        .then_inc(conv_ready, 1)

                            def copy_turned(c):
                                v.wait_ge(x_turned, CC * j + c + 1)
                                v.tensor_copy(xs[p][:, :, c * P:(c + 1) * P], tiles(bank[4][:])).then_inc(x_copied, 1)

                            def copy_turned_b():
                                v.wait_ge(x_turned, CC * (g + 1))
                                v.tensor_copy(bs[r][:], tiles(bank[4][:])[:, :, 0:STATE]).then_inc(x_copied, 1)

                            def heads(ap):
                                return ap.rearrange("p (h d) -> p h d", h=MH)

                            def by_head(tab, c, parts=P):
                                return tab[0:parts, bass.ds((g * BT + c) * MH, MH)].unsqueeze(2).broadcast_to([parts, MH, MP])

                            def decay(c):
                                v.wait_ge(seg_done, BT * g + c + 1)
                                wait(v, weights_ready, BT * g + c)
                                for hd in range(MH):
                                    last = v.scalar_tensor_tensor(seg[:, hd, :], bank[5][:, hd * P:(hd + 1) * P], one(cs, (g * BT + c) * MH + hd),
                                                                  const("causal"), ALU.subtract, ALU.add)
                                last.then_inc(seg_shifted, 1)

                            def weigh(c):
                                wait(v, y_done, BT * g + c)
                                v.wait_ge(x_copied, CC * g + 2)
                                if c < BT - 1:
                                    wait(v, state_done, (BT - 1) * g + c)
                                    v.tensor_tensor(heads(xdec[:]), heads(xs[r][:, c, :]), by_head(dec, c), ALU.mult)
                                v.wait_ge(seg_exped, BT * g + c + 1)
                                if c == 0:
                                    v.wait_ge(cb_done, g + 1)
                                v.tensor_tensor(weights[:], seg[:], bank[6][:, c * P:(c + 1) * P].unsqueeze(1).broadcast_to([P, MH, P]), ALU.mult) \
                                    .then_inc(weights_ready, 1)

                            def finish(c):
                                tile = g * BT + c
                                v.wait_ge(y_done, BT * g + c + 1)
                                if c:
                                    loop(v.tensor_tensor(heads(ytmp[:]), heads(bank[7][:, INNER:2 * INNER]), by_head(ecs, c), ALU.mult))
                                    v.tensor_tensor(ytmp[:], ytmp[:], bank[7][:, 0:INNER], ALU.add).then_inc(y_read, 1)
                                else:
                                    v.tensor_copy(ytmp[:], bank[7][:, 0:INNER]).then_inc(y_read, 1)
                                v.wait_ge(y_read, BT * g + c + 1)
                                loop(v.tensor_tensor(one(u, tile), one(u, tile), ytmp[:].unsqueeze(1), ALU.mult))
                                v.bn_stats(one(u_stats, tile), one(u, tile)).then_inc(u_measured, 1)
                                if c == BT - 1:
                                    return
                                v.wait_ge(state_done, (BT - 1) * g + c + 1)
                                if c:
                                    loop(v.tensor_tensor(heads(carry_dec[:]), heads(carry[:]), by_head(elast, c, STATE), ALU.mult))
                                    v.tensor_tensor(carry[:], carry_dec[:], bank[4][0:STATE, 0:INNER], ALU.add).then_inc(state_ready, 1)
                                else:
                                    v.tensor_copy(carry[:], bank[4][0:STATE, 0:INNER]).then_inc(state_ready, 1)
                                v.wait_ge(state_ready, (BT - 1) * g + c + 1)

                            if conv:
                                for c in range(CC):
                                    v.wait_ge(high_ready, CC * j + c + 1)
                                    wait(v, conv_done, CC * j)
                                    v.tensor_tensor(inputs["low", 0][:, c, data], bank[IN_BANK[c]][:], inputs["high", 0][:, c, data].bitcast(F32),
                                                    ALU.subtract).then_inc(low_ready, 1)
                            if scan:
                                copy_turned_b()
                                decay(0)
                                weigh(0)
                            for n in range(BT):
                                if scan:
                                    if n + 1 < BT:
                                        decay(n + 1)
                                    finish(n)
                                    if n + 1 < BT:
                                        weigh(n + 1)
                                if conv and n % 2:
                                    prelu(n // 2)
                            if scan:
                                assert loop.n == per_scan
                            if conv:
                                wait(v, diagonal_ready, BT * j)
                                now = cs[:, bass.ds(j * BT * MH, BT * MH)]
                                v.tensor_copy(cs_high[:], now).then_inc(cs_here, 1)
                                v.wait_ge(cs_here, 2 * j + 1)
                                v.tensor_tensor(cs_low[:], now, cs_high[:].bitcast(F32), ALU.subtract).then_inc(cs_here, 1)
                                copy_turned(0)
                                copy_turned(1)
                                prelu(2)

                        v.tensor_copy(all_ones[:], const("ones")).then_inc(pads, 1)
                        for part in ("high", "low"):
                            v.tensor_scalar(inputs[part, 0][:, :, 0:TAPS - 1], const("ones")[:, 0:CC * (TAPS - 1)].rearrange("p (c t) -> p c t", c=CC), 0.0, None, ALU.mult).then_inc(pads, 1)
                        stages(v, stage)

                    @block.gpsimd
                    def _(pool):
                        def stage(conv, scan):
                            if scan:
                                g, r = scan
                                pool.wait_ge(cs_here, 2 * g + 2)
                                for c in range(BT):
                                    wait(pool, seg_done, BT * g + c - 1)
                                    for part, sums in enumerate((cs_high, cs_low)):
                                        last = pool.tensor_tensor(
                                            diagonals[c % 2][:, part], ident.unsqueeze(1).broadcast_to([P, MH, P]),
                                            sums[:, c * MH:(c + 1) * MH].bitcast(F32).unsqueeze(2).broadcast_to([P, MH, P]), ALU.mult)
                                    last.then_inc(diagonal_ready, 1)

                        stages(pool, stage)

                with ExitStack() as inner_scope, nc.Block() as block:
                    yw = [sb(inner_scope, f"mamba_yw{p}", [P, BT, INNER]) for p in range(2)]
                    yT = [sb(inner_scope, f"mamba_yT{p}", [P, 2, SEQ]) for p in range(2)]

                    @block.sync
                    def _(sp):
                        sp.dma_start(w1B[:], b_w1).then_inc(reloaded, 16)
                        sp.wait_ge(reloaded, 16)

                    @block.tensor
                    def _(pe):
                        def project(front, back):
                            if front:
                                j, p = front
                                pe.wait_ge(again, j + 1)
                                wait(pe, affine, j - 1)
                                for c in range(2):
                                    for k in range(BT):
                                        last = pe.transpose(bank[2 * p + c][:, k * P:(k + 1) * P], yw[p][:, k, c * P:(c + 1) * P], ident)
                                last.then_inc(turned, 1)
                            if back:
                                b, r = back
                                pe.wait_ge(affine, b + 1)
                                wait(pe, added, b)
                                for k in range(BT):
                                    for c in range(2):
                                        last = pe.matmul(bank[4 + r][:, k * P:(k + 1) * P], yT[r][:, c, k * P:(k + 1) * P], win3[:, c, :],
                                                         start=(c == 0), stop=(c == 1))
                                last.then_inc(projected, 1)

                        stages(pe, project)

                    @block.scalar
                    def _(act):
                        def project(front, back):
                            if front:
                                j, p = front
                                act.wait_ge(turned, j + 1)
                                wait(act, projected, j - 1)
                                for c in range(2):
                                    last = act.activation(yT[p][:, c, :], bank[2 * p + c][:], ACT.Identity, scale=vec[:, V_MG + c:V_MG + c + 1],
                                                          bias=vec[:, V_MB + c:V_MB + c + 1])
                                last.then_inc(affine, 1)

                        stages(act, project)

                    @block.vector
                    def _(v):
                        own = Chain(v, "mamba_out")
                        row_norm(v, own, u_stats[:], out_rstd[:], out_shift[:], INNER, inner_scope, "mamba_out")

                        def norm(which):
                            j, p = which
                            wait(v, turned, j - 1)
                            for k in range(BT):
                                tile = BT * j + k
                                last = v.tensor_scalar(yw[p][:, k, :], one(u, tile), one(out_rstd, tile), one(out_shift, tile), ALU.mult, ALU.add)
                            last.then_inc(again, 1)

                        def project(front, back):
                            if front and ahead_of(front):
                                norm(ahead_of(front))
                            if back:
                                b, r = back
                                v.wait_ge(projected, b + 1)
                                part = X[:, bass.ds(BT * b, BT), :]
                                v.tensor_tensor(part, part, tiles(bank[4 + r][:]), ALU.add).then_inc(added, 1)
                                v.wait_ge(added, b + 1)
                                for k in range(BT):
                                    v.bn_stats(one(stats, BT * b + k), one(X, BT * b + k))

                        norm((0, 0))
                        stages(v, project)

        a = (FA, 1, ACT.Gelu, wgA, w1A, w2A, False, False)
        b = (FB, 2, ACT.Silu, wgB, w1B, w2B, True)
        for phase in ("a0", "attention", "a1", "b0", "mamba", "b1"):
            next_phase()
            if phase[0] == "a" and phase != "attention":
                moe(phase, *a)
            elif phase == "attention":
                attention()
            elif phase == "mamba":
                layer0.close()
                mamba()
            else:
                layer0.close()
                moe(phase, *b, phase == "b1")


def digits():
    return np.array([c << 2 * (STEPS - 1 - step) for step in range(STEPS) for c in (1, 2, 3)] + [0] * 3)


def constants():
    k, m = np.arange(P)[:, None], np.arange(P)[None, :]
    e_t = np.arange(E * TILES)
    part = dict(
        ident=k == m, not_before=np.where(k < m, 0.0, -1.0), upto=k <= m, ones=k >= 0 * m, same_expert=k % E == m % E,
        last_row=(k == P - 1) & (m >= 0), head_mask=k // HD == m // HD,
        causal=np.where(m >= k, 0.0, NEG),
        prefer=np.broadcast_to(E - e_t // TILES, (P, E * TILES)),
        restart=np.broadcast_to(e_t % TILES != 0, (P, E * TILES)),
        row_no=P * np.arange(MAX_BLOCKS)[None, :] + k,
        digits=np.broadcast_to(digits(), (P, DIGITS)),
    )
    return np.concatenate([part[n].astype(np.float32) for n in PARTS], axis=1)


def layouts(inp):
    g = {k: np.asarray(v) for k, v in inp.items()}
    c = np.ascontiguousarray
    rep = lambda v: np.broadcast_to(v, (P, v.shape[-1]))
    return {
        "x": c(g["L0_attn_x"].reshape(TOKENS, D)),
        "consts": constants(),
        "ints": c(np.concatenate([np.broadcast_to(digits(), (P, DIGITS)),
                                  P * np.arange(2 * TILES)[None, :] + np.arange(P)[:, None]], axis=1).astype(np.int32)),
        "vecs": c(np.concatenate([g["L0_attn_bk"][:, None], g["L0_attn_ln_g"][:, None], g["L0_attn_ln_b"][:, None],
                                  g["L1_attn_conv_b"].reshape(CC, P).T, np.broadcast_to(g["L1_attn_prelu_a"], (P, 1)),
                                  g["L1_attn_ln_g"].reshape(2, P).T, g["L1_attn_ln_b"].reshape(2, P).T], axis=1)),
        "rows": c(np.concatenate([rep(g["L0_attn_bq"]), rep(g["L0_attn_bv"]), rep(g["L0_attn_bo"]), rep(g["L1_attn_A_log"])], axis=1)),
        "wqkvo": c(np.stack([g["L0_attn_W" + n].T for n in "qkvo"], axis=1)),
        "a_wg": g["L0_ffn_Wg"],
        "a_w1": c(g["L0_ffn_W1"].transpose(1, 0, 2)),
        "a_w2": c(g["L0_ffn_W2"].reshape(E, FA // P, P, D).transpose(2, 0, 1, 3)),
        "b_wg": c(g["L1_ffn_gate_w"].T),
        "b_w1": c(g["L1_ffn_experts_w1"].transpose(2, 0, 1)),
        "b_w2": c(g["L1_ffn_experts_w2"].transpose(0, 2, 1).reshape(E, FB // P, P, D).transpose(2, 0, 1, 3)),
        "b_sw1": c(g["L1_ffn_shared_w1"].T),
        "b_sw2": c(g["L1_ffn_shared_w2"].T.reshape(FB // P, P, D).transpose(1, 0, 2)),
        "m_in1": c(g["L1_attn_W_in1"][INNER:].T),
        "m_in2": c(g["L1_attn_W_in2"].T),
        "m_in3": c(g["L1_attn_W_in3"].T.reshape(INNER // P, P, D).transpose(1, 0, 2)),
        "m_conv": c(g["L1_attn_conv_w"].transpose(1, 2, 0).reshape(CC, P, TAPS, CH).transpose(1, 0, 2, 3)),
    }


def kernel(**inputs):
    import concourse.bacc as bacc
    from concourse.bass_utils import run_bass_kernel_spmd

    nc = bacc.Bacc("TRN2", target_bir_lowering=False, num_devices=1)
    arrays = layouts(inputs)
    args = {n: nc.dram_tensor(f"in_{n}", a.shape, mybir.dt.from_np(a.dtype), kind="ExternalInput").ap() for n, a in arrays.items()}
    result = nc.dram_tensor("result", (TOKENS, D), F32, kind="ExternalOutput").ap()
    program(nc, **args, out=result)
    r = run_bass_kernel_spmd(nc, [{f"in_{n}": a for n, a in arrays.items()}], core_ids=[0])
    return r.results[0]["result"].reshape(BATCHES, SEQ, D)
```
